# Optimizing a Trainium2 kernel written in Bass

```python
import numpy as np
import jax
import jax.numpy as jnp

def _softmax(x, axis=-1):
    return jax.nn.softmax(x, axis=axis)

def _gelu(x):
    return jax.nn.gelu(x, approximate=True)

def _silu(x):
    return jax.nn.silu(x)

def _sigmoid(x):
    return jax.nn.sigmoid(x)

def _layernorm(x, axis=-1, eps=1e-05):
    m = jnp.mean(x, axis=axis, keepdims=True)
    v = jnp.var(x, axis=axis, keepdims=True)
    return (x - m) / jnp.sqrt(v + eps)

def _scatter_add(tgt, idx, src, axis=0):
    return tgt.at[idx].add(src)

def _segment_sum(src, seg, n):
    return jax.ops.segment_sum(src, seg, n)
kernel_name = 'mk_perceiver_d2_seqx_r8_3d9806'

def setup_inputs(seed: int=0):
    np.random.seed(seed)
    _w = jnp.asarray

    def _rec_inputs():
        import jax
        import jax.numpy as jnp
        _rk = jax.random.key(seed)
        x = 7.22e-05 + 1 * jax.random.normal(jax.random.fold_in(_rk, 1), (32, 32, 128), jnp.float32)
        _lenS = 32 - jax.random.randint(jax.random.fold_in(_rk, 7), (32,), 0, max(1, 32 // 4) + 1, jnp.int32)
        _lenS2 = 257 - jax.random.randint(jax.random.fold_in(_rk, 8), (32,), 0, max(1, 257 // 4) + 1, jnp.int32)
        _ctx_1024P = jax.random.normal(jax.random.fold_in(_rk, 11), (32, 16, 128), jnp.float32)
        _ctx_1024c = jax.random.dirichlet(jax.random.fold_in(_rk, 511), 0.3 * jnp.ones((16,), jnp.float32), (32, 257))
        _ctx_1024t = jnp.einsum('bsk,bkd->bsd', _ctx_1024c, _ctx_1024P)
        _ctx_1024t = _ctx_1024t * jax.lax.rsqrt(jnp.mean(jnp.square(_ctx_1024t)) + 1e-12) * 0.953939
        ctx_1024 = -4.77421e-07 + 0.031248 * (_ctx_1024t + 0.3 * jax.random.normal(jax.random.fold_in(_rk, 611), (32, 257, 128), jnp.float32))
        return (x, ctx_1024)
    x, ctx_1024 = _rec_inputs()

    def _L0_xattn_setup():
        import jax, jax.numpy as jnp
        import numpy as np
        E, T, H, F = (8, 128, 128, 512)
        key = jax.random.key(seed)
        k1, k2, k3 = jax.random.split(key, 3)
        x = jax.random.normal(k1, (E, T, H), dtype=jnp.float32)
        w1 = jax.random.normal(k2, (E, F, H), dtype=jnp.float32) * (1.0 / np.sqrt(H))
        w2 = jax.random.normal(k3, (E, F, H), dtype=jnp.float32) * (1.0 / np.sqrt(F))
        return {'x': x, 'w1': w1, 'w2': w2}
    _L0_xattn_all = _L0_xattn_setup()
    _L0_xattn_in = {k: v for k, v in _L0_xattn_all.items() if k in ()}
    del _L0_xattn_all

    def _L0_attn_setup():
        import math
        import jax, jax.numpy as jnp
        import numpy as np
        HIDDEN = 128
        NUM_LAYERS = 24
        LAYER_ID = 4

        def _time_params():
            h = HIDDEN
            ratio_0_to_1 = LAYER_ID / (NUM_LAYERS - 1)
            ratio_1_to_almost_0 = 1.0 - LAYER_ID / NUM_LAYERS
            zigzag = 0.5 * (jnp.arange(1, h + 1) % 3 - 1)
            time_first = jnp.full(h, math.log(0.3)) + zigzag
            idx = jnp.arange(0, h)
            time_decay = -5 + 8 * (idx / (h - 1)) ** (0.7 + 1.3 * ratio_0_to_1)
            x = jnp.arange(h) / h
            time_mix_key = jnp.power(x, ratio_1_to_almost_0)
            time_mix_value = time_mix_key + 0.3 * ratio_0_to_1
            time_mix_receptance = jnp.power(x, 0.5 * ratio_1_to_almost_0)
            return (time_decay.astype(jnp.float32), time_first.astype(jnp.float32), time_mix_key.astype(jnp.float32), time_mix_value.astype(jnp.float32), time_mix_receptance.astype(jnp.float32))

        def _wkv(time_decay, time_first, k, v):
            B, T, H = k.shape
            td = -jnp.exp(time_decay.astype(jnp.float32))
            tf = time_first.astype(jnp.float32)
            kT = jnp.swapaxes(k, 0, 1).astype(jnp.float32)
            vT = jnp.swapaxes(v, 0, 1).astype(jnp.float32)

            def step(carry, kv):
                num, den, mx = carry
                ck, cv = kv
                max_out = jnp.maximum(mx, ck + tf)
                e1 = jnp.exp(mx - max_out)
                e2 = jnp.exp(ck + tf - max_out)
                out = (e1 * num + e2 * cv) / (e1 * den + e2)
                max_st = jnp.maximum(mx + td, ck)
                e1s = jnp.exp(mx + td - max_st)
                e2s = jnp.exp(ck - max_st)
                return ((e1s * num + e2s * cv, e1s * den + e2s, max_st), out)
            init = (jnp.zeros((B, H), jnp.float32), jnp.zeros((B, H), jnp.float32), jnp.full((B, H), -1e+38, jnp.float32))
            _, outT = jax.lax.scan(step, init, (kT, vT))
            return jnp.swapaxes(outT, 0, 1).astype(k.dtype)
        key = jax.random.key(seed)
        k0, k1, k2, k3, k4 = jax.random.split(key, 5)
        B, T, H = (4, 512, HIDDEN)
        td, tf, tmk, tmv, tmr = _time_params()
        scale = 0.02
        return {'hidden': jax.random.normal(k0, (B, T, H), dtype=jnp.float32), 'Wk': jax.random.normal(k1, (H, H), dtype=jnp.float32) * scale, 'Wv': jax.random.normal(k2, (H, H), dtype=jnp.float32) * scale, 'Wr': jax.random.normal(k3, (H, H), dtype=jnp.float32) * scale, 'Wo': jax.random.normal(k4, (H, H), dtype=jnp.float32) * scale, 'time_decay': td, 'time_first': tf, 'time_mix_key': tmk, 'time_mix_value': tmv, 'time_mix_receptance': tmr}
    _L0_attn_all = _L0_attn_setup()
    _L0_attn_in = {k: v for k, v in _L0_attn_all.items() if k in ('Wk', 'Wv', 'Wr', 'Wo', 'time_decay', 'time_first', 'time_mix_key', 'time_mix_value', 'time_mix_receptance')}
    del _L0_attn_all

    def _L0_ffn_setup():
        import jax, jax.numpy as jnp
        import numpy as np
        H = 128
        DFF = 512
        E_ROUTED = 7
        TOP_K = 2

        def _swiglu(flat, gate_w, up_w, down_w):
            g = flat @ gate_w.T
            up = flat @ up_w.T
            return jax.nn.silu(g) * up @ down_w.T
        key = jax.random.key(seed)
        ks = jax.random.split(key, 8)
        s = 0.02
        return {'x': jax.random.normal(ks[0], (4, 256, H), jnp.float32), 'shared_up': jax.random.normal(ks[1], (DFF, H), jnp.float32) * s, 'shared_gate': jax.random.normal(ks[2], (DFF, H), jnp.float32) * s, 'shared_down': jax.random.normal(ks[3], (H, DFF), jnp.float32) * s, 'routed_up': jax.random.normal(ks[4], (E_ROUTED, DFF, H), jnp.float32) * s, 'routed_gate': jax.random.normal(ks[5], (E_ROUTED, DFF, H), jnp.float32) * s, 'routed_down': jax.random.normal(ks[6], (E_ROUTED, H, DFF), jnp.float32) * s, 'router_w': jax.random.normal(ks[7], (E_ROUTED, H), jnp.float32) * 0.02}
    _L0_ffn_all = _L0_ffn_setup()
    _L0_ffn_in = {k: v for k, v in _L0_ffn_all.items() if k in ('shared_up', 'shared_gate', 'shared_down', 'routed_up', 'routed_gate', 'routed_down', 'router_w')}
    del _L0_ffn_all

    def _L1_xattn_setup():
        import jax, jax.numpy as jnp
        import numpy as np
        B, S, D, DFF = (4, 256, 128, 512)
        EPS = 1e-05

        def layernorm(x, gamma, beta):
            mu = jnp.mean(x, axis=-1, keepdims=True)
            var = jnp.var(x, axis=-1, keepdims=True)
            return (x - mu) * jax.lax.rsqrt(var + EPS) * gamma + beta

        def attention(Q, K, V, causal):
            d_k = Q.shape[-1]
            scores = jnp.einsum('bqd,bkd->bqk', Q, K) / jnp.sqrt(jnp.asarray(d_k, Q.dtype))
            if causal:
                q_len, k_len = (scores.shape[-2], scores.shape[-1])
                mask = jnp.tril(jnp.ones((q_len, k_len), dtype=bool))
                scores = jnp.where(mask[None], scores, jnp.asarray(-jnp.inf, scores.dtype))
            w = jax.nn.softmax(scores, axis=-1)
            return jnp.einsum('bqk,bkd->bqd', w, V)
        key = jax.random.key(seed)
        ks = jax.random.split(key, 12)
        sd = 0.02
        return {'y': jax.random.normal(ks[0], (B, S, D), jnp.float32), 'Z': jax.random.normal(ks[1], (B, S, D), jnp.float32), 'w1': jax.random.normal(ks[2], (D, DFF), jnp.float32) * sd, 'b1': jnp.zeros((DFF,), jnp.float32), 'w2': jax.random.normal(ks[3], (DFF, D), jnp.float32) * sd, 'b2': jnp.zeros((D,), jnp.float32), 'g1': jnp.ones((D,), jnp.float32), 'beta1': jnp.zeros((D,), jnp.float32), 'g2': jnp.ones((D,), jnp.float32), 'beta2': jnp.zeros((D,), jnp.float32), 'g3': jnp.ones((D,), jnp.float32), 'beta3': jnp.zeros((D,), jnp.float32)}
    _L1_xattn_all = _L1_xattn_setup()
    _L1_xattn_in = {k: v for k, v in _L1_xattn_all.items() if k in ('w1', 'b1', 'w2', 'b2', 'g1', 'beta1', 'g2', 'beta2', 'g3', 'beta3')}
    del _L1_xattn_all

    def _L1_attn_setup():
        import jax, jax.numpy as jnp
        import numpy as np
        import math
        B, S, E, H = (2, 256, 128, 16)
        HD = E // H
        HX = 64
        P = HX // 2

        def _l2norm(x, eps=1e-12):
            n = jnp.sqrt(jnp.sum(x * x, axis=-1, keepdims=True))
            return x / jnp.maximum(n, eps)

        def _scramble(t):
            b, h, p, s, _ = t.shape
            return jnp.swapaxes(t, -1, -2).reshape(b, h, p, s, 2)
        key = jax.random.key(seed)
        ks = jax.random.split(key, 12)
        sc = 0.02
        return {'x': jax.random.normal(ks[0], (B, S, E), dtype=jnp.float32), 'Wq': jax.random.normal(ks[1], (E, E), dtype=jnp.float32) * sc, 'bq': jnp.zeros((E,), dtype=jnp.float32), 'Wk': jax.random.normal(ks[2], (E, E), dtype=jnp.float32) * sc, 'bk': jnp.zeros((E,), dtype=jnp.float32), 'Wv': jax.random.normal(ks[3], (E, E), dtype=jnp.float32) * sc, 'bv': jnp.zeros((E,), dtype=jnp.float32), 'Wo': jax.random.normal(ks[4], (E, E), dtype=jnp.float32) * sc, 'bo': jnp.zeros((E,), dtype=jnp.float32), 'Whel': jax.random.normal(ks[5], (H, HX, HD), dtype=jnp.float32) * sc, 'bhel': jnp.zeros((H, HX), dtype=jnp.float32)}
    _L1_attn_all = _L1_attn_setup()
    _L1_attn_in = {k: v for k, v in _L1_attn_all.items() if k in ('Wq', 'bq', 'Wk', 'bk', 'Wv', 'bv', 'Wo', 'bo', 'Whel', 'bhel')}
    del _L1_attn_all

    def _L1_ffn_setup():
        import jax, jax.numpy as jnp
        import numpy as np
        N_EXPERTS = 16
        TOP_K = int(N_EXPERTS * 0.2)
        EPS = 1e-12
        key = jax.random.key(seed)
        ks = jax.random.split(key, 6)
        B, T, D, H, E = (4, 128, 128, 256, N_EXPERTS)
        x = jax.random.normal(ks[0], (B, T, D), dtype=jnp.float32)
        gate = jax.random.normal(ks[1], (D, E), dtype=jnp.float32)
        W1 = jax.random.normal(ks[2], (E, D, H), dtype=jnp.float32) * (1.0 / np.sqrt(D))
        b1 = jax.random.normal(ks[3], (E, H), dtype=jnp.float32) * 0.02
        W2 = jax.random.normal(ks[4], (E, H, D), dtype=jnp.float32) * (1.0 / np.sqrt(H))
        b2 = jax.random.normal(ks[5], (E, D), dtype=jnp.float32) * 0.02
        return {'x': x, 'gate': gate, 'W1': W1, 'b1': b1, 'W2': W2, 'b2': b2}
    _L1_ffn_all = _L1_ffn_setup()
    _L1_ffn_in = {k: v for k, v in _L1_ffn_all.items() if k in ('gate', 'W1', 'b1', 'W2', 'b2')}
    del _L1_ffn_all
    return {'x': x, 'ctx_1024': ctx_1024, 'L0_attn_Wk': _L0_attn_in['Wk'], 'L0_attn_Wv': _L0_attn_in['Wv'], 'L0_attn_Wr': _L0_attn_in['Wr'], 'L0_attn_Wo': _L0_attn_in['Wo'], 'L0_attn_time_decay': _L0_attn_in['time_decay'], 'L0_attn_time_first': _L0_attn_in['time_first'], 'L0_attn_time_mix_key': _L0_attn_in['time_mix_key'], 'L0_attn_time_mix_value': _L0_attn_in['time_mix_value'], 'L0_attn_time_mix_receptance': _L0_attn_in['time_mix_receptance'], 'L0_ffn_shared_up': _L0_ffn_in['shared_up'], 'L0_ffn_shared_gate': _L0_ffn_in['shared_gate'], 'L0_ffn_shared_down': _L0_ffn_in['shared_down'], 'L0_ffn_routed_up': _L0_ffn_in['routed_up'], 'L0_ffn_routed_gate': _L0_ffn_in['routed_gate'], 'L0_ffn_routed_down': _L0_ffn_in['routed_down'], 'L0_ffn_router_w': _L0_ffn_in['router_w'], 'L1_xattn_w1': _L1_xattn_in['w1'], 'L1_xattn_b1': _L1_xattn_in['b1'], 'L1_xattn_w2': _L1_xattn_in['w2'], 'L1_xattn_b2': _L1_xattn_in['b2'], 'L1_xattn_g1': _L1_xattn_in['g1'], 'L1_xattn_beta1': _L1_xattn_in['beta1'], 'L1_xattn_g2': _L1_xattn_in['g2'], 'L1_xattn_beta2': _L1_xattn_in['beta2'], 'L1_xattn_g3': _L1_xattn_in['g3'], 'L1_xattn_beta3': _L1_xattn_in['beta3'], 'L1_attn_Wq': _L1_attn_in['Wq'], 'L1_attn_bq': _L1_attn_in['bq'], 'L1_attn_Wk': _L1_attn_in['Wk'], 'L1_attn_bk': _L1_attn_in['bk'], 'L1_attn_Wv': _L1_attn_in['Wv'], 'L1_attn_bv': _L1_attn_in['bv'], 'L1_attn_Wo': _L1_attn_in['Wo'], 'L1_attn_bo': _L1_attn_in['bo'], 'L1_attn_Whel': _L1_attn_in['Whel'], 'L1_attn_bhel': _L1_attn_in['bhel'], 'L1_ffn_gate': _L1_ffn_in['gate'], 'L1_ffn_W1': _L1_ffn_in['W1'], 'L1_ffn_b1': _L1_ffn_in['b1'], 'L1_ffn_W2': _L1_ffn_in['W2'], 'L1_ffn_b2': _L1_ffn_in['b2']}

def reference(x, ctx_1024, L0_attn_Wk, L0_attn_Wv, L0_attn_Wr, L0_attn_Wo, L0_attn_time_decay, L0_attn_time_first, L0_attn_time_mix_key, L0_attn_time_mix_value, L0_attn_time_mix_receptance, L0_ffn_shared_up, L0_ffn_shared_gate, L0_ffn_shared_down, L0_ffn_routed_up, L0_ffn_routed_gate, L0_ffn_routed_down, L0_ffn_router_w, L1_xattn_w1, L1_xattn_b1, L1_xattn_w2, L1_xattn_b2, L1_xattn_g1, L1_xattn_beta1, L1_xattn_g2, L1_xattn_beta2, L1_xattn_g3, L1_xattn_beta3, L1_attn_Wq, L1_attn_bq, L1_attn_Wk, L1_attn_bk, L1_attn_Wv, L1_attn_bv, L1_attn_Wo, L1_attn_bo, L1_attn_Whel, L1_attn_bhel, L1_ffn_gate, L1_ffn_W1, L1_ffn_b1, L1_ffn_W2, L1_ffn_b2):
    import jax
    import jax.numpy as jnp

    def _L0_xattn_ref(x, w1, w2):
        import jax, jax.numpy as jnp
        import numpy as np
        E, T, H, F = (8, 128, 128, 512)
        h = jnp.einsum('eth,efh->etf', x, w1)
        g = jax.nn.gelu(h, approximate=True)
        out = jnp.einsum('etf,efh->eth', g, w2)
        return out

    def _L0_attn_ref(hidden, Wk, Wv, Wr, Wo, time_decay, time_first, time_mix_key, time_mix_value, time_mix_receptance):
        import math
        import jax, jax.numpy as jnp
        import numpy as np
        HIDDEN = 128
        NUM_LAYERS = 24
        LAYER_ID = 4

        def _time_params():
            h = HIDDEN
            ratio_0_to_1 = LAYER_ID / (NUM_LAYERS - 1)
            ratio_1_to_almost_0 = 1.0 - LAYER_ID / NUM_LAYERS
            zigzag = 0.5 * (jnp.arange(1, h + 1) % 3 - 1)
            time_first = jnp.full(h, math.log(0.3)) + zigzag
            idx = jnp.arange(0, h)
            time_decay = -5 + 8 * (idx / (h - 1)) ** (0.7 + 1.3 * ratio_0_to_1)
            x = jnp.arange(h) / h
            time_mix_key = jnp.power(x, ratio_1_to_almost_0)
            time_mix_value = time_mix_key + 0.3 * ratio_0_to_1
            time_mix_receptance = jnp.power(x, 0.5 * ratio_1_to_almost_0)
            return (time_decay.astype(jnp.float32), time_first.astype(jnp.float32), time_mix_key.astype(jnp.float32), time_mix_value.astype(jnp.float32), time_mix_receptance.astype(jnp.float32))

        def _wkv(time_decay, time_first, k, v):
            B, T, H = k.shape
            td = -jnp.exp(time_decay.astype(jnp.float32))
            tf = time_first.astype(jnp.float32)
            kT = jnp.swapaxes(k, 0, 1).astype(jnp.float32)
            vT = jnp.swapaxes(v, 0, 1).astype(jnp.float32)

            def step(carry, kv):
                num, den, mx = carry
                ck, cv = kv
                max_out = jnp.maximum(mx, ck + tf)
                e1 = jnp.exp(mx - max_out)
                e2 = jnp.exp(ck + tf - max_out)
                out = (e1 * num + e2 * cv) / (e1 * den + e2)
                max_st = jnp.maximum(mx + td, ck)
                e1s = jnp.exp(mx + td - max_st)
                e2s = jnp.exp(ck - max_st)
                return ((e1s * num + e2s * cv, e1s * den + e2s, max_st), out)
            init = (jnp.zeros((B, H), jnp.float32), jnp.zeros((B, H), jnp.float32), jnp.full((B, H), -1e+38, jnp.float32))
            _, outT = jax.lax.scan(step, init, (kT, vT))
            return jnp.swapaxes(outT, 0, 1).astype(k.dtype)
        shifted = jnp.pad(hidden, ((0, 0), (1, 0), (0, 0)))[:, :-1]
        k_in = hidden * time_mix_key + shifted * (1 - time_mix_key)
        v_in = hidden * time_mix_value + shifted * (1 - time_mix_value)
        r_in = hidden * time_mix_receptance + shifted * (1 - time_mix_receptance)
        k = k_in @ Wk
        v = v_in @ Wv
        r = jax.nn.sigmoid(r_in @ Wr)
        rwkv = _wkv(time_decay, time_first, k, v)
        return r * rwkv @ Wo

    def _L0_ffn_ref(x, shared_up, shared_gate, shared_down, routed_up, routed_gate, routed_down, router_w):
        import jax, jax.numpy as jnp
        import numpy as np
        H = 128
        DFF = 512
        E_ROUTED = 7
        TOP_K = 2

        def _swiglu(flat, gate_w, up_w, down_w):
            g = flat @ gate_w.T
            up = flat @ up_w.T
            return jax.nn.silu(g) * up @ down_w.T
        orig_shape = x.shape
        flat = x.reshape(-1, H)
        out = _swiglu(flat, shared_gate, shared_up, shared_down)
        logits = flat @ router_w.T
        probs = jax.nn.softmax(logits, axis=-1)
        top_vals, top_idx = jax.lax.top_k(probs, TOP_K)
        top_vals = top_vals / (top_vals.sum(-1, keepdims=True) + 1e-09)
        combine = jnp.sum(jax.nn.one_hot(top_idx, E_ROUTED, dtype=flat.dtype) * top_vals[..., None], axis=1)
        routed = jnp.zeros_like(flat)
        for e in range(E_ROUTED):
            eo = _swiglu(flat, routed_gate[e], routed_up[e], routed_down[e])
            routed = routed + combine[:, e:e + 1] * eo
        return (out + routed).reshape(orig_shape)

    def _L1_xattn_ref(y, Z, w1, b1, w2, b2, g1, beta1, g2, beta2, g3, beta3):
        import jax, jax.numpy as jnp
        import numpy as np
        B, S, D, DFF = (4, 256, 128, 512)
        EPS = 1e-05

        def layernorm(x, gamma, beta):
            mu = jnp.mean(x, axis=-1, keepdims=True)
            var = jnp.var(x, axis=-1, keepdims=True)
            return (x - mu) * jax.lax.rsqrt(var + EPS) * gamma + beta

        def attention(Q, K, V, causal):
            d_k = Q.shape[-1]
            scores = jnp.einsum('bqd,bkd->bqk', Q, K) / jnp.sqrt(jnp.asarray(d_k, Q.dtype))
            if causal:
                q_len, k_len = (scores.shape[-2], scores.shape[-1])
                mask = jnp.tril(jnp.ones((q_len, k_len), dtype=bool))
                scores = jnp.where(mask[None], scores, jnp.asarray(-jnp.inf, scores.dtype))
            w = jax.nn.softmax(scores, axis=-1)
            return jnp.einsum('bqk,bkd->bqd', w, V)
        sa = attention(y, y, y, causal=True)
        y = layernorm(y + sa, g1, beta1)
        ca = attention(y, Z, Z, causal=False)
        y = layernorm(y + ca, g2, beta2)
        h = jax.nn.relu(jnp.einsum('bsd,df->bsf', y, w1) + b1)
        ff = jnp.einsum('bsf,fd->bsd', h, w2) + b2
        y = layernorm(y + ff, g3, beta3)
        return y

    def _L1_attn_ref(x, Wq, bq, Wk, bk, Wv, bv, Wo, bo, Whel, bhel):
        import jax, jax.numpy as jnp
        import numpy as np
        import math
        B, S, E, H = (2, 256, 128, 16)
        HD = E // H
        HX = 64
        P = HX // 2

        def _l2norm(x, eps=1e-12):
            n = jnp.sqrt(jnp.sum(x * x, axis=-1, keepdims=True))
            return x / jnp.maximum(n, eps)

        def _scramble(t):
            b, h, p, s, _ = t.shape
            return jnp.swapaxes(t, -1, -2).reshape(b, h, p, s, 2)
        b, s, e = x.shape
        h, hx, hd = Whel.shape
        p = hx // 2
        q = x @ Wq.T + bq
        k = x @ Wk.T + bk
        v = x @ Wv.T + bv
        qh = q.reshape(b, s, h, hd)
        kh = k.reshape(b, s, h, hd)
        q_hel = jnp.einsum('bshd,hed->bshe', qh, Whel) + bhel
        k_hel = jnp.einsum('bshd,hed->bshe', kh, Whel) + bhel
        qn = _l2norm(q_hel.reshape(b, s, h, p, 2)).transpose(0, 2, 3, 1, 4)
        kn = _l2norm(k_hel.reshape(b, s, h, p, 2)).transpose(0, 2, 3, 1, 4)
        qn = _scramble(qn)
        kn = _scramble(kn)
        helical = jnp.einsum('bhpsc,bhptc->bhst', qn, kn) / p
        dot = jnp.einsum('bshd,bthd->bhst', qh, kh) / math.sqrt(hd)
        alpha = 0.5
        attn = jax.nn.softmax(alpha * dot + (1.0 - alpha) * helical, axis=-1)
        vh = v.reshape(b, s, h, hd)
        out = jnp.einsum('bhst,bthd->bshd', attn, vh).reshape(b, s, e)
        return out @ Wo.T + bo

    def _L1_ffn_ref(x, gate, W1, b1, W2, b2):
        import jax, jax.numpy as jnp
        import numpy as np
        N_EXPERTS = 16
        TOP_K = int(N_EXPERTS * 0.2)
        EPS = 1e-12
        raw_gate = jax.nn.softmax(jnp.einsum('btd,de->bte', x, gate), axis=-1)
        _, topk_idx = jax.lax.top_k(raw_gate, TOP_K)
        mask = jax.nn.one_hot(topk_idx, raw_gate.shape[-1], dtype=raw_gate.dtype).sum(axis=2)
        gate_topk = mask * raw_gate
        gate_topk = gate_topk / jnp.maximum(jnp.sum(jnp.abs(gate_topk), axis=-1, keepdims=True), EPS)
        hidden = jax.nn.relu(jnp.einsum('btd,edh->bteh', x, W1) + b1)
        expert_out = jnp.einsum('bteh,ehd->bted', hidden, W2) + b2
        return jnp.einsum('bte,bted->btd', gate_topk, expert_out)
    x = x + _L0_xattn_ref(_layernorm(x, axis=-1), ctx_1024, ctx_1024)
    x = x + _L0_attn_ref(_layernorm(x, axis=-1), L0_attn_Wk, L0_attn_Wv, L0_attn_Wr, L0_attn_Wo, L0_attn_time_decay, L0_attn_time_first, L0_attn_time_mix_key, L0_attn_time_mix_value, L0_attn_time_mix_receptance)
    x = x + _L0_ffn_ref(_layernorm(x, axis=-1), L0_ffn_shared_up, L0_ffn_shared_gate, L0_ffn_shared_down, L0_ffn_routed_up, L0_ffn_routed_gate, L0_ffn_routed_down, L0_ffn_router_w)
    x = x + _L1_xattn_ref(_layernorm(x, axis=-1), ctx_1024, L1_xattn_w1, L1_xattn_b1, L1_xattn_w2, L1_xattn_b2, L1_xattn_g1, L1_xattn_beta1, L1_xattn_g2, L1_xattn_beta2, L1_xattn_g3, L1_xattn_beta3)
    x = x + _L1_attn_ref(_layernorm(x, axis=-1), L1_attn_Wq, L1_attn_bq, L1_attn_Wk, L1_attn_bk, L1_attn_Wv, L1_attn_bv, L1_attn_Wo, L1_attn_bo, L1_attn_Whel, L1_attn_bhel)
    x = x + _L1_ffn_ref(_layernorm(x, axis=-1), L1_ffn_gate, L1_ffn_W1, L1_ffn_b1, L1_ffn_W2, L1_ffn_b2)
    return x

_drawn_inputs = setup_inputs


def setup_inputs(seed=0):
    import zlib

    import numpy as np

    out = dict(_drawn_inputs(seed))
    spreads = {'L1_xattn_b1': (0.0, 1.466),
     'L1_xattn_b2': (0.0, 0.438),
     'L1_xattn_g1': (1.0, 0.6),
     'L1_xattn_beta1': (0.0, 0.392),
     'L1_xattn_g2': (1.0, 0.563),
     'L1_xattn_beta2': (0.0, 0.495),
     'L1_xattn_g3': (1.0, 0.2),
     'L1_xattn_beta3': (0.0, 0.411),
     'L1_attn_bq': (0.0, 0.8),
     'L1_attn_bk': (0.0, 2.0),
     'L1_attn_bv': (0.0, 0.597),
     'L1_attn_bo': (0.0, 0.495),
     'L1_attn_bhel': (0.0, 2.0)}
    factors = {'L0_attn_Wk': 8.0,
     'L0_attn_Wv': 4.011,
     'L0_attn_Wr': 8.0,
     'L0_attn_Wo': 3.992,
     'L0_attn_time_decay': 6.473,
     'L0_attn_time_first': 8.0,
     'L0_attn_time_mix_key': 8.0,
     'L0_attn_time_mix_value': 8.0,
     'L0_attn_time_mix_receptance': 8.0,
     'L0_ffn_shared_up': 4.543,
     'L0_ffn_shared_gate': 4.307,
     'L0_ffn_shared_down': 4.322,
     'L0_ffn_routed_up': 6.346,
     'L0_ffn_routed_gate': 6.316,
     'L0_ffn_routed_down': 6.389,
     'L0_ffn_router_w': 7.794,
     'L1_attn_Wq': 8.0,
     'L1_attn_Wk': 8.0,
     'L1_attn_Wv': 8.0,
     'L1_attn_Wo': 3.582,
     'L1_attn_Whel': 200.0,
     'L1_ffn_b1': 26.234,
     'L1_ffn_b2': 6.938,
     'L1_xattn_w1': 4.48}
    for name, (base, spread) in spreads.items():
        noise = np.random.default_rng([zlib.crc32(name.encode()), seed]).standard_normal(out[name].shape)
        drawn = base * np.exp(spread * noise) if base else spread * noise
        out[name] = jnp.asarray(drawn.astype(out[name].dtype))
    for name, factor in factors.items():
        out[name] = (out[name] * factor).astype(out[name].dtype)
    return out
```

```python
from contextlib import ExitStack

import concourse.bass as bass
from concourse import mybir

F32 = mybir.dt.float32
F32R = mybir.dt.float32r
BF16 = mybir.dt.bfloat16
I32 = mybir.dt.int32
ALU = mybir.AluOpType
ACT = mybir.ActivationFunctionType
AX = mybir.AxisListType

P = 128
NSEQ, T, D = 32, 32, 128
NT = NSEQ * T // P
HT = NT // 2
HN = HT * P
SPT = P // T
SPH = SPT * HT
S = 257
EPS = 1e-5
NE0, FF0, TOP0 = 8, 512, 2
NE1, FF1, TOP1 = 16, 256, 3
FFD = 512
NH, HD, HP = 16, 8, 32
NEG = -1e38
LN2 = 0.6931471805599453
MAGIC = 0x5F3759DF

VECS = [("tmk", 1), ("tmv", 1), ("tmr", 1), ("td", 1), ("tf", 1), ("db1", FFD // P), ("bqE", 2), ("bkE", 2),
        ("bhel", NH // 2 * 2), ("bqD", 4), ("bkD", 4), ("b1m", NE1 * FF1 // P)]
MATS = [("Wk", D), ("Wv", D), ("Wr", D), ("Wo", D), ("router", NE0 - 1), ("dw1", FFD), ("dw2", FFD),
        ("WqE", D), ("WkE", D), ("WvT", D), ("WoT", D), ("Whel", NH // 2 * 2 * P), ("WqD", 4 * P), ("WkD", 4 * P),
        ("gate", NE1)]
ROWS = [("g1", D), ("be1", D), ("g2", D), ("be2", D), ("g3", D), ("be3", D), ("b2", D), ("bv", D), ("bo", D)]
CONSTS = [("ident", P), ("causal", P), ("seq4", SPT), ("slot4", SPT * HD), ("maskA", 1), ("maskB", 1),
          ("newseq", T), ("rev0", NE0 - 1), ("rev1", NE1), ("sel0", NE0 + 1), ("sel1", NE1)]
def offsets(table):
    at, out = 0, {}
    for name, width in table:
        out[name] = (at, width)
        at += width
    return out, at


VEC_AT, VEC_W = offsets(VECS)
MAT_AT, MAT_W = offsets(MATS)
ROW_AT, ROW_W = offsets(ROWS)
CON_AT, CON_W = offsets(CONSTS)


def build(nc, d):
    with ExitStack() as ctx:
        def sb(name, shape, dt=F32):
            return ctx.enter_context(nc.sbuf_tensor(name, shape, dt))

        def sem(name):
            return ctx.enter_context(nc.semaphore(name))

        turn = [ctx.enter_context(nc.psum_tensor(f"turn{k}", [P, 512], F32)) for k in range(2)]
        pair = [ctx.enter_context(nc.psum_tensor(f"pair{k}", [P, 2, 512], F32)) for k in range(3)]
        bank = [turn[k][:, :] for k in range(2)] + [pair[k][:, j, :] for k in range(3) for j in range(2)]

        vec = sb("vec", [P, VEC_W])
        mat = sb("mat", [P, MAT_W])
        row = sb("row", [P, ROW_W])
        con = sb("con", [P, CON_W])
        selb = sb("selb", [3 * NE1, NE0 + 1 + NE1], BF16)
        mb2 = sb("mb2", [3 * NE1, D])
        identb = sb("identb", [P, P], BF16)
        zerob = sb("zerob", [P, P], BF16)
        cq, ck = sb("cq", [P, 1]), sb("ck", [P, 1])

        X = sb("X", [P, NT, D])
        Y = sb("Y", [P, NT, D])
        Y2b = sb("Y2b", [P, NT * D + 8])
        Y2 = Y2b[:, 0:NT * D].rearrange("p (t h) -> p t h", t=NT)
        YT = sb("YT", [P, NT * P])
        st = sb("st", [P, NT, 6])
        mv = sb("mv", [P, NT, 2])
        ve, ry, rt = sb("ve", [P, NT]), sb("ry", [P, NT]), sb("rt", [P, NT])
        nmx, ssum = sb("nmx", [P, NT]), sb("ssum", [P, NT])
        omt, tdn = sb("omt", [P, 3]), sb("tdn", [P, 1])

        arena = sb("arena", [P, NSEQ * (S + 2 * D)])
        zT = arena[:, 0:NSEQ * S].rearrange("p (b s) -> p b s", s=S)
        z = arena[:, NSEQ * S:NSEQ * (S + 2 * D)].rearrange("p (b c h) -> p b c h", c=2, h=D)
        zlast = sb("zlast", [SPT, NT, D])
        work = sb("work", [P, 18 * HN + 8])

        W0C, W1C = 3 * FF0, 2 * 2 * FF1
        yTh, yTl = sb("yTh", [P, NT * P], F32R), sb("yTl", [P, NT * P], F32R)
        gp, gq, gr, gsel = (sb(n, [P, NT, NE1]) for n in ("gp", "gq", "gr", "gsel"))
        gs1 = sb("gs1", [P, NT])
        gpart = sb("gpart", [P, NT * 3 * NE1], BF16)
        g3b = sb("g3b", [3 * NE1, NT * P], BF16)
        wraw = sb("wraw", [P, W0C])
        wh = [sb(f"wh{k}", [P, W0C], F32R) for k in range(2)]
        wl = [sb(f"wl{k}", [P, W0C], F32R) for k in range(2)]
        xch = [sb(f"xch{k}", [P, HN], F32R) for k in range(2)]
        xcl = [sb(f"xcl{k}", [P, HN], F32R) for k in range(2)]
        ph = [sb(f"ph{k}", [P, HN], F32R) for k in range(2)]
        pl = [sb(f"pl{k}", [P, HN], F32R) for k in range(2)]

        def slot(k, n=1):
            return work[:, k * HN:(k + n) * HN]

        def vcol(name, k=0, n=1):
            return vec[:, VEC_AT[name][0] + k:VEC_AT[name][0] + k + n]

        def mcol(name, k=0, n=None):
            a, w = MAT_AT[name]
            return mat[:, a + k:a + k + (w if n is None else n)]

        def rcol(name):
            return row[:, ROW_AT[name][0]:ROW_AT[name][0] + D]

        def ccol(name):
            return con[:, CON_AT[name][0]:CON_AT[name][0] + CON_AT[name][1]]

        def half(buf, h):
            return buf[:, h * HT:(h + 1) * HT, :].rearrange("p t h -> p (t h)")

        def yt(h):
            return YT[:, h * HN:(h + 1) * HN]

        def blk(ap, i):
            return ap[:, i * P:(i + 1) * P]

        ident = ccol("ident")
        cprobs = lambda t: work[:, t * 260:t * 260 + S]
        clast = lambda t: work[:, 2100 + t * SPT:2100 + (t + 1) * SPT]
        cpT = lambda t: work[:, 2200 + t * 256:2200 + (t + 1) * 256]
        clastT = lambda t: work[0:SPT, 4300 + t * P:4300 + (t + 1) * P]
        rmix = lambda h, g: slot(3 * h + g)
        rexp = lambda h, k: slot(6 + 4 * h + k)
        mpo, mo, tdt = slot(14), slot(15), slot(16)
        run = [work[:, 17 * HN:18 * HN + 1], Y2b[:, 0:HN + 1], Y2b[:, HN + 2:2 * HN + 3]]
        rw = lambda h: rexp(h, 0)
        xc = slot(0)
        act_out, prod = [slot(1), slot(2)], [slot(3), slot(4), slot(9), slot(10)]
        moe_copy = lambda h: slot(5 + h)
        g3f = work[0:3 * NE1, 7 * HN:9 * HN]
        sprob, spT, smask = (lambda h: slot(11 + h)), (lambda h: slot(13 + h)), (lambda h: slot(15 + h))
        hid = lambda h: slot(4 * h, 4)
        qe = lambda w: slot(w)
        hb = lambda n: slot(2 + n % 4)
        sq = lambda n: slot(6 + n % 2)
        n2 = lambda n: work[:, 8 * HN + (n % 2) * 256:8 * HN + (n % 2) * 256 + 256]
        sx = lambda n: slot(9 + n % 2)
        ex = lambda n: slot(11 + n % 2)
        ets = lambda n: slot(13 + n % 2)
        oT = lambda h: slot(15 + h)
        y4 = slot(11, 4)
        hm, hsum = work[:, 17 * HN:17 * HN + 16], (lambda n: work[:, 17 * HN + 32 + 16 * (n % 2):17 * HN + 48 + 16 * (n % 2)])
        arena_slot = lambda k: arena[:, k * HN:(k + 1) * HN]
        qn = lambda w, u: arena_slot(8 * w + u)
        qd = lambda g: arena_slot(16 + g)
        kdm = lambda m, g: arena_slot(20 + 4 * m + g)
        vb = lambda i: arena_slot(28 + i)

        def parts_of(w):
            return gpart[:, 0:NT * 3 * w].rearrange("p (t n) -> p t n", t=NT)

        x_loaded, con_loaded, par_loaded, zl_loaded = sem("x_loaded"), sem("con_loaded"), sem("par_loaded"), sem("zl_loaded")
        z_loaded = [sem(f"z_loaded{t}") for t in range(NT)]
        dve_step, act_step, pool_step = sem("dve_step"), sem("act_step"), sem("pool_step")
        const_ready = sem("const_ready")
        tok_ready = sem("tok_ready")
        tr_done = sem("tr_done")
        feat_ready = sem("feat_ready")
        c_scores, c_max, c_probs, c_last, c_ptr, c_pT, c_out, c_x = (
            sem("c_" + n) for n in ("scores", "max", "probs", "last", "ptr", "pT", "out", "x"))
        r_mix, r_kvr, r_kv, r_er, r_arg, r_exp, r_rw, r_out = (
            sem("r_" + n) for n in ("mix", "kvr", "kv", "er", "arg", "exp", "rw", "out"))
        m_logits, m_shift, m_exp, m_parts, m_gT, m_g3, m_split = (
            sem("m_" + n) for n in ("logits", "shift", "exp", "parts", "gT", "g3", "split"))
        a_scores, a_masked, a_prob, a_out, a_y2 = (sem("a_" + n) for n in ("scores", "masked", "prob", "out", "y2"))
        f_h, f_relu, f_out = (sem("f_" + n) for n in ("h", "relu", "out"))
        h_e, h_ec, h_hel, h_hb, h_sq, h_n2, h_inv, h_qn, h_d, h_dc, h_v, h_vb = (
            sem("h_" + n) for n in ("e", "ec", "hel", "hb", "sq", "n2", "inv", "qn", "d", "dc", "v", "vb"))
        h_y4 = sem("h_y4")
        h_s, h_sxa, h_sxd, h_sub, h_exp, h_et, h_ets, h_pv, h_o, h_out, h_x = (
            sem("h_" + n) for n in ("s", "sxa", "sxd", "sub", "exp", "et", "ets", "pv", "o", "out", "x"))
        moe = [{n: sem(f"moe{k}_{n}") for n in (
            "wload", "whi", "wsplit", "gbc", "xcm", "xch", "xcp", "gate", "mm", "act", "mul", "hi", "prod", "down",
            "accdone", "copied", "back", "x")} for k in range(2)]
        stored = sem("stored")
        NF0, NF1 = FF0 // P, FF1 // P
        STEPS0 = [(k, h, f) for k in range(2) for h in range(2) for f in range(NF0)]
        STEPS1 = [(k, h, f) for k in range(4) for h in range(2) for f in range(NF1)]
        FREE0 = {"mul": 2, "prod": 4, "down": 2, "xcm": 2, "mm": 2 * NF0}
        FREE1 = {"mul": 2 * NF1, "prod": 4, "down": 4, "act": 4}
        WC = FF0
        WCH0, WCH1 = W0C // WC, W1C // WC
        ph4 = [b[:, 0:HN] for b in ph] + [b[:, W1C:W1C + HN] for b in wh]
        pl4 = [b[:, 0:HN] for b in pl] + [b[:, W1C:W1C + HN] for b in wl]

        def bodies(eng, n, body):
            with eng.Fori(0, n - 1) as i:
                body(i, False)
            body(n - 1, True)

        def own_wait(eng):
            eng.nop(nofuse=True)

        block = ctx.enter_context(nc.Block())

        @block.sync
        def _(sp):
            xv = d["x"].rearrange("(t p) h -> p t h", p=P)
            sp.dma_start(X[:, :, :], xv).then_inc(x_loaded, 16)
            sp.dma_start(con[:, :], d["con"]).then_inc(con_loaded, 16)
            sp.dma_start(zlast[:, :, :], d["zlast"]).then_inc(zl_loaded, 16)
            for t in range(NT):
                sp.dma_start(zT[:, SPT * t:SPT * t + SPT, :], d["zT"][t]).then_inc(z_loaded[t], 16)
                sp.dma_start(z[:, SPT * t:SPT * t + SPT, :, :], d["z"][t]).then_inc(z_loaded[t], 16)
            sp.dma_start(vec[:, :], d["vec"]).then_inc(par_loaded, 16)
            sp.dma_start(mat[:, :], d["mat"]).then_inc(par_loaded, 16)
            sp.dma_start(row[:, :], d["row"].to_broadcast([P, ROW_W])).then_inc(par_loaded, 16)
            sp.dma_start(mb2[:, :], d["mb2"]).then_inc(par_loaded, 16)
            for k, (w, cols, n) in enumerate(((d["w0"], W0C, NE0), (d["w1"], W1C, NE1 // 2))):
                m = moe[k]
                if k == 1:
                    sp.wait_ge(moe[0]["wsplit"], NE0 * WCH0)
                sp.dma_start(wraw[:, 0:cols], w[0]).then_inc(m["wload"], 16)
                with sp.Fori(1, n) as e:
                    sp.wait_ge(m["wsplit"], (WCH0, WCH1)[k] * e)
                    sp.dma_start(wraw[:, 0:cols], w[bass.ds(e, 1), :, :].rearrange("e p n -> p (e n)"))\
                        .then_inc(m["wload"], 16)
            ov = d["out"].rearrange("(t p) h -> p t h", p=P)
            for h in range(2):
                sp.wait_ge(moe[1]["x"], h + 1)
                sp.dma_start(ov[:, h * HT:(h + 1) * HT, :], X[:, h * HT:(h + 1) * HT, :]).then_inc(stored, 16)
            sp.wait_ge(stored, 32)

        @block.tensor
        def _(pe):
            turns = [0]

            def turn4(src):
                n = turns[0]
                turns[0] += 1
                pe.wait_ge(tok_ready, n + 1)
                if n >= 2:
                    pe.wait_ge(feat_ready, n - 1)
                for i in range(HT):
                    last = pe.transpose(blk(bank[n % 2], i), src(i), ident)
                last.then_inc(tr_done, 1)
                return n + 1

            def mm3(out, ah, al, bh, bl, start, stop):
                pe.matmul(out, ah, bh, start=start, stop=False)
                pe.matmul(out, ah, bl, start=False, stop=False)
                return pe.matmul(out, al, bh, start=False, stop=stop)

            def cross(h, call):
                def scores(i):
                    t, u = h * HT + i, (2 * call + h) * HT + i
                    pe.wait_ge(z_loaded[t], 32)
                    if u >= 2:
                        pe.wait_ge(c_last, u - 1)
                    for j in range(SPT):
                        b = SPT * t + j
                        last = pe.matmul(bank[2 + u % 2][T * j:T * j + T, 0:S], YT[:, b * T:(b + 1) * T], zT[:, b, :],
                                         start=True, stop=True)
                    last.then_inc(c_scores, 1)

                def weigh(i):
                    t, u = h * HT + i, (2 * call + h) * HT + i
                    pe.wait_ge(c_last, u + 1)
                    if u >= 2:
                        pe.wait_ge(c_pT, u - 1)
                    b = bank[4 + u % 2]
                    for c in range(2):
                        pe.transpose(blk(b, c), blk(cprobs(t), c), ident)
                    pe.transpose(b[0:SPT, 2 * P:3 * P], clast(t), ident).then_inc(c_ptr, 1)
                    pe.wait_ge(c_pT, u + 1)
                    if u >= 2:
                        pe.wait_ge(c_x, u - 1)
                    o = bank[6 + u % 2]
                    pe.matmul(o[:, 0:D], clastT(t), zlast[:, t, :], start=True, stop=False, skip_group_check=True)
                    for j in range(SPT):
                        for c in range(2):
                            last = pe.matmul(o[T * j:T * j + T, 0:D], cpT(t)[:, c * P + T * j:c * P + T * j + T],
                                             z[:, SPT * t + j, c, :], start=False, stop=c == 1, skip_group_check=True)
                    last.then_inc(c_out, 1)

                scores(0)
                for i in range(HT):
                    if i + 1 < HT:
                        scores(i + 1)
                    weigh(i)

            def route(name, ne, rows, call):
                for t in range(NT):
                    last = pe.matmul(bank[2][:, t * NE1:t * NE1 + ne], blk(YT, t), mcol(name), start=True, stop=True)
                last.then_inc(m_logits, 1)
                for h in range(2):
                    pe.wait_ge(m_parts, call + 1)
                    for i in range(HT):
                        last = pe.transpose(blk(bank[3 + h].bitcast(BF16), i)[0:rows, :],
                                            parts_of(rows // 3)[:, h * HT + i, :], identb[:, :])
                    last.then_inc(m_gT, 1)

            def close(acc, rows, m):
                for h in range(2):
                    last = pe.matmul(acc[h], zerob[0:rows, :], g3b[0:rows, h * HN:(h + 1) * HN], start=False, stop=True)
                last.then_inc(m["accdone"], 1)

            def turn_back(m):
                for h in range(2):
                    pe.wait_ge(m["copied"], h + 1)
                    for i in range(HT):
                        last = pe.transpose(blk(bank[2 + h], i), blk(moe_copy(h), i), ident)
                    last.then_inc(m["back"], 1)

            acc = [bank[6], bank[7]]

            def moe0():
                m = moe[0]
                ROWS = 3 * NE0

                def spread(expert, un, g):
                    h = un % 2
                    pe.wait_ge(m["xcm"], g + FREE0["xcm"] - 1)
                    own_wait(pe)
                    pe.matmul(bank[h], selb[0:ROWS, bass.ds(expert, 1)].to_broadcast([ROWS, P]),
                              g3b[0:ROWS, h * HN:(h + 1) * HN], start=True, stop=True).then_inc(m["gbc"], 1)

                def up(i, q, last=False):
                    k, h, f = STEPS0[q % len(STEPS0)]
                    expert = 2 * i + q // (2 * NF0)
                    if h == 0 and f == 0:
                        pe.wait_ge(m["wsplit"], WCH0 * (expert + 1))
                    if f == 1 and not (last and q > len(STEPS0) - NF0):
                        spread(2 * i + (q // NF0 + 1) // 2, q // NF0 + 1, 4 * i + q // NF0 + 1)
                    pe.wait_ge(m["mul"], len(STEPS0) * i + q + FREE0["mul"] - 1)
                    a, b = slice(f * P, (f + 1) * P), slice(FF0 + f * P, FF0 + (f + 1) * P)
                    cols = slice(h * HN, (h + 1) * HN)
                    mm3(bank[2 + q % 2], wh[k][:, a], wl[k][:, a], yTh[:, cols], yTl[:, cols], True, True)\
                        .then_inc(m["gate"], 1)
                    if f == 0:
                        pe.wait_ge(m["xcp"], 4 * i + q // NF0 + 1)
                    mm3(bank[4 + q % 2], wh[k][:, b], wl[k][:, b], xch[h][:, :], xcl[h][:, :], True, True)\
                        .then_inc(m["mm"], 1)

                def down(i, q):
                    k, h, f = STEPS0[q]
                    pe.wait_ge(m["prod"], len(STEPS0) * i + q + 1 + FREE0["prod"])
                    c = slice(2 * FF0 + f * P, 2 * FF0 + (f + 1) * P)
                    mm3(acc[h], wh[k][:, c], wl[k][:, c], ph[q % 2][:, :], pl[q % 2][:, :], False, False)\
                        .then_inc(m["down"], 1)

                pe.wait_ge(m_g3, 2)
                pe.wait_ge(m_split, 2)
                for h in range(2):
                    pe.matmul(acc[h], zerob[0:ROWS, :], g3b[0:ROWS, h * HN:(h + 1) * HN], start=True, stop=False)
                spread(0, 0, 0)
                pe.sem_inc(m["mm"], FREE0["mm"])
                pe.sem_inc(m["down"], FREE0["down"])
                up(0, 0)
                up(0, 1)

                def body(i, last):
                    for q in range(len(STEPS0)):
                        if not last or q + 2 < len(STEPS0):
                            up(i, q + 2, last)
                        down(i, q)

                bodies(pe, NE0 // 2, body)
                close(acc, ROWS, m)
                turn_back(m)

            def moe1():
                m = moe[1]
                pe.wait_ge(m_g3, 4)
                pe.wait_ge(m_split, 4)
                for h in range(2):
                    pe.matmul(acc[h], mb2[:, :], g3f[:, h * HN:(h + 1) * HN], start=True, stop=False)
                pe.sem_inc(m["down"], FREE1["down"])

                def up(i, q):
                    k, h, f = STEPS1[q % len(STEPS1)]
                    base, expert = len(STEPS1) * i, 4 * i + q // (2 * NF1)
                    cols = slice(h * HN, (h + 1) * HN)
                    if f == 0:
                        if h == 0 and k % 2 == 0:
                            pe.wait_ge(m["wsplit"], WCH1 * (2 * i + q // (4 * NF1) + 1))
                        pe.wait_ge(m["mul"], base + q - 2 * NF1 + NF1 + FREE1["mul"])
                        own_wait(pe)
                        pe.matmul(bank[h], selb[:, bass.ds(expert + (NE0 + 1), 1)].to_broadcast([3 * NE1, P]),
                                  g3b[:, cols], start=True, stop=True).then_inc(m["gbc"], 1)
                    pe.wait_ge(m["act"], base + q - 3 + FREE1["act"])
                    a = slice((k % 2) * 2 * FF1 + f * P, (k % 2) * 2 * FF1 + (f + 1) * P)
                    mm3(bank[2 + q % 4], wh[k // 2][:, a], wl[k // 2][:, a], yTh[:, cols], yTl[:, cols], True, True)\
                        .then_inc(m["mm"], 1)

                def down(i, q):
                    k, h, f = STEPS1[q]
                    pe.wait_ge(m["prod"], len(STEPS1) * i + q + 1 + FREE1["prod"])
                    c = slice((k % 2) * 2 * FF1 + FF1 + f * P, (k % 2) * 2 * FF1 + FF1 + (f + 1) * P)
                    mm3(acc[h], wh[k // 2][:, c], wl[k // 2][:, c], ph4[q % 4], pl4[q % 4], False, False)\
                        .then_inc(m["down"], 1)

                for q in range(3):
                    up(0, q)

                def body(i, last):
                    for q in range(len(STEPS1)):
                        if not last or q + 3 < len(STEPS1):
                            up(i, q + 3)
                        down(i, q)

                bodies(pe, NE1 // 4, body)
                close(acc, 3 * NE1, m)
                turn_back(m)

            pe.wait_ge(con_loaded, 16)
            for h in range(2):
                n = turn4(lambda i: Y[:, h * HT + i, :])
                pe.wait_ge(feat_ready, n)
                if h == 0:
                    pe.wait_ge(zl_loaded, 16)
                cross(h, 0)
            pe.wait_ge(const_ready, 1)
            for h in range(2):
                turn4(lambda i: Y[:, h * HT + i, :])
                if h == 0:
                    pe.wait_ge(c_x, 2 * HT)
                for g, name in enumerate(("Wk", "Wv", "Wr")):
                    pe.wait_ge(r_mix, 3 * h + g + 1)
                    last = pe.matmul(bank[2 + 3 * h + g], mcol(name), rmix(h, g), start=True, stop=True)
                last.then_inc(r_kvr, 1)
            for h in range(2):
                pe.wait_ge(r_rw, h + 1)
                for i in range(HT):
                    last = pe.matmul(blk(bank[2 + h], i), blk(rw(h), i), mcol("Wo"), start=True, stop=True)
                last.then_inc(r_out, 1)
            for h in range(2):
                n = turn4(lambda i: Y[:, h * HT + i, :])
            pe.wait_ge(feat_ready, n)
            route("router", NE0 - 1, 3 * NE0, 0)
            moe0()
            for h in range(2):
                n = turn4(lambda i: Y[:, h * HT + i, :])
                pe.wait_ge(feat_ready, n)
                for i in range(HT):
                    y = blk(yt(h), i)
                    last = pe.matmul(blk(bank[2 + h], i), y, y, start=True, stop=True)
                last.then_inc(a_scores, 1)
            for h in range(2):
                n = turn4(lambda i: blk(sprob(h), i))
                pe.wait_ge(feat_ready, n)
                for i in range(HT):
                    last = pe.matmul(blk(bank[6 + h], i), blk(spT(h), i), Y[:, h * HT + i, :], start=True, stop=True)
                last.then_inc(a_out, 1)
            for h in range(2):
                n = turn4(lambda i: Y2[:, h * HT + i, :])
                pe.wait_ge(feat_ready, n)
                if h == 0:
                    pe.wait_ge(a_y2, 2)
                cross(h, 1)
            for h in range(2):
                n = turn4(lambda i: Y2[:, h * HT + i, :])
                pe.wait_ge(feat_ready, n)
                if h == 0:
                    pe.wait_ge(c_x, 4 * HT)
                for f in range(FFD // P):
                    u = h * (FFD // P) + f
                    if u >= 2:
                        pe.wait_ge(f_relu, u - 1)
                    pe.matmul(bank[2 + u % 2], blk(mcol("dw1"), f), yt(h), start=True, stop=True).then_inc(f_h, 1)
                pe.wait_ge(f_relu, (h + 1) * (FFD // P))
                for i in range(HT):
                    for f in range(FFD // P):
                        last = pe.matmul(blk(bank[4 + h], i), blk(hid(h), f * HT + i), blk(mcol("dw2"), f),
                                         start=f == 0, stop=f == FFD // P - 1)
                last.then_inc(f_out, 1)

            def attend(n):
                pe.wait_ge(h_exp, n + 1)
                if n >= 1:
                    pe.wait_ge(h_ets, n)
                for g in range(4):
                    last = pe.transpose(blk(bank[6], g), blk(ex(n), g), ident)
                last.then_inc(h_et, 1)
                pe.wait_ge(h_ets, n + 1)
                if n >= 1:
                    pe.wait_ge(h_o, n)
                for g in range(4):
                    last = pe.matmul(blk(bank[7], g), blk(ets(n), g), blk(vb(n % HT), g), start=True, stop=True)
                last.then_inc(h_pv, 1)

            for h in range(2):
                n = turn4(lambda i: Y[:, h * HT + i, :])
                pe.wait_ge(feat_ready, n)
                parity = yt(h).rearrange("p (m c) -> p c m", c=2)
                if h == 1:
                    pe.wait_ge(h_x, 1)
                for w, name in enumerate(("WqE", "WkE")):
                    for g in range(2):
                        for c in range(2):
                            last = pe.matmul(bank[6 + w][64 * c:64 * c + 64, g * 256:(g + 1) * 256],
                                             mcol(name, g * 64, 64), parity[:, c, :], start=True, stop=True)
                    last.then_inc(h_e, 1)
                for w in range(2):
                    pe.wait_ge(h_ec, 2 * h + w + 1)
                    for u in range(NH // 2):
                        n = (2 * h + w) * (NH // 2) + u
                        if n >= 2:
                            pe.wait_ge(h_hb, n - 1)
                        for c in range(2):
                            last = pe.matmul(bank[2 + n % 2][:, c * 256:(c + 1) * 256], blk(mcol("Whel"), u * 2 + c),
                                             qe(w)[:, (u // 4) * 256:(u // 4 + 1) * 256], start=True, stop=True)
                        last.then_inc(h_hel, 1)
                for w, name in enumerate(("WqD", "WkD")):
                    for g in range(4):
                        n = (2 * h + w) * 4 + g
                        if n >= 2:
                            pe.wait_ge(h_dc, n - 1)
                        pe.matmul(bank[4 + n % 2], blk(mcol(name), g), yt(h), start=True, stop=True).then_inc(h_d, 1)
                pe.wait_ge(h_y4, h + 1)
                for i in range(HT):
                    n = h * HT + i
                    if i >= 2:
                        pe.wait_ge(h_vb, n - 1)
                    for j in range(SPT):
                        last = pe.matmul(blk(bank[6 + n % 2], j), blk(y4, i * SPT + j), mcol("WvT"), start=True, stop=True)
                    last.then_inc(h_v, 1)
                pe.wait_ge(h_qn, (h + 1) * NH)
                pe.wait_ge(h_dc, (h + 1) * 8)
                pe.wait_ge(h_vb, (h + 1) * HT)
                for i in range(HT):
                    n = h * HT + i
                    cols = slice(i * P, (i + 1) * P)
                    for q in range(2):
                        un = 2 * n + q
                        if un >= 2:
                            pe.wait_ge(h_sxa, un - 1)
                            pe.wait_ge(h_sxd, un - 1)
                        for k in range(4):
                            for j in range(2):
                                hd = 8 * q + 2 * k + j
                                rows = slice(64 * j, 64 * j + 64)
                                o = pair[un % 2][:, j, k * P:(k + 1) * P]
                                pe.matmul(o, qn(0, hd // 2)[rows, cols], qn(1, hd // 2)[rows, cols], start=True,
                                          stop=False, skip_group_check=True)
                                last = pe.matmul(o, qd(hd // 4)[rows, cols], kdm(hd % 4 // 2, hd // 4)[rows, cols],
                                                 start=False, stop=True, skip_group_check=True)
                        last.then_inc(h_s, 1)
                    if i >= 1:
                        attend(n - 1)
                attend((h + 1) * HT - 1)
                n = turn4(lambda i: Y[:, h * HT + i, :])
                pe.wait_ge(feat_ready, n)
                for i in range(HT):
                    last = pe.matmul(blk(bank[6], i), blk(oT(h), i), mcol("WoT"), start=True, stop=True)
                last.then_inc(h_out, 1)
            for h in range(2):
                n = turn4(lambda i: Y[:, h * HT + i, :])
            pe.wait_ge(feat_ready, n)
            route("gate", NE1, 3 * NE1, 1)
            moe1()

        @block.scalar
        def _(act):
            count = {"turn": 0, "step": 0}

            def step(ins):
                count["step"] += 1
                ins.then_inc(act_step, 1)
                act.wait_ge(act_step, count["step"])

            def copy_turned(dst):
                n = count["turn"]
                count["turn"] += 1
                act.wait_ge(tr_done, n + 1)
                act.activation(dst, bank[n % 2], ACT.Copy).then_inc(feat_ready, 1)

            scale = float(D) ** -0.5
            for h in range(2):
                copy_turned(yt(h))
                for i in range(HT):
                    u = h * HT + i
                    act.wait_ge(c_scores, u + 1)
                    act.activation(cprobs(u), bank[2 + u % 2][:, 0:S], ACT.Gelu_apprx_tanh).then_inc(c_probs, 1)
            act.wait_ge(const_ready, 1)
            step(act.activation(tdn[:, :], vcol("td"), ACT.Exp))
            for h in range(2):
                copy_turned(yt(h))
            for h in range(2):
                act.wait_ge(r_kvr, h + 1)
                for g in range(2):
                    last = act.activation(rmix(h, g), bank[2 + 3 * h + g], ACT.Copy)
                last.then_inc(r_kv, 1)
                act.activation(rmix(h, 2), bank[4 + 3 * h], ACT.Exp, scale=-1.0).then_inc(r_er, 1)
            for h in range(2):
                for k in range(4):
                    act.wait_ge(r_arg, 4 * h + k + 1)
                    act.activation(rexp(h, k), rexp(h, k), ACT.Exp).then_inc(r_exp, 1)
            for h in range(2):
                copy_turned(yt(h))
            act.wait_ge(m_shift, 1)
            act.activation(gq[:, :, 0:NE0 - 1], gq[:, :, 0:NE0 - 1], ACT.Exp).then_inc(m_exp, 1)
            def weights_hi(m, load, k, c, free):
                act.wait_ge(m["wload"], 16 * load + 16)
                if free is not None:
                    act.wait_ge(m["down"], free)
                cols = slice(c * WC, (c + 1) * WC)
                act.activation(wh[k][:, cols], wraw[:, cols], ACT.Copy).then_inc(m["whi"], 1)

            def body0(i, last):
                m, base = moe[0], len(STEPS0) * i
                for q in range(len(STEPS0)):
                    k, h, f = STEPS0[q]
                    act.wait_ge(m["gate"], base + q + 1)
                    act.wait_ge(m["mul"], base + q + FREE0["mul"] - 1)
                    act.activation(act_out[q % 2], bank[2 + q % 2], ACT.Silu).then_inc(m["act"], 1)
                    un = q // NF0
                    if f == 1 and not (last and un == 3):
                        act.wait_ge(m["xcm"], 4 * i + un + 2 + FREE0["xcm"])
                        act.wait_ge(m["mm"], NF0 * (4 * i + un) + FREE0["mm"])
                        act.activation(xch[(un + 1) % 2][:, :], xc, ACT.Copy).then_inc(m["xch"], 1)
                    c = q % (2 * NF0) - 2
                    if 0 <= c < WCH0 and not (last and k == 1):
                        weights_hi(m, 2 * i + k + 1, (k + 1) % 2, c, 2 * NF0 * (2 * i + k) + FREE0["down"])
                    act.wait_ge(m["mul"], base + q + 1 + FREE0["mul"])
                    act.wait_ge(m["down"], base + q + FREE0["down"] - 1)
                    act.activation(ph[q % 2][:, :], prod[q % 4], ACT.Copy).then_inc(m["hi"], 1)

            m = moe[0]
            act.preload_act_table(ACT.Silu)
            for c in range(WCH0):
                weights_hi(m, 0, 0, c, None)
            act.wait_ge(m["xcm"], 1 + FREE0["xcm"])
            act.activation(xch[0][:, :], xc, ACT.Copy).then_inc(m["xch"], 1)
            bodies(act, NE0 // 2, body0)
            act.wait_ge(m["accdone"], 1)
            for h in range(2):
                act.activation(moe_copy(h), bank[6 + h], ACT.Copy).then_inc(m["copied"], 1)
            for h in range(2):
                copy_turned(yt(h))
            for h in range(2):
                act.wait_ge(a_masked, h + 1)
                for i in range(HT):
                    t = h * HT + i
                    last = act.activation(blk(sprob(h), i), blk(smask(h), i), ACT.Exp, bias=nmx[:, t:t + 1],
                                          scale=scale, accum_out=ssum[:, t:t + 1])
                last.then_inc(a_prob, 1)
            for h in range(2):
                copy_turned(spT(h))
            for h in range(2):
                copy_turned(yt(h))
                for i in range(HT):
                    t, u = h * HT + i, (2 + h) * HT + i
                    act.wait_ge(c_max, t + 1)
                    act.activation(cprobs(t), bank[2 + u % 2][:, 0:S], ACT.Exp, bias=nmx[:, t:t + 1], scale=scale,
                                   accum_out=ssum[:, t:t + 1]).then_inc(c_probs, 1)
            for h in range(2):
                copy_turned(yt(h))
                for f in range(FFD // P):
                    u = h * (FFD // P) + f
                    act.wait_ge(f_h, u + 1)
                    act.activation(hid(h)[:, f * HN:(f + 1) * HN], bank[2 + u % 2], ACT.Relu,
                                   bias=vcol("db1", f)).then_inc(f_relu, 1)
            act.preload_act_table_set("natural_log_exp_and_others")
            def copy_weights(n):
                act.wait_ge(h_et, n + 1)
                if n >= 2:
                    act.wait_ge(h_pv, n - 1)
                act.activation(ets(n), bank[6], ACT.Copy).then_inc(h_ets, 1)

            for h in range(2):
                copy_turned(yt(h))
                for w in range(2):
                    for u in range(NH // 2 + 1):
                        n = (2 * h + w) * (NH // 2) + u
                        if u < NH // 2:
                            act.wait_ge(h_hb, n + 1)
                            if n >= 2:
                                act.wait_ge(h_n2, n - 1)
                            act.activation(sq(n), hb(n), ACT.Square).then_inc(h_sq, 1)
                        if u >= 1:
                            act.wait_ge(h_n2, n)
                            v = n2(n - 1)
                            step(act.activation(v, v, ACT.Ln, scale=float(2 ** 20)))
                            act.activation(v, v, ACT.Exp, scale=-0.5, bias=(cq, ck)[w][:, :]).then_inc(h_inv, 1)
                for i in range(HT):
                    n = h * HT + i
                    for q in range(2):
                        un = 2 * n + q
                        act.wait_ge(h_s, un + 1)
                        if n >= 2:
                            act.wait_ge(h_exp, n - 1)
                        for j in (2, 3):
                            rows = slice(T * j, T * j + T)
                            last = act.activation(
                                sx(n)[rows, q * 256:(q + 1) * 256].rearrange("p (j k t) -> p j k t", j=2, k=4),
                                pair[un % 2][rows, :, :].rearrange("p j (k t) -> p j k t", k=4)[:, :, :, rows], ACT.Copy)
                        last.then_inc(h_sxa, 1)
                    act.wait_ge(h_sub, n + 1)
                    if n >= 2:
                        act.wait_ge(h_et, n - 1)
                    act.activation(ex(n), sx(n), ACT.Exp).then_inc(h_exp, 1)
                    if i >= 1:
                        copy_weights(n - 1)
                copy_weights((h + 1) * HT - 1)
                copy_turned(oT(h))
            for h in range(2):
                copy_turned(yt(h))
            act.wait_ge(m_shift, 2)
            act.activation(gq[:, :, 0:NE1], gq[:, :, 0:NE1], ACT.Exp).then_inc(m_exp, 1)
            m = moe[1]
            act.sem_inc(m["act"], FREE1["act"])
            for c in range(WCH1):
                weights_hi(m, 0, 0, c, None)

            def relu(i, q):
                base = len(STEPS1) * i
                m = moe[1]
                act.wait_ge(m["mm"], base + q + 1)
                act.wait_ge(m["mul"], base + q - 1 + FREE1["mul"])
                own_wait(act)
                k, h, f = STEPS1[q % len(STEPS1)]
                at = 4 * NF1 * i + (VEC_AT["b1m"][0] + q // (2 * NF1) * NF1 + f)
                act.activation(act_out[q % 2], bank[2 + q % 4], ACT.Relu, bias=vec[:, bass.ds(at, 1)])\
                    .then_inc(m["act"], 1)

            def body1(i, last):
                m, base = moe[1], len(STEPS1) * i
                for q in range(len(STEPS1)):
                    k, h, f = STEPS1[q]
                    act.wait_ge(m["mul"], base + q + 1 + FREE1["mul"])
                    act.wait_ge(m["down"], base + q - 3 + FREE1["down"])
                    act.activation(ph4[q % 4], prod[q % 4], ACT.Copy).then_inc(m["hi"], 1)
                    if not last or q + 2 < len(STEPS1):
                        relu(i, q + 2)
                    c = q % (4 * NF1) - 2
                    if 0 <= c < WCH1 and not (last and k >= 2):
                        weights_hi(m, 2 * i + k // 2 + 1, (k // 2 + 1) % 2, c, 4 * NF1 * (2 * i + k // 2) + FREE1["down"])

            relu(0, 0)
            relu(0, 1)
            bodies(act, NE1 // 4, body1)
            act.wait_ge(m["accdone"], 1)
            for h in range(2):
                act.activation(moe_copy(h), bank[6 + h], ACT.Copy).then_inc(m["copied"], 1)

        @block.gpsimd
        def _(pool):
            pool.memset(zerob[:, :], 0.0)
            pool.memset(cq[:, :], LN2 * 10 - LN2 * 6)
            pool.memset(ck[:, :], LN2 * 10)
            pool.wait_ge(con_loaded, 16)
            pool.tensor_copy(identb[:, :], ident)
            pool.tensor_copy(selb[:, :], con[0:3 * NE1, CON_AT["sel0"][0]:CON_AT["sel1"][0] + CON_AT["sel1"][1]])\
                .then_inc(pool_step, 1)
            pool.wait_ge(pool_step, 1)
            pool.wait_ge(par_loaded, 4 * 16)
            pool.sem_inc(const_ready, 1)

            def weights_lo(m, nch, load, k):
                for c in range(nch):
                    cols = slice(c * WC, (c + 1) * WC)
                    pool.wait_ge(m["whi"], nch * load + c + 1)
                    pool.tensor_tensor(wl[k][:, cols], wraw[:, cols], wh[k][:, cols].bitcast(F32), ALU.subtract)\
                        .then_inc(m["wsplit"], 1)

            def pool_body0(i, last):
                weights_lo(moe[0], WCH0, 2 * i + 1, 1)
                if not last:
                    weights_lo(moe[0], WCH0, 2 * i + 2, 0)

            weights_lo(moe[0], WCH0, 0, 0)
            bodies(pool, NE0 // 2, pool_body0)
            for h in range(2):
                pool.wait_ge(feat_ready, 15 + 2 * h)
                rep = yt(h).rearrange("p (b a t) -> p b a t", a=1, t=T).to_broadcast([P, SPH, SPT, T])
                pool.tensor_copy(y4.rearrange("p (b a t) -> p b a t", a=SPT, t=T), rep).then_inc(h_y4, 1)

            def pool_body1(i, last):
                weights_lo(moe[1], WCH1, 2 * i + 1, 1)
                if not last:
                    weights_lo(moe[1], WCH1, 2 * i + 2, 0)

            weights_lo(moe[1], WCH1, 0, 0)
            bodies(pool, NE1 // 4, pool_body1)

        @block.vector
        def _(dve):
            count = {"step": 0}

            def step(ins):
                count["step"] += 1
                ins.then_inc(dve_step, 1)
                dve.wait_ge(dve_step, count["step"])

            def layernorm(h, src, dst):
                ts, hs = range(h * HT, (h + 1) * HT), slice(h * HT, (h + 1) * HT)
                for t in ts:
                    last = dve.bn_stats(st[:, t, :], src[:, t, :])
                step(last)
                for t in ts:
                    last = dve.bn_aggr(mv[:, t, :], st[:, t, :])
                step(last)
                v, r, w = ve[:, hs], ry[:, hs], rt[:, hs]
                step(dve.tensor_scalar(v, mv[:, hs, 1], EPS, None, ALU.add))
                step(dve.tensor_scalar(r.bitcast(I32), v.bitcast(I32), 1, None, ALU.logical_shift_right))
                step(dve.tensor_scalar(r.bitcast(I32), r.bitcast(I32), -1.0, float(MAGIC), ALU.mult, ALU.add))
                for _ in range(3):
                    step(dve.tensor_tensor(w, r, r, ALU.mult))
                    step(dve.tensor_tensor(w, w, v, ALU.mult))
                    step(dve.tensor_scalar(w, w, -0.5, 1.5, ALU.mult, ALU.add))
                    step(dve.tensor_tensor(r, r, w, ALU.mult))
                for t in ts:
                    last = dve.tensor_scalar(dst[:, t, :], src[:, t, :], mv[:, t, 0:1], ry[:, t:t + 1],
                                             ALU.subtract, ALU.mult)
                return last

            def along(name):
                return rcol(name).rearrange("p (a h) -> p a h", a=1).to_broadcast([P, HT, D])

            def affine(h, buf, g, b):
                v = buf[:, h * HT:(h + 1) * HT, :]
                step(dve.tensor_tensor(v, v, along(g), ALU.mult))
                return dve.tensor_tensor(v, v, along(b), ALU.add)

            def cross(h, call):
                for i in range(HT):
                    t, u = h * HT + i, (2 * call + h) * HT + i
                    if call == 1:
                        dve.wait_ge(c_scores, u + 1)
                        step(dve.tensor_reduce(nmx[:, t:t + 1], bank[2 + u % 2][:, 0:S], AX.X, ALU.max))
                        dve.tensor_scalar(nmx[:, t:t + 1], nmx[:, t:t + 1], -float(D) ** -0.5, None, ALU.mult)\
                            .then_inc(c_max, 1)
                    dve.wait_ge(c_probs, u + 1)
                    dve.tensor_scalar(clast(t), ccol("seq4"), cprobs(t)[:, S - 1:S], None, ALU.mult).then_inc(c_last, 1)
                    if call == 1:
                        step(dve.reciprocal(ssum[:, t:t + 1], ssum[:, t:t + 1]))
                    dve.wait_ge(c_ptr, u + 1)
                    b = bank[4 + u % 2]
                    dve.tensor_copy(clastT(t), b[0:SPT, 2 * P:3 * P])
                    dve.tensor_copy(cpT(t), b[:, 0:2 * P]).then_inc(c_pT, 1)
                    dve.wait_ge(c_out, u + 1)
                    o = bank[6 + u % 2]
                    if call == 0:
                        dve.tensor_tensor(X[:, t, :], o[:, 0:D], X[:, t, :], ALU.add).then_inc(c_x, 1)
                    else:
                        dve.scalar_tensor_tensor(Y2[:, t, :], o[:, 0:D], ssum[:, t:t + 1], Y2[:, t, :],
                                                 ALU.mult, ALU.add).then_inc(c_x, 1)
                dve.wait_ge(c_x, (2 * call + h + 1) * HT)

            def over_experts(v, ne):
                return v[:, :].rearrange("p (t a) -> p t a", a=1).to_broadcast([P, NT, ne])

            def softmax_router(ne, r0, call):
                dve.wait_ge(m_logits, call + 1)
                lg = bank[2][:, 0:NT * NE1].rearrange("p (t e) -> p t e", e=NE1)[:, :, 0:ne]
                step(dve.tensor_reduce(gs1[:, :], lg, AX.X, ALU.max))
                dve.tensor_tensor(gq[:, :, 0:ne], lg, over_experts(gs1, ne), ALU.subtract).then_inc(m_shift, 1)
                dve.wait_ge(m_exp, call + 1)
                step(dve.tensor_reduce(gs1[:, :], gq[:, :, 0:ne], AX.X, ALU.add))
                step(dve.reciprocal(gs1[:, :], gs1[:, :]))
                step(dve.tensor_tensor(gp[:, :, r0:r0 + ne], gq[:, :, 0:ne], over_experts(gs1, ne), ALU.mult))

            def keep_top(k, ne, r0, rev):
                pv, qv, rv, sv = (b[:, :, r0:r0 + ne] for b in (gp, gq, gr, gsel))
                order = ccol(rev).rearrange("p (a e) -> p a e", a=1).to_broadcast([P, NT, ne])
                step(dve.tensor_copy(qv, pv))
                for j in range(k):
                    step(dve.tensor_reduce(gs1[:, :], qv, AX.X, ALU.max))
                    step(dve.tensor_tensor(rv, qv, over_experts(gs1, ne), ALU.is_equal))
                    step(dve.tensor_tensor(rv, rv, order, ALU.mult))
                    step(dve.tensor_reduce(gs1[:, :], rv, AX.X, ALU.max))
                    step(dve.tensor_tensor(rv, rv, over_experts(gs1, ne), ALU.is_equal))
                    if j == 0:
                        step(dve.tensor_copy(sv, rv))
                    else:
                        step(dve.tensor_tensor(sv, sv, rv, ALU.add))
                    step(dve.scalar_tensor_tensor(qv, rv, -2.0, qv, ALU.mult, ALU.add))
                step(dve.tensor_tensor(pv, pv, sv, ALU.mult))
                step(dve.tensor_reduce(gs1[:, :], pv, AX.X, ALU.add))

            def routing_parts(w, call):
                p3 = [parts_of(w)[:, :, a * w:(a + 1) * w] for a in range(3)]
                r, g = gr[:, :, 0:w], gp[:, :, 0:w]
                step(dve.tensor_copy(p3[0], g))
                step(dve.tensor_tensor(r, g, p3[0], ALU.subtract))
                step(dve.tensor_copy(p3[1], r))
                step(dve.tensor_tensor(r, r, p3[1], ALU.subtract))
                dve.tensor_copy(p3[2], r).then_inc(m_parts, 1)
                for h in range(2):
                    dve.wait_ge(m_gT, 2 * call + h + 1)
                    src = bank[3 + h].bitcast(BF16)[0:3 * w, 0:HN]
                    c = slice(h * HN, (h + 1) * HN)
                    if call == 1:
                        dve.tensor_copy(g3f[:, c], src)
                    dve.tensor_copy(g3b[0:3 * w, c], src).then_inc(m_g3, 1)

            def split_y(h, turns):
                dve.wait_ge(feat_ready, turns)
                c = slice(h * HN, (h + 1) * HN)
                step(dve.tensor_copy(yTh[:, c], YT[:, c]))
                dve.tensor_tensor(yTl[:, c], YT[:, c], yTh[:, c].bitcast(F32), ALU.subtract).then_inc(m_split, 1)

            def moe_end(m):
                for h in range(2):
                    dve.wait_ge(m["back"], h + 1)
                    dve.tensor_tensor(half(X, h), bank[2 + h], half(X, h), ALU.add).then_inc(m["x"], 1)

            dve.wait_ge(x_loaded, 16)
            for h in range(2):
                layernorm(h, X, Y).then_inc(tok_ready, 1)
            dve.wait_ge(con_loaded, 16)
            for h in range(2):
                cross(h, 0)
            dve.wait_ge(const_ready, 1)
            for h in range(2):
                layernorm(h, X, Y).then_inc(tok_ready, 1)
            for g, name in enumerate(("tmk", "tmv", "tmr")):
                dve.tensor_scalar(omt[:, g:g + 1], vcol(name), -1.0, 1.0, ALU.mult, ALU.add)
            for r in run:
                dve.memset(r[:, 0:1], 0.0)
            dve.wait_ge(act_step, 1)
            step(dve.tensor_scalar(tdn[:, :], tdn[:, :], -1.0, None, ALU.mult))
            newseq = ccol("newseq").rearrange("p (a t) -> p a t", a=1).to_broadcast([P, SPH, T])
            step(dve.tensor_scalar(tdt.rearrange("p (b t) -> p b t", t=T), newseq, tdn[:, :], None, ALU.add))
            for h in range(2):
                dve.wait_ge(feat_ready, 2 + h + 1)
                yv = yt(h).rearrange("p (b t) -> p b t", t=T)
                for g, name in enumerate(("tmk", "tmv", "tmr")):
                    mix = rmix(h, g).rearrange("p (b t) -> p b t", t=T)
                    step(dve.tensor_scalar(rmix(h, g), yt(h), vcol(name), None, ALU.mult))
                    dve.scalar_tensor_tensor(mix[:, :, 1:T], yv[:, :, 0:T - 1], omt[:, g:g + 1], mix[:, :, 1:T],
                                             ALU.mult, ALU.add).then_inc(r_mix, 1)
            for h in range(2):
                dve.wait_ge(r_kv, h + 1)
                K, V = rmix(h, 0), rmix(h, 1)
                E1S, E2S, E1, E2 = (rexp(h, k) for k in range(4))
                mx, num, den = (r[:, 1:HN + 1] for r in run)
                mxp, nump, denp = (r[:, 0:HN] for r in run)
                step(dve.tensor_tensor_scan(mx, tdt, K, NEG, ALU.add, ALU.max))
                step(dve.tensor_tensor(E1S, mxp, tdt, ALU.add))
                dve.tensor_tensor(E1S, E1S, mx, ALU.subtract).then_inc(r_arg, 1)
                dve.tensor_tensor(E2S, K, mx, ALU.subtract).then_inc(r_arg, 1)
                b3 = lambda a: a.rearrange("p (b t) -> p b t", t=T)
                step(dve.tensor_tensor(b3(mpo), b3(mxp), newseq, ALU.add))
                step(dve.scalar_tensor_tensor(mo, K, vcol("tf"), mpo, ALU.add, ALU.max))
                dve.tensor_tensor(E1, mpo, mo, ALU.subtract).then_inc(r_arg, 1)
                dve.scalar_tensor_tensor(E2, K, vcol("tf"), mo, ALU.add, ALU.subtract).then_inc(r_arg, 1)
                dve.wait_ge(r_exp, 4 * h + 4)
                step(dve.tensor_tensor(mpo, E2S, V, ALU.mult))
                dve.tensor_tensor_scan(num, E1S, mpo, 0.0, ALU.mult, ALU.add)
                step(dve.tensor_tensor_scan(den, E1S, E2S, 0.0, ALU.mult, ALU.add))
                dve.tensor_tensor(mpo, E1, nump, ALU.mult)
                step(dve.tensor_tensor(mo, E2, V, ALU.mult))
                dve.tensor_tensor(mpo, mpo, mo, ALU.add)
                step(dve.tensor_tensor(E1S, E1, denp, ALU.mult))
                step(dve.tensor_tensor(mo, E1S, E2, ALU.add))
                dve.wait_ge(r_er, h + 1)
                step(dve.scalar_tensor_tensor(mo, rmix(h, 2), 1.0, mo, ALU.add, ALU.mult))
                step(dve.reciprocal(mo, mo))
                dve.tensor_tensor(rw(h), mpo, mo, ALU.mult).then_inc(r_rw, 1)
            for h in range(2):
                dve.wait_ge(r_out, h + 1)
                step(dve.tensor_tensor(half(X, h), bank[2 + h], half(X, h), ALU.add))
                layernorm(h, X, Y).then_inc(tok_ready, 1)
            for h in range(2):
                split_y(h, 4 + h + 1)
            softmax_router(NE0 - 1, 1, 0)
            keep_top(TOP0, NE0 - 1, 1, "rev0")
            step(dve.tensor_scalar(gs1[:, :], gs1[:, :], 1e-9, None, ALU.add))
            step(dve.reciprocal(gs1[:, :], gs1[:, :]))
            step(dve.tensor_tensor(gp[:, :, 1:NE0], gp[:, :, 1:NE0], over_experts(gs1, NE0 - 1), ALU.mult))
            step(dve.memset(gp[:, :, 0:1], 1.0))
            routing_parts(NE0, 0)
            m = moe[0]
            dve.sem_inc(m["mul"], FREE0["mul"])
            dve.sem_inc(m["prod"], FREE0["prod"])
            dve.sem_inc(m["xcm"], FREE0["xcm"])

            def scale_input(un, g):
                dve.wait_ge(m["gbc"], g + 1)
                dve.tensor_tensor(xc, bank[un % 2], yt(un % 2), ALU.mult).then_inc(m["xcm"], 1)

            def input_lo(un, g):
                dve.wait_ge(m["xch"], g + 1)
                dve.tensor_tensor(xcl[un % 2][:, :], xc, xch[un % 2][:, :].bitcast(F32), ALU.subtract)\
                    .then_inc(m["xcp"], 1)

            scale_input(0, 0)
            input_lo(0, 0)

            def body0(i, last):
                base = len(STEPS0) * i
                for q in range(len(STEPS0)):
                    k, h, f = STEPS0[q]
                    dve.wait_ge(m["act"], base + q + 1)
                    dve.wait_ge(m["mm"], base + q + 1 + FREE0["mm"])
                    dve.wait_ge(m["prod"], base + q - 3 + FREE0["prod"])
                    dve.tensor_tensor(prod[q % 4], act_out[q % 2], bank[4 + q % 2], ALU.mult).then_inc(m["mul"], 1)
                    un = q // NF0
                    if f == 0 and not (last and un == 3):
                        dve.wait_ge(m["xcp"], 4 * i + un + 1)
                        scale_input(un + 1, 4 * i + un + 1)
                    if f == 1 and not (last and un == 3):
                        input_lo(un + 1, 4 * i + un + 1)
                    dve.wait_ge(m["hi"], base + q + 1)
                    dve.tensor_tensor(pl[q % 2][:, :], prod[q % 4], ph[q % 2][:, :].bitcast(F32), ALU.subtract)\
                        .then_inc(m["prod"], 1)

            bodies(dve, NE0 // 2, body0)
            moe_end(m)
            dve.wait_ge(m["x"], 2)
            for h in range(2):
                layernorm(h, X, Y).then_inc(tok_ready, 1)
            for h in range(2):
                hs = slice(h * HT, (h + 1) * HT)
                s3 = smask(h).rearrange("p (t k) -> p t k", t=HT)
                causal = ccol("causal").rearrange("p (a k) -> p a k", a=1).to_broadcast([P, HT, P])
                dve.wait_ge(a_scores, h + 1)
                step(dve.tensor_tensor(s3, bank[2 + h].rearrange("p (t k) -> p t k", t=HT), causal, ALU.add))
                step(dve.tensor_reduce(nmx[:, hs], s3, AX.X, ALU.max))
                dve.tensor_scalar(nmx[:, hs], nmx[:, hs], -float(D) ** -0.5, None, ALU.mult).then_inc(a_masked, 1)
            for h in range(2):
                hs = slice(h * HT, (h + 1) * HT)
                dve.wait_ge(a_prob, h + 1)
                dve.sem_inc(tok_ready, 1)
                step(dve.reciprocal(ssum[:, hs], ssum[:, hs]))
            for h in range(2):
                dve.wait_ge(a_out, h + 1)
                for i in range(HT):
                    t = h * HT + i
                    last = dve.scalar_tensor_tensor(Y2[:, t, :], blk(bank[6 + h], i), ssum[:, t:t + 1], Y[:, t, :],
                                                    ALU.mult, ALU.add)
                last.then_inc(a_y2, 1)
                dve.wait_ge(a_y2, h + 1)
                step(layernorm(h, Y2, Y2))
                affine(h, Y2, "g1", "be1").then_inc(tok_ready, 1)
            dve.wait_ge(tok_ready, 12)
            for h in range(2):
                cross(h, 1)
            for h in range(2):
                step(layernorm(h, Y2, Y2))
                affine(h, Y2, "g2", "be2").then_inc(tok_ready, 1)
            for h in range(2):
                dve.wait_ge(tok_ready, 13 + h)
                dve.wait_ge(tr_done, 13 + h)
                v = Y2[:, h * HT:(h + 1) * HT, :]
                step(dve.tensor_tensor(v, v, along("b2"), ALU.add))
                dve.wait_ge(f_out, h + 1)
                step(dve.tensor_tensor(half(Y2, h), bank[4 + h], half(Y2, h), ALU.add))
                step(layernorm(h, Y2, Y2))
                step(affine(h, Y2, "g3", "be3"))
                step(dve.tensor_tensor(half(X, h), half(Y2, h), half(X, h), ALU.add))
            turns = 14
            for h in range(2):
                layernorm(h, X, Y).then_inc(tok_ready, 1)
                turns += 1
                for w, name in enumerate(("bqE", "bkE")):
                    dve.wait_ge(h_e, 2 * h + w + 1)
                    bias = vcol(name, 0, 2).rearrange("p (g a) -> p g a", a=1).to_broadcast([P, 2, 256])
                    dve.tensor_tensor(qe(w).rearrange("p (g m) -> p g m", g=2),
                                      bank[6 + w].rearrange("p (g m) -> p g m", g=2), bias, ALU.add).then_inc(h_ec, 1)

                def rotations(n):
                    u = n % (NH // 2)
                    bias = vcol("bhel", 2 * u, 2).rearrange("p (c a) -> p c a", a=1).to_broadcast([P, 2, 256])
                    dve.wait_ge(h_hel, n + 1)
                    dve.tensor_tensor(hb(n).rearrange("p (c m) -> p c m", c=2),
                                      bank[2 + n % 2].rearrange("p (c m) -> p c m", c=2), bias, ALU.add).then_inc(h_hb, 1)

                def norms(n):
                    dve.wait_ge(h_sq, n + 1)
                    if n >= 2:
                        dve.wait_ge(h_qn, n - 1)
                    step(dve.tensor_tensor(n2(n), sq(n)[:, 0:256], sq(n)[:, 256:512], ALU.add))
                    dve.tensor_scalar(n2(n), n2(n), 1e-24, None, ALU.max).then_inc(h_n2, 1)

                def normalise(n):
                    w, u = n // (NH // 2) % 2, n % (NH // 2)
                    dve.wait_ge(h_inv, n + 1)
                    inv = n2(n).rearrange("p (a m) -> p a m", a=1).rearrange("p a (b s) -> p (a b) s", s=T // 2)
                    for c in range(2):
                        out = qn(w, u).rearrange("p (b c s) -> p c b s", c=2, s=T // 2)[:, c]
                        src = hb(n)[:, c * 256:(c + 1) * 256].rearrange("p (b s) -> p b s", s=T // 2)
                        last = dve.tensor_tensor(out, src, inv, ALU.mult)
                    last.then_inc(h_qn, 1)

                n0 = 2 * h * (NH // 2)
                for k in range(NH + 2):
                    if k < NH:
                        rotations(n0 + k)
                    if 1 <= k <= NH:
                        norms(n0 + k - 1)
                    if k >= 2:
                        normalise(n0 + k - 2)
                for w, name in enumerate(("bqD", "bkD")):
                    for g in range(4):
                        n = (2 * h + w) * 4 + g
                        dve.wait_ge(h_d, n + 1)
                        b = bank[4 + n % 2]
                        if w == 0:
                            dve.tensor_scalar(qd(g), b, vcol(name, g), 0.5 * float(HD) ** -0.5, ALU.add, ALU.mult)\
                                .then_inc(h_dc, 1)
                        else:
                            dve.tensor_scalar(kdm(0, g), b, vcol(name, g), ccol("maskA"), ALU.add, ALU.mult)
                            dve.tensor_scalar(kdm(1, g), b, vcol(name, g), ccol("maskB"), ALU.add, ALU.mult)\
                                .then_inc(h_dc, 1)
                for i in range(HT):
                    n = h * HT + i
                    dve.wait_ge(h_v, n + 1)
                    keep = ccol("slot4").rearrange("p (a x) -> p a x", a=1).to_broadcast([P, 4, 32])
                    for j in range(SPT):
                        last = dve.tensor_tensor(vb(i).rearrange("p (g b x) -> p b g x", g=4, b=4)[:, j],
                                                 blk(bank[6 + n % 2], j).rearrange("p (g x) -> p g x", g=4), keep, ALU.mult)
                    last.then_inc(h_vb, 1)

                def by_head(v, m):
                    return v.rearrange("p (g a) -> p g a", a=1).to_broadcast([v.shape[0], NH, m])

                def result(n):
                    dve.wait_ge(h_exp, n + 1)
                    r = hsum(n)
                    step(dve.tensor_reduce(r, ex(n).rearrange("p (g t) -> p g t", t=T), AX.X, ALU.add))
                    step(dve.reciprocal(r, r))
                    dve.wait_ge(h_pv, n + 1)
                    for j in range(SPT):
                        rows = slice(T * j, T * j + T)
                        inv = r[rows, :].rearrange("p (g s a) -> p g s a", g=4, a=1).to_broadcast([T, 4, 4, HD])
                        src = bank[7][rows, :].rearrange("p (g b s x) -> p b g s x", g=4, b=4, s=4)[:, j]
                        out = Y[rows, n, :].rearrange("p (g s x) -> p g s x", g=4, s=4)
                        last = dve.tensor_tensor(out, src, inv, ALU.mult)
                    last.then_inc(h_o, 1)

                for i in range(HT):
                    n = h * HT + i
                    for q in range(2):
                        un = 2 * n + q
                        dve.wait_ge(h_s, un + 1)
                        for j in (0, 1):
                            rows = slice(T * j, T * j + T)
                            last = dve.tensor_copy(
                                sx(n)[rows, q * 256:(q + 1) * 256].rearrange("p (j k t) -> p j k t", j=2, k=4),
                                pair[un % 2][rows, :, :].rearrange("p j (k t) -> p j k t", k=4)[:, :, :, rows])
                        last.then_inc(h_sxd, 1)
                    dve.wait_ge(h_sxd, 2 * n + 2)
                    dve.wait_ge(h_sxa, 2 * n + 2)
                    s3 = sx(n).rearrange("p (g t) -> p g t", t=T)
                    step(dve.tensor_reduce(hm, s3, AX.X, ALU.max))
                    dve.tensor_tensor(s3, s3, by_head(hm, T), ALU.subtract).then_inc(h_sub, 1)
                    if i >= 1:
                        result(n - 1)
                result((h + 1) * HT - 1)
                dve.wait_ge(h_o, (h + 1) * HT)
                v = Y[:, h * HT:(h + 1) * HT, :]
                dve.tensor_tensor(v, v, along("bv"), ALU.add).then_inc(tok_ready, 1)
                turns += 1
                xv = X[:, h * HT:(h + 1) * HT, :]
                step(dve.tensor_tensor(xv, xv, along("bo"), ALU.add))
                dve.wait_ge(h_out, h + 1)
                dve.tensor_tensor(half(X, h), bank[6], half(X, h), ALU.add).then_inc(h_x, 1)
            dve.wait_ge(h_x, 2)
            for h in range(2):
                layernorm(h, X, Y).then_inc(tok_ready, 1)
            for h in range(2):
                split_y(h, turns + h + 1)
            softmax_router(NE1, 0, 1)
            keep_top(TOP1, NE1, 0, "rev1")
            step(dve.tensor_scalar(gs1[:, :], gs1[:, :], 1e-12, None, ALU.max))
            step(dve.reciprocal(gs1[:, :], gs1[:, :]))
            step(dve.tensor_tensor(gp[:, :, :], gp[:, :, :], over_experts(gs1, NE1), ALU.mult))
            routing_parts(NE1, 1)
            m = moe[1]
            dve.sem_inc(m["mul"], FREE1["mul"])
            dve.sem_inc(m["prod"], FREE1["prod"])

            def weigh(i, q):
                base = len(STEPS1) * i
                k, h, f = STEPS1[q % len(STEPS1)]
                dve.wait_ge(m["act"], base + q + 1 + FREE1["act"])
                if f == 0:
                    dve.wait_ge(m["gbc"], 8 * i + q // NF1 + 1)
                dve.wait_ge(m["prod"], base + q - 3 + FREE1["prod"])
                dve.tensor_tensor(prod[q % 4], act_out[q % 2], bank[h], ALU.mult).then_inc(m["mul"], 1)

            def body1(i, last):
                for q in range(len(STEPS1)):
                    if not last or q + 1 < len(STEPS1):
                        weigh(i, q + 1)
                    dve.wait_ge(m["hi"], len(STEPS1) * i + q + 1)
                    dve.tensor_tensor(pl4[q % 4], prod[q % 4], ph4[q % 4].bitcast(F32), ALU.subtract)\
                        .then_inc(m["prod"], 1)

            weigh(0, 0)
            bodies(dve, NE1 // 4, body1)
            moe_end(m)


def kernel(**inputs):
    import numpy as np
    import concourse.bacc as bacc
    from concourse.bass_utils import run_bass_kernel_spmd

    a = {k: np.asarray(v) for k, v in inputs.items()}
    f32 = np.float32

    def columns(v, n):
        return v.reshape(n, P).T

    def chunks(m):
        return m.reshape(-1, P, m.shape[1]).transpose(1, 0, 2).reshape(P, -1)

    slots = [8 * q + 2 * k + j for q in range(2) for j in range(2) for k in range(4)]
    slot_feats = np.array([s * HD + e for s in slots for e in range(HD)])
    strip_of = {0: 0, 2: 1, 1: 2, 3: 3}

    def strips(m):
        out = np.zeros((m.shape[1], 4, 4, T), f32)
        for g in range(4):
            for r, s in strip_of.items():
                out[:, g, s, 0:HD] = m[(4 * g + r) * HD:(4 * g + r + 1) * HD].T
        return out.reshape(m.shape[1], 4 * P)

    wh_ = a["L1_attn_Whel"].reshape(NH, HP, 2, HD)
    whel = np.zeros((2, 8, HD, NH // 2, 2, 2, 2, HP), f32)
    bhel = np.zeros((2, 2, HP, NH // 2, 2), f32)
    for u in range(NH // 2):
        for j in range(2):
            hd = 2 * u + j
            for par in range(2):
                for c in range(2):
                    whel[par, hd % 8, :, u, c, j, par, :] = wh_[hd, :, c, :].T
                    bhel[j, par, :, u, c] = a["L1_attn_bhel"][hd].reshape(HP, 2)[:, c]
    whel = whel.reshape(P, -1)
    bhel = bhel.reshape(P, -1)

    def parity_bias(b):
        return np.concatenate([b.reshape(2, 64).T] * 2, 0)

    vecs = {"tmk": a["L0_attn_time_mix_key"][:, None], "tmv": a["L0_attn_time_mix_value"][:, None],
            "tmr": a["L0_attn_time_mix_receptance"][:, None], "td": a["L0_attn_time_decay"][:, None],
            "tf": a["L0_attn_time_first"][:, None], "db1": columns(a["L1_xattn_b1"], FFD // P),
            "bqE": parity_bias(a["L1_attn_bq"]), "bkE": parity_bias(a["L1_attn_bk"]), "bhel": bhel,
            "bqD": strips(a["L1_attn_bq"][:, None]).reshape(4, P).T, "bkD": strips(a["L1_attn_bk"][:, None]).reshape(4, P).T,
            "b1m": columns(a["L1_ffn_b1"].reshape(-1), NE1 * FF1 // P)}
    mats = {"Wk": a["L0_attn_Wk"], "Wv": a["L0_attn_Wv"], "Wr": a["L0_attn_Wr"], "Wo": a["L0_attn_Wo"],
            "router": a["L0_ffn_router_w"].T, "dw1": a["L1_xattn_w1"], "dw2": chunks(a["L1_xattn_w2"]),
            "WqE": a["L1_attn_Wq"].T, "WkE": a["L1_attn_Wk"].T, "WvT": a["L1_attn_Wv"][slot_feats].T,
            "WoT": a["L1_attn_Wo"].T[slot_feats], "Whel": whel, "WqD": strips(a["L1_attn_Wq"]),
            "WkD": strips(a["L1_attn_Wk"]), "gate": a["L1_ffn_gate"]}
    rows = {"g1": a["L1_xattn_g1"], "be1": a["L1_xattn_beta1"], "g2": a["L1_xattn_g2"], "be2": a["L1_xattn_beta2"],
            "g3": a["L1_xattn_g3"], "be3": a["L1_xattn_beta3"], "b2": a["L1_xattn_b2"],
            "bv": a["L1_attn_bv"][slot_feats], "bo": a["L1_attn_bo"]}

    tok = np.arange(P)
    same = tok[:, None] // T == tok[None, :] // T
    sel = np.zeros((P, NE0 + 1 + NE1), f32)
    for part in range(3):
        for e in range(NE0):
            sel[part * NE0 + e, e] = 1
        for e in range(NE1):
            sel[part * NE1 + e, NE0 + 1 + e] = 1
    consts = {"ident": np.eye(P), "causal": np.where(same & (tok[None, :] <= tok[:, None]), 0, NEG),
              "seq4": tok[:, None] // T == np.arange(SPT), "slot4": tok[:, None] // T == np.arange(SPT * HD) // HD,
              "maskA": (tok // T % 2 == 0)[:, None], "maskB": (tok // T % 2 == 1)[:, None],
              "newseq": np.broadcast_to(np.where(np.arange(T) == 0, NEG, 0), (P, T)),
              "rev0": np.broadcast_to(np.arange(NE0 - 1, 0, -1), (P, NE0 - 1)),
              "rev1": np.broadcast_to(np.arange(NE1, 0, -1), (P, NE1)),
              "sel0": sel[:, 0:NE0 + 1], "sel1": sel[:, NE0 + 1:]}

    def pack(table, parts):
        for name, width in table:
            assert parts[name].shape[1] == width, (name, parts[name].shape)
        return np.concatenate([np.asarray(parts[name], f32) for name, _ in table], 1)

    ctx_ = a["ctx_1024"].reshape(NT, SPT, S, D)
    gate = np.concatenate([a["L0_ffn_shared_gate"][None], a["L0_ffn_routed_gate"]])
    up = np.concatenate([a["L0_ffn_shared_up"][None], a["L0_ffn_routed_up"]])
    down = np.concatenate([a["L0_ffn_shared_down"][None], a["L0_ffn_routed_down"]])
    down = down.transpose(0, 2, 1).reshape(NE0, FF0 // P, P, D).transpose(0, 2, 1, 3).reshape(NE0, P, FF0)
    w2 = a["L1_ffn_W2"].reshape(NE1, FF1 // P, P, D).transpose(0, 2, 1, 3).reshape(NE1, P, FF1)
    w1 = np.concatenate([a["L1_ffn_W1"], w2], 2)
    arrays = {
        "x": a["x"].reshape(NT * P, D),
        "zT": ctx_.transpose(0, 3, 1, 2), "z": ctx_[:, :, 0:2 * P].reshape(NT, SPT, 2, P, D).transpose(0, 3, 1, 2, 4),
        "zlast": ctx_[:, :, S - 1].transpose(1, 0, 2),
        "vec": pack(VECS, vecs), "mat": pack(MATS, mats), "row": pack(ROWS, {k: v[None] for k, v in rows.items()}),
        "con": pack(CONSTS, consts), "mb2": np.concatenate([a["L1_ffn_b2"]] * 3),
        "w0": np.concatenate([gate.transpose(0, 2, 1), up.transpose(0, 2, 1), down], 2),
        "w1": w1.reshape(NE1 // 2, 2, P, 2 * FF1).transpose(0, 2, 1, 3).reshape(NE1 // 2, P, 4 * FF1),
    }
    arrays = {k: np.ascontiguousarray(v) for k, v in arrays.items()}

    nc = bacc.Bacc("TRN2", target_bir_lowering=False, num_devices=1)
    args = {k: nc.dram_tensor(f"in_{k}", v.shape, F32, kind="ExternalInput").ap() for k, v in arrays.items()}
    args["out"] = nc.dram_tensor("out_x", (NT * P, D), F32, kind="ExternalOutput").ap()
    build(nc, args)
    r = run_bass_kernel_spmd(nc, [{f"in_{k}": v for k, v in arrays.items()}], core_ids=[0])
    return r.results[0]["out_x"].reshape(NSEQ, T, D)
```

```python
import math
from contextlib import ExitStack

import concourse.bass as bass
from concourse import mybir

F32 = mybir.dt.float32
F32R = mybir.dt.float32r
BF16 = mybir.dt.bfloat16
I32 = mybir.dt.int32
ALU = mybir.AluOpType
ACT = mybir.ActivationFunctionType
AX = mybir.AxisListType

P = 128
NSEQ, T, D = 32, 32, 128
NT = NSEQ * T // P
HT = NT // 2
HN = HT * P
SPT = P // T
SPH = SPT * HT
S = 257
EPS = 1e-5
NE0, FF0, TOP0 = 8, 512, 2
NE1, FF1, TOP1 = 16, 256, 3
FFD = 512
NH, HD, HP = 16, 8, 32
NEG = -1e38
LN2 = math.log(2.0)
QF = float(HD) ** 0.5 / HP
MAGIC = 0x5F3759DF

VECS = [("tmk", 1), ("tmv", 1), ("tmr", 1), ("td", 1), ("tf", 1), ("db1", FFD // P), ("bqE", 2), ("bkE", 2),
        ("b1m", NE1 * FF1 // P)]
MATS = [("Wk", D), ("Wv", D), ("Wr", D), ("Wo", D), ("router", NE0 - 1), ("dw1", FFD), ("dw2", FFD),
        ("WqE", D), ("WkE", D), ("WvT", D), ("WoT", D), ("Whel", NH // 2 * 2 * P), ("WqD", 4 * P), ("WkD", 4 * P),
        ("gate", NE1)]
ROWS = [("g1", D), ("be1", D), ("g2", D), ("be2", D), ("g3", D), ("be3", D), ("b2", D), ("bv", D), ("bo", D)]
CONSTS = [("ident", P), ("causal", P), ("seq4", SPT), ("slot4", SPT * HD), ("biaslo", 1), ("maskA", 1), ("maskB", 1),
          ("newseq", T), ("rev0", NE0 - 1), ("rev1", NE1), ("sel0", NE0 + 1), ("sel1", NE1)]
def offsets(table):
    at, out = 0, {}
    for name, width in table:
        out[name] = (at, width)
        at += width
    return out, at


VEC_AT, VEC_W = offsets(VECS)
MAT_AT, MAT_W = offsets(MATS)
ROW_AT, ROW_W = offsets(ROWS)
CON_AT, CON_W = offsets(CONSTS)


def build(nc, d):
    with ExitStack() as ctx:
        def sb(name, shape, dt=F32):
            return ctx.enter_context(nc.sbuf_tensor(name, shape, dt))

        def sem(name):
            return ctx.enter_context(nc.semaphore(name))

        turn = [ctx.enter_context(nc.psum_tensor(f"turn{k}", [P, 512], F32)) for k in range(2)]
        pair = [ctx.enter_context(nc.psum_tensor(f"pair{k}", [P, 2, 512], F32)) for k in range(3)]
        bank = [turn[k][:, :] for k in range(2)] + [pair[k][:, j, :] for k in range(3) for j in range(2)]

        vec = sb("vec", [P, VEC_W])
        mat = sb("mat", [P, MAT_W])
        row = sb("row", [P, ROW_W])
        con = sb("con", [P, CON_W])
        selb = sb("selb", [3 * NE1, NE0 + 1 + NE1], BF16)
        mb2 = sb("mb2", [3 * NE1, D])
        identb = sb("identb", [P, P], BF16)
        zerob = sb("zerob", [P, P], BF16)
        cq, ck = sb("cq", [P, 1]), sb("ck", [P, 1])

        X = sb("X", [P, NT, D])
        Y = sb("Y", [P, NT, D])
        Y2b = sb("Y2b", [P, NT * D + 8])
        Y2 = Y2b[:, 0:NT * D].rearrange("p (t h) -> p t h", t=NT)
        YT = sb("YT", [P, NT * P])
        st = sb("st", [P, NT, 6])
        mv = sb("mv", [P, NT, 2])
        ve, ry, rt = sb("ve", [P, NT]), sb("ry", [P, NT]), sb("rt", [P, NT])
        nmx, ssum = sb("nmx", [P, NT]), sb("ssum", [P, NT])
        omt, tdn = sb("omt", [P, 3]), sb("tdn", [P, 1])
        hstat, lntiny = sb("hstat", [P, 48]), sb("lntiny", [P, 1])

        with nc.sbuf_tensor("arena", [P, NSEQ * (S + 2 * D)], F32) as arena:
            pass
        arena_r = sb("arena_r", [P, NSEQ * (S + 2 * D)], F32R)
        zT = arena[:, 0:NSEQ * S].rearrange("p (b s) -> p b s", s=S)
        z = arena[:, NSEQ * S:NSEQ * (S + 2 * D)].rearrange("p (b c h) -> p b c h", c=2, h=D)
        zlast = sb("zlast", [SPT, NT, D])
        work = sb("work", [P, 18 * HN + 8])

        W0C, W1C = 3 * FF0, 2 * 2 * FF1
        yTh, yTl = sb("yTh", [P, NT * P], F32R), sb("yTl", [P, NT * P], F32R)
        gp, gq, gr, gsel = (sb(n, [P, NT, NE1]) for n in ("gp", "gq", "gr", "gsel"))
        gs1 = sb("gs1", [P, NT])
        gpart = sb("gpart", [P, NT * 3 * NE1], BF16)
        g3b = sb("g3b", [3 * NE1, NT * P], BF16)
        wraw = sb("wraw", [P, W0C])
        wh = [sb(f"wh{k}", [P, W0C], F32R) for k in range(2)]
        wl = [sb(f"wl{k}", [P, W0C], F32R) for k in range(2)]
        xch = [sb(f"xch{k}", [P, HN], F32R) for k in range(2)]
        xcl = [sb(f"xcl{k}", [P, HN], F32R) for k in range(2)]
        ph = [sb(f"ph{k}", [P, HN], F32R) for k in range(2)]
        pl = [sb(f"pl{k}", [P, HN], F32R) for k in range(2)]

        def slot(k, n=1):
            return work[:, k * HN:(k + n) * HN]

        def vcol(name, k=0, n=1):
            return vec[:, VEC_AT[name][0] + k:VEC_AT[name][0] + k + n]

        def mcol(name, k=0, n=None):
            a, w = MAT_AT[name]
            return mat[:, a + k:a + k + (w if n is None else n)]

        def rcol(name):
            return row[:, ROW_AT[name][0]:ROW_AT[name][0] + D]

        def ccol(name):
            return con[:, CON_AT[name][0]:CON_AT[name][0] + CON_AT[name][1]]

        def half(buf, h):
            return buf[:, h * HT:(h + 1) * HT, :].rearrange("p t h -> p (t h)")

        def yt(h):
            return YT[:, h * HN:(h + 1) * HN]

        def blk(ap, i):
            return ap[:, i * P:(i + 1) * P]

        ident = ccol("ident")
        cprobs = lambda t: work[:, t * 260:t * 260 + S]
        clast = lambda t: work[:, 2100 + t * SPT:2100 + (t + 1) * SPT]
        cpT = lambda t: work[:, 2200 + t * 256:2200 + (t + 1) * 256]
        clastT = lambda t: work[0:SPT, 4300 + t * P:4300 + (t + 1) * P]
        rmix = lambda h, g: slot(3 * h + g)
        rexp = lambda h, k: slot(6 + 4 * h + k)
        mpo, mo, tdt = slot(14), slot(15), slot(16)
        run = [work[:, 17 * HN:18 * HN + 1], Y2b[:, 0:HN + 1], Y2b[:, HN + 2:2 * HN + 3]]
        rw = lambda h: rexp(h, 0)
        xc = slot(0)
        act_out, prod = [slot(1), slot(2)], [slot(3), slot(4), slot(9), slot(10)]
        moe_copy = lambda h: slot(5 + h)
        g3f = work[0:3 * NE1, 7 * HN:9 * HN]
        sprob, spT, smask = (lambda h: slot(11 + h)), (lambda h: slot(13 + h)), (lambda h: slot(15 + h))
        hid = lambda h: slot(4 * h, 4)
        HEL = [(u // 4, u % 4) for u in range(8)]
        aslot = lambda k: arena[:, k * HN:(k + 1) * HN]
        rot = lambda n: aslot(n % 8)
        dot_q, dot_k = (lambda u: aslot(8 + u % 2)), (lambda u, k: aslot(10 + 2 * k + u % 2))
        rslot = lambda k: arena_r[:, k * HN:(k + 1) * HN]
        qe_h, qe_l = (lambda h, w: rslot(22 + 4 * h + 2 * w)), (lambda h, w: rslot(23 + 4 * h + 2 * w))
        sq = lambda m: slot(4 + 2 * (m % 2), 2)
        n2 = lambda m: slot(8 + m % 2)
        sx, ex, ets = (lambda u: slot(10 + u % 2)), (lambda u: slot(12 + u % 2)), (lambda u: slot(14 + u % 2))
        oT = lambda h: slot(16)
        hsum, hm = (lambda u: hstat[:, 16 * (u % 2):16 * (u % 2) + 16]), hstat[:, 32:48]
        vb_at = [Y2b[:, 0:HN], Y2b[:, HN:2 * HN], arena[:, 30 * HN:31 * HN], arena[:, 31 * HN:32 * HN],
                 wraw[:, 0:HN], wraw[:, HN:2 * HN], wraw[:, 2 * HN:3 * HN], slot(17)]
        vb = lambda t: vb_at[t]
        bias_at, ones = [ph[0], ph[1], pl[0]], pl[1]

        def hel_bias(k):
            r, c = (0, k) if k < 12 else (32, k - 12)
            return bias_at[c // 4][r:r + 2, (c % 4) * P:(c % 4 + 1) * P], ones[r:r + 2, :]

        def own_banks(rows):
            return pair[2][rows, :, :].rearrange("p j (i k t) -> p j i k t", i=2, k=2)[:, :, :, :, rows]

        def own_scores(u, p, rows):
            return sx(u)[rows, :].rearrange("p (i j k t) -> p j i k t", i=4, j=2, k=2)[:, :, 2 * p:2 * p + 2]

        def whel(parts, k):
            return parts[k // 12][:, (k % 12) * P:(k % 12 + 1) * P]

        def parts_of(w):
            return gpart[:, 0:NT * 3 * w].rearrange("p (t n) -> p t n", t=NT)

        x_loaded, con_loaded, par_loaded, zl_loaded = sem("x_loaded"), sem("con_loaded"), sem("par_loaded"), sem("zl_loaded")
        z_loaded = [sem(f"z_loaded{t}") for t in range(NT)]
        dve_step, act_step, pool_step = sem("dve_step"), sem("act_step"), sem("pool_step")
        const_ready = sem("const_ready")
        tok_ready = sem("tok_ready")
        tr_done = sem("tr_done")
        feat_ready = sem("feat_ready")
        c_scores, c_max, c_probs, c_last, c_ptr, c_pT, c_out, c_x = (
            sem("c_" + n) for n in ("scores", "max", "probs", "last", "ptr", "pT", "out", "x"))
        r_mix, r_kvr, r_kv, r_er, r_arg, r_exp, r_rw, r_out = (
            sem("r_" + n) for n in ("mix", "kvr", "kv", "er", "arg", "exp", "rw", "out"))
        m_logits, m_shift, m_exp, m_parts, m_gT, m_g3, m_split = (
            sem("m_" + n) for n in ("logits", "shift", "exp", "parts", "gT", "g3", "split"))
        a_scores, a_masked, a_prob, a_out, a_y2 = (sem("a_" + n) for n in ("scores", "masked", "prob", "out", "y2"))
        f_h, f_relu, f_out = (sem("f_" + n) for n in ("h", "relu", "out"))
        h_w, bias_loaded, h_bias, h_split = sem("h_w"), sem("bias_loaded"), sem("h_bias"), sem("h_split")
        h_e, h_eh, h_ec, h_hel, h_sq, h_n2, h_inv, h_norm, h_d, h_dq, h_dk, h_v, h_vb = (
            sem("h_" + n) for n in ("e", "eh", "ec", "hel", "sq", "n2", "inv", "norm", "d", "dq", "dk", "v", "vb"))
        h_s, h_sxa, h_sxd, h_sub, h_exp, h_sum, h_et, h_ets, h_pv, h_o, h_out, h_x = (
            sem("h_" + n) for n in ("s", "sxa", "sxd", "sub", "exp", "sum", "et", "ets", "pv", "o", "out", "x"))
        moe = [{n: sem(f"moe{k}_{n}") for n in (
            "wload", "whi", "wsplit", "gbc", "xcm", "xch", "xcp", "gate", "mm", "act", "mul", "hi", "prod", "down",
            "accdone", "copied", "back", "x")} for k in range(2)]
        stored = sem("stored")
        NF0, NF1 = FF0 // P, FF1 // P
        STEPS0 = [(k, h, f) for k in range(2) for h in range(2) for f in range(NF0)]
        STEPS1 = [(k, h, f) for k in range(4) for h in range(2) for f in range(NF1)]
        FREE0 = {"mul": 2, "prod": 4, "down": 2, "xcm": 2, "mm": 2 * NF0}
        FREE1 = {"mul": 2 * NF1, "prod": 4, "down": 4, "act": 4}
        WC = FF0
        WCH0, WCH1 = W0C // WC, W1C // WC
        ph4 = [b[:, 0:HN] for b in ph] + [b[:, W1C:W1C + HN] for b in wh]
        pl4 = [b[:, 0:HN] for b in pl] + [b[:, W1C:W1C + HN] for b in wl]

        def bodies(eng, n, body):
            with eng.Fori(0, n - 1) as i:
                body(i, False)
            body(n - 1, True)

        def own_wait(eng):
            eng.nop(nofuse=True)

        block = ctx.enter_context(nc.Block())

        @block.sync
        def _(sp):
            xv = d["x"].rearrange("(t p) h -> p t h", p=P)
            sp.dma_start(X[:, :, :], xv).then_inc(x_loaded, 16)
            sp.dma_start(con[:, :], d["con"]).then_inc(con_loaded, 16)
            sp.dma_start(zlast[:, :, :], d["zlast"]).then_inc(zl_loaded, 16)
            for t in range(NT):
                sp.dma_start(zT[:, SPT * t:SPT * t + SPT, :], d["zT"][t]).then_inc(z_loaded[t], 16)
                sp.dma_start(z[:, SPT * t:SPT * t + SPT, :, :], d["z"][t]).then_inc(z_loaded[t], 16)
            sp.dma_start(vec[:, :], d["vec"]).then_inc(par_loaded, 16)
            sp.dma_start(mat[:, :], d["mat"]).then_inc(par_loaded, 16)
            sp.dma_start(row[:, :], d["row"].to_broadcast([P, ROW_W])).then_inc(par_loaded, 16)
            sp.dma_start(mb2[:, :], d["mb2"]).then_inc(par_loaded, 16)
            for k, (w, cols, n) in enumerate(((d["w0"], W0C, NE0), (d["w1"], W1C, NE1 // 2))):
                m = moe[k]
                if k == 1:
                    sp.wait_ge(moe[0]["wsplit"], NE0 * WCH0)
                    sp.dma_start(wraw[0:34, :], d["hbias"]).then_inc(bias_loaded, 16)
                    sp.wait_ge(h_pv, len(HEL))
                sp.dma_start(wraw[:, 0:cols], w[0]).then_inc(m["wload"], 16)
                with sp.Fori(1, n) as e:
                    sp.wait_ge(m["wsplit"], (WCH0, WCH1)[k] * e)
                    sp.dma_start(wraw[:, 0:cols], w[bass.ds(e, 1), :, :].rearrange("e p n -> p (e n)"))\
                        .then_inc(m["wload"], 16)
            ov = d["out"].rearrange("(t p) h -> p t h", p=P)
            for h in range(2):
                sp.wait_ge(moe[1]["x"], h + 1)
                sp.dma_start(ov[:, h * HT:(h + 1) * HT, :], X[:, h * HT:(h + 1) * HT, :]).then_inc(stored, 16)
            sp.wait_ge(stored, 32)

        @block.tensor
        def _(pe):
            turns = [0]

            def turn4(src):
                n = turns[0]
                turns[0] += 1
                pe.wait_ge(tok_ready, n + 1)
                if n >= 2:
                    pe.wait_ge(feat_ready, n - 1)
                for i in range(HT):
                    last = pe.transpose(blk(bank[n % 2], i), src(i), ident)
                last.then_inc(tr_done, 1)
                return n + 1

            def mm3(out, ah, al, bh, bl, start, stop):
                pe.matmul(out, ah, bh, start=start, stop=False)
                pe.matmul(out, ah, bl, start=False, stop=False)
                return pe.matmul(out, al, bh, start=False, stop=stop)

            def cross(h, call):
                def scores(i):
                    t, u = h * HT + i, (2 * call + h) * HT + i
                    pe.wait_ge(z_loaded[t], 32)
                    if u >= 2:
                        pe.wait_ge(c_last, u - 1)
                    for j in range(SPT):
                        b = SPT * t + j
                        last = pe.matmul(bank[2 + u % 2][T * j:T * j + T, 0:S], YT[:, b * T:(b + 1) * T], zT[:, b, :],
                                         start=True, stop=True)
                    last.then_inc(c_scores, 1)

                def weigh(i):
                    t, u = h * HT + i, (2 * call + h) * HT + i
                    pe.wait_ge(c_last, u + 1)
                    if u >= 2:
                        pe.wait_ge(c_pT, u - 1)
                    b = bank[4 + u % 2]
                    for c in range(2):
                        pe.transpose(blk(b, c), blk(cprobs(t), c), ident)
                    pe.transpose(b[0:SPT, 2 * P:3 * P], clast(t), ident).then_inc(c_ptr, 1)
                    pe.wait_ge(c_pT, u + 1)
                    if u >= 2:
                        pe.wait_ge(c_x, u - 1)
                    o = bank[6 + u % 2]
                    pe.matmul(o[:, 0:D], clastT(t), zlast[:, t, :], start=True, stop=False, skip_group_check=True)
                    for j in range(SPT):
                        for c in range(2):
                            last = pe.matmul(o[T * j:T * j + T, 0:D], cpT(t)[:, c * P + T * j:c * P + T * j + T],
                                             z[:, SPT * t + j, c, :], start=False, stop=c == 1, skip_group_check=True)
                    last.then_inc(c_out, 1)

                scores(0)
                for i in range(HT):
                    if i + 1 < HT:
                        scores(i + 1)
                    weigh(i)

            def route(name, ne, rows, call):
                for t in range(NT):
                    last = pe.matmul(bank[2][:, t * NE1:t * NE1 + ne], blk(YT, t), mcol(name), start=True, stop=True)
                last.then_inc(m_logits, 1)
                for h in range(2):
                    pe.wait_ge(m_parts, call + 1)
                    for i in range(HT):
                        last = pe.transpose(blk(bank[3 + h].bitcast(BF16), i)[0:rows, :],
                                            parts_of(rows // 3)[:, h * HT + i, :], identb[:, :])
                    last.then_inc(m_gT, 1)

            def close(acc, rows, m):
                for h in range(2):
                    last = pe.matmul(acc[h], zerob[0:rows, :], g3b[0:rows, h * HN:(h + 1) * HN], start=False, stop=True)
                last.then_inc(m["accdone"], 1)

            def turn_back(m):
                for h in range(2):
                    pe.wait_ge(m["copied"], h + 1)
                    for i in range(HT):
                        last = pe.transpose(blk(bank[2 + h], i), blk(moe_copy(h), i), ident)
                    last.then_inc(m["back"], 1)

            acc = [bank[6], bank[7]]

            def moe0():
                m = moe[0]
                ROWS = 3 * NE0

                def spread(expert, un, g):
                    h = un % 2
                    pe.wait_ge(m["xcm"], g + FREE0["xcm"] - 1)
                    own_wait(pe)
                    pe.matmul(bank[h], selb[0:ROWS, bass.ds(expert, 1)].to_broadcast([ROWS, P]),
                              g3b[0:ROWS, h * HN:(h + 1) * HN], start=True, stop=True).then_inc(m["gbc"], 1)

                def up(i, q, last=False):
                    k, h, f = STEPS0[q % len(STEPS0)]
                    expert = 2 * i + q // (2 * NF0)
                    if h == 0 and f == 0:
                        pe.wait_ge(m["wsplit"], WCH0 * (expert + 1))
                    if f == 1 and not (last and q > len(STEPS0) - NF0):
                        spread(2 * i + (q // NF0 + 1) // 2, q // NF0 + 1, 4 * i + q // NF0 + 1)
                    pe.wait_ge(m["mul"], len(STEPS0) * i + q + FREE0["mul"] - 1)
                    a, b = slice(f * P, (f + 1) * P), slice(FF0 + f * P, FF0 + (f + 1) * P)
                    cols = slice(h * HN, (h + 1) * HN)
                    mm3(bank[2 + q % 2], wh[k][:, a], wl[k][:, a], yTh[:, cols], yTl[:, cols], True, True)\
                        .then_inc(m["gate"], 1)
                    if f == 0:
                        pe.wait_ge(m["xcp"], 4 * i + q // NF0 + 1)
                    mm3(bank[4 + q % 2], wh[k][:, b], wl[k][:, b], xch[h][:, :], xcl[h][:, :], True, True)\
                        .then_inc(m["mm"], 1)

                def down(i, q):
                    k, h, f = STEPS0[q]
                    pe.wait_ge(m["prod"], len(STEPS0) * i + q + 1 + FREE0["prod"])
                    c = slice(2 * FF0 + f * P, 2 * FF0 + (f + 1) * P)
                    mm3(acc[h], wh[k][:, c], wl[k][:, c], ph[q % 2][:, :], pl[q % 2][:, :], False, False)\
                        .then_inc(m["down"], 1)

                pe.wait_ge(m_g3, 2)
                pe.wait_ge(m_split, 2)
                for h in range(2):
                    pe.matmul(acc[h], zerob[0:ROWS, :], g3b[0:ROWS, h * HN:(h + 1) * HN], start=True, stop=False)
                spread(0, 0, 0)
                pe.sem_inc(m["mm"], FREE0["mm"])
                pe.sem_inc(m["down"], FREE0["down"])
                up(0, 0)
                up(0, 1)

                def body(i, last):
                    for q in range(len(STEPS0)):
                        if not last or q + 2 < len(STEPS0):
                            up(i, q + 2, last)
                        down(i, q)

                bodies(pe, NE0 // 2, body)
                close(acc, ROWS, m)
                turn_back(m)

            def moe1():
                m = moe[1]
                pe.wait_ge(m_g3, 4)
                pe.wait_ge(m_split, 4)
                for h in range(2):
                    pe.matmul(acc[h], mb2[:, :], g3f[:, h * HN:(h + 1) * HN], start=True, stop=False)
                pe.sem_inc(m["down"], FREE1["down"])

                def up(i, q):
                    k, h, f = STEPS1[q % len(STEPS1)]
                    base, expert = len(STEPS1) * i, 4 * i + q // (2 * NF1)
                    cols = slice(h * HN, (h + 1) * HN)
                    if f == 0:
                        if h == 0 and k % 2 == 0:
                            pe.wait_ge(m["wsplit"], WCH1 * (2 * i + q // (4 * NF1) + 1))
                        pe.wait_ge(m["mul"], base + q - 2 * NF1 + NF1 + FREE1["mul"])
                        own_wait(pe)
                        pe.matmul(bank[h], selb[:, bass.ds(expert + (NE0 + 1), 1)].to_broadcast([3 * NE1, P]),
                                  g3b[:, cols], start=True, stop=True).then_inc(m["gbc"], 1)
                    pe.wait_ge(m["act"], base + q - 3 + FREE1["act"])
                    a = slice((k % 2) * 2 * FF1 + f * P, (k % 2) * 2 * FF1 + (f + 1) * P)
                    mm3(bank[2 + q % 4], wh[k // 2][:, a], wl[k // 2][:, a], yTh[:, cols], yTl[:, cols], True, True)\
                        .then_inc(m["mm"], 1)

                def down(i, q):
                    k, h, f = STEPS1[q]
                    pe.wait_ge(m["prod"], len(STEPS1) * i + q + 1 + FREE1["prod"])
                    c = slice((k % 2) * 2 * FF1 + FF1 + f * P, (k % 2) * 2 * FF1 + FF1 + (f + 1) * P)
                    mm3(acc[h], wh[k // 2][:, c], wl[k // 2][:, c], ph4[q % 4], pl4[q % 4], False, False)\
                        .then_inc(m["down"], 1)

                for q in range(3):
                    up(0, q)

                def body(i, last):
                    for q in range(len(STEPS1)):
                        if not last or q + 3 < len(STEPS1):
                            up(i, q + 3)
                        down(i, q)

                bodies(pe, NE1 // 4, body)
                close(acc, 3 * NE1, m)
                turn_back(m)

            pe.wait_ge(con_loaded, 16)
            for h in range(2):
                n = turn4(lambda i: Y[:, h * HT + i, :])
                pe.wait_ge(feat_ready, n)
                if h == 0:
                    pe.wait_ge(zl_loaded, 16)
                cross(h, 0)
            pe.wait_ge(const_ready, 1)
            for h in range(2):
                turn4(lambda i: Y[:, h * HT + i, :])
                if h == 0:
                    pe.wait_ge(c_x, 2 * HT)
                for g, name in enumerate(("Wk", "Wv", "Wr")):
                    pe.wait_ge(r_mix, 3 * h + g + 1)
                    last = pe.matmul(bank[2 + 3 * h + g], mcol(name), rmix(h, g), start=True, stop=True)
                last.then_inc(r_kvr, 1)
            for h in range(2):
                pe.wait_ge(r_rw, h + 1)
                for i in range(HT):
                    last = pe.matmul(blk(bank[2 + h], i), blk(rw(h), i), mcol("Wo"), start=True, stop=True)
                last.then_inc(r_out, 1)
            for h in range(2):
                n = turn4(lambda i: Y[:, h * HT + i, :])
            pe.wait_ge(feat_ready, n)
            route("router", NE0 - 1, 3 * NE0, 0)
            moe0()
            for h in range(2):
                n = turn4(lambda i: Y[:, h * HT + i, :])
                pe.wait_ge(feat_ready, n)
                for i in range(HT):
                    y = blk(yt(h), i)
                    last = pe.matmul(blk(bank[2 + h], i), y, y, start=True, stop=True)
                last.then_inc(a_scores, 1)
            for h in range(2):
                n = turn4(lambda i: blk(sprob(h), i))
                pe.wait_ge(feat_ready, n)
                for i in range(HT):
                    last = pe.matmul(blk(bank[6 + h], i), blk(spT(h), i), Y[:, h * HT + i, :], start=True, stop=True)
                last.then_inc(a_out, 1)
            for h in range(2):
                n = turn4(lambda i: Y2[:, h * HT + i, :])
                pe.wait_ge(feat_ready, n)
                if h == 0:
                    pe.wait_ge(a_y2, 2)
                cross(h, 1)
            for h in range(2):
                n = turn4(lambda i: Y2[:, h * HT + i, :])
                pe.wait_ge(feat_ready, n)
                if h == 0:
                    pe.wait_ge(c_x, 4 * HT)
                for f in range(FFD // P):
                    u = h * (FFD // P) + f
                    if u >= 2:
                        pe.wait_ge(f_relu, u - 1)
                    pe.matmul(bank[2 + u % 2], blk(mcol("dw1"), f), yt(h), start=True, stop=True).then_inc(f_h, 1)
                pe.wait_ge(f_relu, (h + 1) * (FFD // P))
                for i in range(HT):
                    for f in range(FFD // P):
                        last = pe.matmul(blk(bank[4 + h], i), blk(hid(h), f * HT + i), blk(mcol("dw2"), f),
                                         start=f == 0, stop=f == FFD // P - 1)
                last.then_inc(f_out, 1)

            def project(h):
                parity = yt(h).rearrange("p (m c) -> p c m", c=2)
                if h == 1:
                    pe.wait_ge(h_ec, 2)
                for w, name in enumerate(("WqE", "WkE")):
                    for g in range(2):
                        for c in range(2):
                            last = pe.matmul(bank[6 + w][64 * c:64 * c + 64, g * 256:(g + 1) * 256],
                                             mcol(name, g * 64, 64), parity[:, c, :], start=True, stop=True)
                    last.then_inc(h_e, 1)

            def dots(u, w):
                h, g = HEL[u]
                cols = slice(h * HN, (h + 1) * HN)
                if u >= 1:
                    pe.wait_ge((h_dq, h_dk)[w], u)
                if w == 0:
                    if u >= 3:
                        pe.wait_ge(h_ets, u - 2)
                    if u >= 2:
                        pe.wait_ge(h_vb, min(HT + u - 1, NT))
                    if u == 7:
                        pe.wait_ge(feat_ready, 17)
                else:
                    if u >= 3:
                        pe.wait_ge(h_o, u - 2)
                    if u == 7:
                        pe.wait_ge(h_x, 1)
                bias, one = hel_bias(16 + 4 * w + g)
                pe.matmul(bank[w], bias, one, start=True, stop=False)
                mm3(bank[w], blk(xch[w], g), blk(xcl[w], g), yTh[:, cols], yTl[:, cols], False, True).then_inc(h_d, 1)

            def rotate(u, w, j):
                h, g = HEL[u]
                n, pr = 4 * u + 2 * w + j, 2 * g + j
                if n >= 4:
                    pe.wait_ge(h_norm, n - 3)
                cols = slice((pr // 4) * 256, (pr // 4 + 1) * 256)
                for c in range(2):
                    bias, one = hel_bias(2 * pr + c)
                    o = bank[2 + n % 4][:, c * 256:(c + 1) * 256]
                    pe.matmul(o, bias, one[:, 0:256], start=True, stop=False)
                    last = mm3(o, whel(wh, 2 * pr + c), whel(wl, 2 * pr + c), qe_h(h, w)[:, cols], qe_l(h, w)[:, cols],
                               False, True)
                last.then_inc(h_hel, 1)

            def score(u, p):
                if p == 0:
                    pe.wait_ge(h_norm, 4 * u + 4)
                    pe.wait_ge(h_dq, u + 1)
                    pe.wait_ge(h_dk, u + 1)
                if 2 * u + p >= 1:
                    pe.wait_ge(h_sxa, 2 * u + p)
                    pe.wait_ge(h_sxd, 2 * u + p)
                for i in range(2):
                    cols = slice((2 * p + i) * P, (2 * p + i + 1) * P)
                    for k in range(2):
                        for n, (a, b) in enumerate(((rot(4 * u + k), rot(4 * u + 2 + k)), (dot_q(u), dot_k(u, k)))):
                            for j in range(2):
                                rows = slice(64 * j, 64 * j + 64)
                                last = pe.matmul(pair[2][:, j, (2 * i + k) * P:(2 * i + k + 1) * P], a[rows, cols],
                                                 b[rows, cols], start=n == 0, stop=n == 1, skip_group_check=True)
                last.then_inc(h_s, 1)

            def turn_weights(u):
                pe.wait_ge(h_exp, u + 1)
                pe.wait_ge(h_dq, min(u + 3, 8))
                if u >= 1:
                    pe.wait_ge(h_ets, u)
                if u == 5:
                    pe.wait_ge(feat_ready, 17)
                for i in range(HT):
                    last = pe.transpose(blk(bank[0], i), blk(ex(u), i), ident)
                last.then_inc(h_et, 1)

            def weigh_values(u):
                h, g = HEL[u]
                pe.wait_ge(h_ets, u + 1)
                pe.wait_ge(h_vb, HT * (h + 1))
                pe.wait_ge(h_dk, min(u + 3, 8))
                if u >= 1:
                    pe.wait_ge(h_o, u)
                if u == 5:
                    pe.wait_ge(h_x, 1)
                for i in range(HT):
                    last = pe.matmul(blk(bank[1], i), blk(ets(u), i), blk(vb(h * HT + i), g), start=True, stop=True)
                last.then_inc(h_pv, 1)

            def values(t, b):
                by_slot = mcol("WvT").rearrange("p (g s x) -> p s g x", g=4, s=4)
                for s in range(4):
                    for j in range(SPT):
                        c = (t * SPT + j) * T
                        last = pe.matmul(b[32 * s:32 * s + 32, 32 * j:32 * j + 32], YT[:, c:c + T], by_slot[:, s],
                                         start=True, stop=True)
                last.then_inc(h_v, 1)

            def project_out(h):
                pe.wait_ge(h_ets, 4 * h + 4 + (h == 0))
                pe.wait_ge(h_o, 4 * h + 4 + (h == 0))
                n = turn4(lambda i: Y[:, h * HT + i, :])
                pe.wait_ge(feat_ready, n)
                for i in range(HT):
                    last = pe.matmul(blk(bank[n % 2], i), blk(oT(h), i), mcol("WoT"), start=True, stop=True)
                last.then_inc(h_out, 1)

            for h in range(2):
                n = turn4(lambda i: Y[:, h * HT + i, :])
                pe.wait_ge(feat_ready, n)
                project(h)
            pe.wait_ge(h_w, 1)
            pe.wait_ge(h_bias, 1)
            pe.wait_ge(h_split, 2)
            pe.wait_ge(h_ec, 4)
            for u in range(len(HEL) + 2):
                if u < len(HEL):
                    for w in range(2):
                        dots(u, w)
                    for w in range(2):
                        for j in range(2):
                            rotate(u, w, j)
                if u == 0:
                    for t in range(HT):
                        if t >= 2:
                            pe.wait_ge(h_vb, t - 1)
                        values(t, bank[6 + t % 2])
                    pe.wait_ge(h_vb, HT)
                if u >= 2:
                    turn_weights(u - 2)
                if 1 <= u <= len(HEL):
                    score(u - 1, 0)
                if 1 <= u <= HT:
                    pe.wait_ge(h_dq, u + 1)
                    if u >= 2:
                        pe.wait_ge(h_ets, u - 1)
                    values(HT + u - 1, bank[0])
                if u >= 2:
                    weigh_values(u - 2)
                if 1 <= u <= len(HEL):
                    score(u - 1, 1)
                if u == 6:
                    project_out(0)
            project_out(1)
            for h in range(2):
                n = turn4(lambda i: Y[:, h * HT + i, :])
            pe.wait_ge(feat_ready, n)
            route("gate", NE1, 3 * NE1, 1)
            moe1()

        @block.scalar
        def _(act):
            count = {"turn": 0, "step": 0}

            def step(ins):
                count["step"] += 1
                ins.then_inc(act_step, 1)
                act.wait_ge(act_step, count["step"])

            def copy_turned(dst):
                n = count["turn"]
                count["turn"] += 1
                act.wait_ge(tr_done, n + 1)
                act.activation(dst, bank[n % 2], ACT.Copy).then_inc(feat_ready, 1)

            scale = float(D) ** -0.5
            for h in range(2):
                copy_turned(yt(h))
                for i in range(HT):
                    u = h * HT + i
                    act.wait_ge(c_scores, u + 1)
                    act.activation(cprobs(u), bank[2 + u % 2][:, 0:S], ACT.Gelu_apprx_tanh).then_inc(c_probs, 1)
            act.wait_ge(const_ready, 1)
            step(act.activation(tdn[:, :], vcol("td"), ACT.Exp))
            for h in range(2):
                copy_turned(yt(h))
            for h in range(2):
                act.wait_ge(r_kvr, h + 1)
                for g in range(2):
                    last = act.activation(rmix(h, g), bank[2 + 3 * h + g], ACT.Copy)
                last.then_inc(r_kv, 1)
                act.activation(rmix(h, 2), bank[4 + 3 * h], ACT.Exp, scale=-1.0).then_inc(r_er, 1)
            for h in range(2):
                for k in range(4):
                    act.wait_ge(r_arg, 4 * h + k + 1)
                    act.activation(rexp(h, k), rexp(h, k), ACT.Exp).then_inc(r_exp, 1)
            for h in range(2):
                copy_turned(yt(h))
            act.wait_ge(m_shift, 1)
            act.activation(gq[:, :, 0:NE0 - 1], gq[:, :, 0:NE0 - 1], ACT.Exp).then_inc(m_exp, 1)
            def weights_hi(m, load, k, c, free):
                act.wait_ge(m["wload"], 16 * load + 16)
                if free is not None:
                    act.wait_ge(m["down"], free)
                cols = slice(c * WC, (c + 1) * WC)
                act.activation(wh[k][:, cols], wraw[:, cols], ACT.Copy).then_inc(m["whi"], 1)

            def body0(i, last):
                m, base = moe[0], len(STEPS0) * i
                for q in range(len(STEPS0)):
                    k, h, f = STEPS0[q]
                    act.wait_ge(m["gate"], base + q + 1)
                    act.wait_ge(m["mul"], base + q + FREE0["mul"] - 1)
                    act.activation(act_out[q % 2], bank[2 + q % 2], ACT.Silu).then_inc(m["act"], 1)
                    un = q // NF0
                    if f == 1 and not (last and un == 3):
                        act.wait_ge(m["xcm"], 4 * i + un + 2 + FREE0["xcm"])
                        act.wait_ge(m["mm"], NF0 * (4 * i + un) + FREE0["mm"])
                        act.activation(xch[(un + 1) % 2][:, :], xc, ACT.Copy).then_inc(m["xch"], 1)
                    c = q % (2 * NF0) - 2
                    if 0 <= c < WCH0 and not (last and k == 1):
                        weights_hi(m, 2 * i + k + 1, (k + 1) % 2, c, 2 * NF0 * (2 * i + k) + FREE0["down"])
                    act.wait_ge(m["mul"], base + q + 1 + FREE0["mul"])
                    act.wait_ge(m["down"], base + q + FREE0["down"] - 1)
                    act.activation(ph[q % 2][:, :], prod[q % 4], ACT.Copy).then_inc(m["hi"], 1)

            m = moe[0]
            act.preload_act_table(ACT.Silu)
            for c in range(WCH0):
                weights_hi(m, 0, 0, c, None)
            act.wait_ge(m["xcm"], 1 + FREE0["xcm"])
            act.activation(xch[0][:, :], xc, ACT.Copy).then_inc(m["xch"], 1)
            bodies(act, NE0 // 2, body0)
            act.wait_ge(m["accdone"], 1)
            for h in range(2):
                act.activation(moe_copy(h), bank[6 + h], ACT.Copy).then_inc(m["copied"], 1)
            for h in range(2):
                copy_turned(yt(h))
            for h in range(2):
                act.wait_ge(a_masked, h + 1)
                for i in range(HT):
                    t = h * HT + i
                    last = act.activation(blk(sprob(h), i), blk(smask(h), i), ACT.Exp, bias=nmx[:, t:t + 1],
                                          scale=scale, accum_out=ssum[:, t:t + 1])
                last.then_inc(a_prob, 1)
            for h in range(2):
                copy_turned(spT(h))
            for h in range(2):
                copy_turned(yt(h))
                for i in range(HT):
                    t, u = h * HT + i, (2 + h) * HT + i
                    act.wait_ge(c_max, t + 1)
                    act.activation(cprobs(t), bank[2 + u % 2][:, 0:S], ACT.Exp, bias=nmx[:, t:t + 1], scale=scale,
                                   accum_out=ssum[:, t:t + 1]).then_inc(c_probs, 1)
            for h in range(2):
                copy_turned(yt(h))
                for f in range(FFD // P):
                    u = h * (FFD // P) + f
                    act.wait_ge(f_h, u + 1)
                    act.activation(hid(h)[:, f * HN:(f + 1) * HN], bank[2 + u % 2], ACT.Relu,
                                   bias=vcol("db1", f)).then_inc(f_relu, 1)
            act.preload_act_table_set("natural_log_exp_and_others")
            def squares(m):
                if m >= 2:
                    act.wait_ge(h_n2, m - 1)
                for j in range(2):
                    n = 2 * m + j
                    act.wait_ge(h_hel, n + 1)
                    act.activation(sq(m)[:, j * HN:(j + 1) * HN], bank[2 + n % 4], ACT.Square).then_inc(h_sq, 1)

            def inverse(m):
                act.wait_ge(h_n2, m + 1)
                step(act.activation(n2(m), n2(m), ACT.Ln, scale=float(2 ** 20), bias=lntiny[:, :]))
                act.activation(n2(m), n2(m), ACT.Exp, scale=-0.5, bias=(cq, ck)[m % 2][:, :]).then_inc(h_inv, 1)

            def extract(u, p):
                act.wait_ge(h_s, 2 * u + p + 1)
                if u >= 2:
                    act.wait_ge(h_exp, u - 1)
                for j in (2, 3):
                    rows = slice(T * j, T * j + T)
                    last = act.activation(own_scores(u, p, rows), own_banks(rows), ACT.Copy)
                last.then_inc(h_sxa, 1)

            for h in range(2):
                copy_turned(yt(h))
                for w, name in enumerate(("bqE", "bkE")):
                    act.wait_ge(h_e, 2 * h + w + 1)
                    for g in range(2):
                        c = slice(g * 256, (g + 1) * 256)
                        last = act.activation(qe_h(h, w)[:, c], bank[6 + w][:, c], ACT.Identity, bias=vcol(name, g))
                    last.then_inc(h_eh, 1)
            for u in range(len(HEL) + 2):
                if u < len(HEL):
                    act.wait_ge(h_d, 2 * u + 1)
                    if u >= 2:
                        act.wait_ge(h_s, 2 * u - 2)
                    act.activation(dot_q(u), bank[0], ACT.Copy).then_inc(h_dq, 1)
                if u >= 2:
                    act.wait_ge(h_sub, u - 1)
                    if u >= 4:
                        act.wait_ge(h_et, u - 3)
                        act.wait_ge(h_sum, u - 3)
                    act.activation(ex(u - 2), sx(u - 2), ACT.Exp, scale=0.5 * float(HD) ** -0.5).then_inc(h_exp, 1)
                if u < len(HEL):
                    squares(2 * u)
                    squares(2 * u + 1)
                    inverse(2 * u)
                if u >= 2:
                    act.wait_ge(h_et, u - 1)
                    if u >= 4:
                        act.wait_ge(h_pv, u - 3)
                    act.activation(ets(u - 2), bank[0], ACT.Copy).then_inc(h_ets, 1)
                if u < len(HEL):
                    inverse(2 * u + 1)
                if 1 <= u <= len(HEL):
                    extract(u - 1, 0)
                    extract(u - 1, 1)
                if u == 6:
                    copy_turned(oT(0))
            copy_turned(oT(1))
            for h in range(2):
                copy_turned(yt(h))
            act.wait_ge(m_shift, 2)
            act.activation(gq[:, :, 0:NE1], gq[:, :, 0:NE1], ACT.Exp).then_inc(m_exp, 1)
            m = moe[1]
            act.sem_inc(m["act"], FREE1["act"])
            for c in range(WCH1):
                weights_hi(m, 0, 0, c, None)

            def relu(i, q):
                base = len(STEPS1) * i
                m = moe[1]
                act.wait_ge(m["mm"], base + q + 1)
                act.wait_ge(m["mul"], base + q - 1 + FREE1["mul"])
                own_wait(act)
                k, h, f = STEPS1[q % len(STEPS1)]
                at = 4 * NF1 * i + (VEC_AT["b1m"][0] + q // (2 * NF1) * NF1 + f)
                act.activation(act_out[q % 2], bank[2 + q % 4], ACT.Relu, bias=vec[:, bass.ds(at, 1)])\
                    .then_inc(m["act"], 1)

            def body1(i, last):
                m, base = moe[1], len(STEPS1) * i
                for q in range(len(STEPS1)):
                    k, h, f = STEPS1[q]
                    act.wait_ge(m["mul"], base + q + 1 + FREE1["mul"])
                    act.wait_ge(m["down"], base + q - 3 + FREE1["down"])
                    act.activation(ph4[q % 4], prod[q % 4], ACT.Copy).then_inc(m["hi"], 1)
                    if not last or q + 2 < len(STEPS1):
                        relu(i, q + 2)
                    c = q % (4 * NF1) - 2
                    if 0 <= c < WCH1 and not (last and k >= 2):
                        weights_hi(m, 2 * i + k // 2 + 1, (k // 2 + 1) % 2, c, 4 * NF1 * (2 * i + k // 2) + FREE1["down"])

            relu(0, 0)
            relu(0, 1)
            bodies(act, NE1 // 4, body1)
            act.wait_ge(m["accdone"], 1)
            for h in range(2):
                act.activation(moe_copy(h), bank[6 + h], ACT.Copy).then_inc(m["copied"], 1)

        @block.gpsimd
        def _(pool):
            pool.memset(zerob[:, :], 0.0)
            pool.memset(cq[:, :], LN2 * 10 + math.log(QF))
            pool.memset(lntiny[:, :], 1e-26)
            pool.memset(ck[:, :], LN2 * 10)
            pool.wait_ge(con_loaded, 16)
            pool.tensor_copy(identb[:, :], ident)
            pool.tensor_copy(selb[:, :], con[0:3 * NE1, CON_AT["sel0"][0]:CON_AT["sel1"][0] + CON_AT["sel1"][1]])\
                .then_inc(pool_step, 1)
            pool.wait_ge(pool_step, 1)
            pool.wait_ge(par_loaded, 4 * 16)
            pool.sem_inc(const_ready, 1)

            def weights_lo(m, nch, load, k):
                for c in range(nch):
                    cols = slice(c * WC, (c + 1) * WC)
                    pool.wait_ge(m["whi"], nch * load + c + 1)
                    pool.tensor_tensor(wl[k][:, cols], wraw[:, cols], wh[k][:, cols].bitcast(F32), ALU.subtract)\
                        .then_inc(m["wsplit"], 1)

            def pool_body0(i, last):
                weights_lo(moe[0], WCH0, 2 * i + 1, 1)
                if not last:
                    weights_lo(moe[0], WCH0, 2 * i + 2, 0)

            weights_lo(moe[0], WCH0, 0, 0)
            bodies(pool, NE0 // 2, pool_body0)
            pool.wait_ge(moe[0]["accdone"], 1)
            pool.memset(ones[0:34, :].bitcast(F32), 1.0)
            parts = [(wh[0][:, :], wl[0][:, :], mcol("Whel", 0, W0C)),
                     (wh[1][:, 0:HN], wl[1][:, 0:HN], mcol("Whel", W0C, HN)),
                     (xch[0][:, :], xcl[0][:, :], mcol("WqD")), (xch[1][:, :], xcl[1][:, :], mcol("WkD"))]
            for hi, lo, w in parts:
                pool.tensor_copy(hi, w).then_inc(pool_step, 1)
            pool.wait_ge(pool_step, 5)
            for hi, lo, w in parts:
                last = pool.tensor_tensor(lo, w, hi.bitcast(F32), ALU.subtract)
            last.then_inc(h_w, 1)

            def add_squares(m):
                pool.wait_ge(h_sq, 2 * m + 2)
                if m >= 2:
                    pool.wait_ge(h_norm, 2 * m - 2)
                s4 = sq(m).rearrange("p (j c m) -> p j c m", j=2, c=2)
                pool.tensor_tensor(n2(m).rearrange("p (j m) -> p j m", j=2), s4[:, :, 0], s4[:, :, 1], ALU.add)\
                    .then_inc(h_n2, 1)

            for m in range(2 * len(HEL)):
                add_squares(m)

            def pool_body1(i, last):
                weights_lo(moe[1], WCH1, 2 * i + 1, 1)
                if not last:
                    weights_lo(moe[1], WCH1, 2 * i + 2, 0)

            weights_lo(moe[1], WCH1, 0, 0)
            bodies(pool, NE1 // 4, pool_body1)

        @block.vector
        def _(dve):
            count = {"step": 0}

            def step(ins):
                count["step"] += 1
                ins.then_inc(dve_step, 1)
                dve.wait_ge(dve_step, count["step"])

            def layernorm(h, src, dst):
                ts, hs = range(h * HT, (h + 1) * HT), slice(h * HT, (h + 1) * HT)
                for t in ts:
                    last = dve.bn_stats(st[:, t, :], src[:, t, :])
                step(last)
                for t in ts:
                    last = dve.bn_aggr(mv[:, t, :], st[:, t, :])
                step(last)
                v, r, w = ve[:, hs], ry[:, hs], rt[:, hs]
                step(dve.tensor_scalar(v, mv[:, hs, 1], EPS, None, ALU.add))
                step(dve.tensor_scalar(r.bitcast(I32), v.bitcast(I32), 1, None, ALU.logical_shift_right))
                step(dve.tensor_scalar(r.bitcast(I32), r.bitcast(I32), -1.0, float(MAGIC), ALU.mult, ALU.add))
                for _ in range(3):
                    step(dve.tensor_tensor(w, r, r, ALU.mult))
                    step(dve.tensor_tensor(w, w, v, ALU.mult))
                    step(dve.tensor_scalar(w, w, -0.5, 1.5, ALU.mult, ALU.add))
                    step(dve.tensor_tensor(r, r, w, ALU.mult))
                for t in ts:
                    last = dve.tensor_scalar(dst[:, t, :], src[:, t, :], mv[:, t, 0:1], ry[:, t:t + 1],
                                             ALU.subtract, ALU.mult)
                return last

            def along(name):
                return rcol(name).rearrange("p (a h) -> p a h", a=1).to_broadcast([P, HT, D])

            def affine(h, buf, g, b):
                v = buf[:, h * HT:(h + 1) * HT, :]
                step(dve.tensor_tensor(v, v, along(g), ALU.mult))
                return dve.tensor_tensor(v, v, along(b), ALU.add)

            def cross(h, call):
                for i in range(HT):
                    t, u = h * HT + i, (2 * call + h) * HT + i
                    if call == 1:
                        dve.wait_ge(c_scores, u + 1)
                        step(dve.tensor_reduce(nmx[:, t:t + 1], bank[2 + u % 2][:, 0:S], AX.X, ALU.max))
                        dve.tensor_scalar(nmx[:, t:t + 1], nmx[:, t:t + 1], -float(D) ** -0.5, None, ALU.mult)\
                            .then_inc(c_max, 1)
                    dve.wait_ge(c_probs, u + 1)
                    dve.tensor_scalar(clast(t), ccol("seq4"), cprobs(t)[:, S - 1:S], None, ALU.mult).then_inc(c_last, 1)
                    if call == 1:
                        step(dve.reciprocal(ssum[:, t:t + 1], ssum[:, t:t + 1]))
                    dve.wait_ge(c_ptr, u + 1)
                    b = bank[4 + u % 2]
                    dve.tensor_copy(clastT(t), b[0:SPT, 2 * P:3 * P])
                    dve.tensor_copy(cpT(t), b[:, 0:2 * P]).then_inc(c_pT, 1)
                    dve.wait_ge(c_out, u + 1)
                    o = bank[6 + u % 2]
                    if call == 0:
                        dve.tensor_tensor(X[:, t, :], o[:, 0:D], X[:, t, :], ALU.add).then_inc(c_x, 1)
                    else:
                        dve.scalar_tensor_tensor(Y2[:, t, :], o[:, 0:D], ssum[:, t:t + 1], Y2[:, t, :],
                                                 ALU.mult, ALU.add).then_inc(c_x, 1)
                dve.wait_ge(c_x, (2 * call + h + 1) * HT)

            def over_experts(v, ne):
                return v[:, :].rearrange("p (t a) -> p t a", a=1).to_broadcast([P, NT, ne])

            def softmax_router(ne, r0, call):
                dve.wait_ge(m_logits, call + 1)
                lg = bank[2][:, 0:NT * NE1].rearrange("p (t e) -> p t e", e=NE1)[:, :, 0:ne]
                step(dve.tensor_reduce(gs1[:, :], lg, AX.X, ALU.max))
                dve.tensor_tensor(gq[:, :, 0:ne], lg, over_experts(gs1, ne), ALU.subtract).then_inc(m_shift, 1)
                dve.wait_ge(m_exp, call + 1)
                step(dve.tensor_reduce(gs1[:, :], gq[:, :, 0:ne], AX.X, ALU.add))
                step(dve.reciprocal(gs1[:, :], gs1[:, :]))
                step(dve.tensor_tensor(gp[:, :, r0:r0 + ne], gq[:, :, 0:ne], over_experts(gs1, ne), ALU.mult))

            def keep_top(k, ne, r0, rev):
                pv, qv, rv, sv = (b[:, :, r0:r0 + ne] for b in (gp, gq, gr, gsel))
                order = ccol(rev).rearrange("p (a e) -> p a e", a=1).to_broadcast([P, NT, ne])
                step(dve.tensor_copy(qv, pv))
                for j in range(k):
                    step(dve.tensor_reduce(gs1[:, :], qv, AX.X, ALU.max))
                    step(dve.tensor_tensor(rv, qv, over_experts(gs1, ne), ALU.is_equal))
                    step(dve.tensor_tensor(rv, rv, order, ALU.mult))
                    step(dve.tensor_reduce(gs1[:, :], rv, AX.X, ALU.max))
                    step(dve.tensor_tensor(rv, rv, over_experts(gs1, ne), ALU.is_equal))
                    if j == 0:
                        step(dve.tensor_copy(sv, rv))
                    else:
                        step(dve.tensor_tensor(sv, sv, rv, ALU.add))
                    step(dve.scalar_tensor_tensor(qv, rv, -2.0, qv, ALU.mult, ALU.add))
                step(dve.tensor_tensor(pv, pv, sv, ALU.mult))
                step(dve.tensor_reduce(gs1[:, :], pv, AX.X, ALU.add))

            def routing_parts(w, call):
                p3 = [parts_of(w)[:, :, a * w:(a + 1) * w] for a in range(3)]
                r, g = gr[:, :, 0:w], gp[:, :, 0:w]
                step(dve.tensor_copy(p3[0], g))
                step(dve.tensor_tensor(r, g, p3[0], ALU.subtract))
                step(dve.tensor_copy(p3[1], r))
                step(dve.tensor_tensor(r, r, p3[1], ALU.subtract))
                dve.tensor_copy(p3[2], r).then_inc(m_parts, 1)
                for h in range(2):
                    dve.wait_ge(m_gT, 2 * call + h + 1)
                    src = bank[3 + h].bitcast(BF16)[0:3 * w, 0:HN]
                    c = slice(h * HN, (h + 1) * HN)
                    if call == 1:
                        dve.tensor_copy(g3f[:, c], src)
                    dve.tensor_copy(g3b[0:3 * w, c], src).then_inc(m_g3, 1)

            def split_y(h, turns, done=m_split):
                dve.wait_ge(feat_ready, turns)
                c = slice(h * HN, (h + 1) * HN)
                step(dve.tensor_copy(yTh[:, c], YT[:, c]))
                dve.tensor_tensor(yTl[:, c], YT[:, c], yTh[:, c].bitcast(F32), ALU.subtract).then_inc(done, 1)

            def moe_end(m):
                for h in range(2):
                    dve.wait_ge(m["back"], h + 1)
                    dve.tensor_tensor(half(X, h), bank[2 + h], half(X, h), ALU.add).then_inc(m["x"], 1)

            dve.wait_ge(x_loaded, 16)
            for h in range(2):
                layernorm(h, X, Y).then_inc(tok_ready, 1)
            dve.wait_ge(con_loaded, 16)
            for h in range(2):
                cross(h, 0)
            dve.wait_ge(const_ready, 1)
            for h in range(2):
                layernorm(h, X, Y).then_inc(tok_ready, 1)
            for g, name in enumerate(("tmk", "tmv", "tmr")):
                dve.tensor_scalar(omt[:, g:g + 1], vcol(name), -1.0, 1.0, ALU.mult, ALU.add)
            for r in run:
                dve.memset(r[:, 0:1], 0.0)
            dve.wait_ge(act_step, 1)
            step(dve.tensor_scalar(tdn[:, :], tdn[:, :], -1.0, None, ALU.mult))
            newseq = ccol("newseq").rearrange("p (a t) -> p a t", a=1).to_broadcast([P, SPH, T])
            step(dve.tensor_scalar(tdt.rearrange("p (b t) -> p b t", t=T), newseq, tdn[:, :], None, ALU.add))
            for h in range(2):
                dve.wait_ge(feat_ready, 2 + h + 1)
                yv = yt(h).rearrange("p (b t) -> p b t", t=T)
                for g, name in enumerate(("tmk", "tmv", "tmr")):
                    mix = rmix(h, g).rearrange("p (b t) -> p b t", t=T)
                    step(dve.tensor_scalar(rmix(h, g), yt(h), vcol(name), None, ALU.mult))
                    dve.scalar_tensor_tensor(mix[:, :, 1:T], yv[:, :, 0:T - 1], omt[:, g:g + 1], mix[:, :, 1:T],
                                             ALU.mult, ALU.add).then_inc(r_mix, 1)
            for h in range(2):
                dve.wait_ge(r_kv, h + 1)
                K, V = rmix(h, 0), rmix(h, 1)
                E1S, E2S, E1, E2 = (rexp(h, k) for k in range(4))
                mx, num, den = (r[:, 1:HN + 1] for r in run)
                mxp, nump, denp = (r[:, 0:HN] for r in run)
                step(dve.tensor_tensor_scan(mx, tdt, K, NEG, ALU.add, ALU.max))
                step(dve.tensor_tensor(E1S, mxp, tdt, ALU.add))
                dve.tensor_tensor(E1S, E1S, mx, ALU.subtract).then_inc(r_arg, 1)
                dve.tensor_tensor(E2S, K, mx, ALU.subtract).then_inc(r_arg, 1)
                b3 = lambda a: a.rearrange("p (b t) -> p b t", t=T)
                step(dve.tensor_tensor(b3(mpo), b3(mxp), newseq, ALU.add))
                step(dve.scalar_tensor_tensor(mo, K, vcol("tf"), mpo, ALU.add, ALU.max))
                dve.tensor_tensor(E1, mpo, mo, ALU.subtract).then_inc(r_arg, 1)
                dve.scalar_tensor_tensor(E2, K, vcol("tf"), mo, ALU.add, ALU.subtract).then_inc(r_arg, 1)
                dve.wait_ge(r_exp, 4 * h + 4)
                step(dve.tensor_tensor(mpo, E2S, V, ALU.mult))
                dve.tensor_tensor_scan(num, E1S, mpo, 0.0, ALU.mult, ALU.add)
                step(dve.tensor_tensor_scan(den, E1S, E2S, 0.0, ALU.mult, ALU.add))
                dve.tensor_tensor(mpo, E1, nump, ALU.mult)
                step(dve.tensor_tensor(mo, E2, V, ALU.mult))
                dve.tensor_tensor(mpo, mpo, mo, ALU.add)
                step(dve.tensor_tensor(E1S, E1, denp, ALU.mult))
                step(dve.tensor_tensor(mo, E1S, E2, ALU.add))
                dve.wait_ge(r_er, h + 1)
                step(dve.scalar_tensor_tensor(mo, rmix(h, 2), 1.0, mo, ALU.add, ALU.mult))
                step(dve.reciprocal(mo, mo))
                dve.tensor_tensor(rw(h), mpo, mo, ALU.mult).then_inc(r_rw, 1)
            for h in range(2):
                dve.wait_ge(r_out, h + 1)
                step(dve.tensor_tensor(half(X, h), bank[2 + h], half(X, h), ALU.add))
                layernorm(h, X, Y).then_inc(tok_ready, 1)
            for h in range(2):
                split_y(h, 4 + h + 1)
            softmax_router(NE0 - 1, 1, 0)
            keep_top(TOP0, NE0 - 1, 1, "rev0")
            step(dve.tensor_scalar(gs1[:, :], gs1[:, :], 1e-9, None, ALU.add))
            step(dve.reciprocal(gs1[:, :], gs1[:, :]))
            step(dve.tensor_tensor(gp[:, :, 1:NE0], gp[:, :, 1:NE0], over_experts(gs1, NE0 - 1), ALU.mult))
            step(dve.memset(gp[:, :, 0:1], 1.0))
            routing_parts(NE0, 0)
            m = moe[0]
            dve.sem_inc(m["mul"], FREE0["mul"])
            dve.sem_inc(m["prod"], FREE0["prod"])
            dve.sem_inc(m["xcm"], FREE0["xcm"])

            def scale_input(un, g):
                dve.wait_ge(m["gbc"], g + 1)
                dve.tensor_tensor(xc, bank[un % 2], yt(un % 2), ALU.mult).then_inc(m["xcm"], 1)

            def input_lo(un, g):
                dve.wait_ge(m["xch"], g + 1)
                dve.tensor_tensor(xcl[un % 2][:, :], xc, xch[un % 2][:, :].bitcast(F32), ALU.subtract)\
                    .then_inc(m["xcp"], 1)

            scale_input(0, 0)
            input_lo(0, 0)

            def body0(i, last):
                base = len(STEPS0) * i
                for q in range(len(STEPS0)):
                    k, h, f = STEPS0[q]
                    dve.wait_ge(m["act"], base + q + 1)
                    dve.wait_ge(m["mm"], base + q + 1 + FREE0["mm"])
                    dve.wait_ge(m["prod"], base + q - 3 + FREE0["prod"])
                    dve.tensor_tensor(prod[q % 4], act_out[q % 2], bank[4 + q % 2], ALU.mult).then_inc(m["mul"], 1)
                    un = q // NF0
                    if f == 0 and not (last and un == 3):
                        dve.wait_ge(m["xcp"], 4 * i + un + 1)
                        scale_input(un + 1, 4 * i + un + 1)
                    if f == 1 and not (last and un == 3):
                        input_lo(un + 1, 4 * i + un + 1)
                    dve.wait_ge(m["hi"], base + q + 1)
                    dve.tensor_tensor(pl[q % 2][:, :], prod[q % 4], ph[q % 2][:, :].bitcast(F32), ALU.subtract)\
                        .then_inc(m["prod"], 1)

            bodies(dve, NE0 // 2, body0)
            moe_end(m)
            dve.wait_ge(m["x"], 2)
            for h in range(2):
                layernorm(h, X, Y).then_inc(tok_ready, 1)
            for h in range(2):
                hs = slice(h * HT, (h + 1) * HT)
                s3 = smask(h).rearrange("p (t k) -> p t k", t=HT)
                causal = ccol("causal").rearrange("p (a k) -> p a k", a=1).to_broadcast([P, HT, P])
                dve.wait_ge(a_scores, h + 1)
                step(dve.tensor_tensor(s3, bank[2 + h].rearrange("p (t k) -> p t k", t=HT), causal, ALU.add))
                step(dve.tensor_reduce(nmx[:, hs], s3, AX.X, ALU.max))
                dve.tensor_scalar(nmx[:, hs], nmx[:, hs], -float(D) ** -0.5, None, ALU.mult).then_inc(a_masked, 1)
            for h in range(2):
                hs = slice(h * HT, (h + 1) * HT)
                dve.wait_ge(a_prob, h + 1)
                dve.sem_inc(tok_ready, 1)
                step(dve.reciprocal(ssum[:, hs], ssum[:, hs]))
            for h in range(2):
                dve.wait_ge(a_out, h + 1)
                for i in range(HT):
                    t = h * HT + i
                    last = dve.scalar_tensor_tensor(Y2[:, t, :], blk(bank[6 + h], i), ssum[:, t:t + 1], Y[:, t, :],
                                                    ALU.mult, ALU.add)
                last.then_inc(a_y2, 1)
                dve.wait_ge(a_y2, h + 1)
                step(layernorm(h, Y2, Y2))
                affine(h, Y2, "g1", "be1").then_inc(tok_ready, 1)
            dve.wait_ge(tok_ready, 12)
            for h in range(2):
                cross(h, 1)
            for h in range(2):
                step(layernorm(h, Y2, Y2))
                affine(h, Y2, "g2", "be2").then_inc(tok_ready, 1)
            for h in range(2):
                dve.wait_ge(tok_ready, 13 + h)
                dve.wait_ge(tr_done, 13 + h)
                v = Y2[:, h * HT:(h + 1) * HT, :]
                step(dve.tensor_tensor(v, v, along("b2"), ALU.add))
                dve.wait_ge(f_out, h + 1)
                step(dve.tensor_tensor(half(Y2, h), bank[4 + h], half(Y2, h), ALU.add))
                step(layernorm(h, Y2, Y2))
                step(affine(h, Y2, "g3", "be3"))
                step(dve.tensor_tensor(half(X, h), half(Y2, h), half(X, h), ALU.add))
            turns = 18
            for h in range(2):
                layernorm(h, X, Y).then_inc(tok_ready, 1)
            dve.wait_ge(bias_loaded, 16)
            dve.wait_ge(moe[0]["accdone"], 1)
            for c, b in enumerate(bias_at):
                raw = wraw[0:34, c * HN:(c + 1) * HN]
                step(dve.tensor_copy(b[0:34, :], raw))
                last = dve.scalar_tensor_tensor(b[0:34, :], b[0:34, :].bitcast(F32), ccol("biaslo")[0:34, :], raw,
                                                ALU.mult, ALU.add)
            last.then_inc(h_bias, 1)
            for h in range(2):
                split_y(h, 15 + h, h_split)
                for w, name in enumerate(("bqE", "bkE")):
                    dve.wait_ge(h_eh, 2 * h + w + 1)
                    for g in range(2):
                        c = slice(g * 256, (g + 1) * 256)
                        last = dve.scalar_tensor_tensor(qe_l(h, w)[:, c], bank[6 + w][:, c], vcol(name, g),
                                                        qe_h(h, w)[:, c].bitcast(F32), ALU.add, ALU.subtract)
                    last.then_inc(h_ec, 1)

            def mask_dot(u):
                dve.wait_ge(h_d, 2 * u + 2)
                if u >= 2:
                    dve.wait_ge(h_s, 2 * u - 2)
                dve.tensor_scalar(dot_k(u, 0), bank[1], ccol("maskA"), None, ALU.mult)
                dve.tensor_scalar(dot_k(u, 1), bank[1], ccol("maskB"), None, ALU.mult).then_inc(h_dk, 1)

            def extract(u, p):
                dve.wait_ge(h_s, 2 * u + p + 1)
                if u >= 2:
                    dve.wait_ge(h_exp, u - 1)
                for j in (0, 1):
                    rows = slice(T * j, T * j + T)
                    last = dve.tensor_copy(own_scores(u, p, rows), own_banks(rows))
                last.then_inc(h_sxd, 1)

            def normalise(m):
                dve.wait_ge(h_inv, m + 1)
                if m >= 4:
                    dve.wait_ge(h_s, 2 * (m // 2) - 2)
                for j in range(2):
                    n = 2 * m + j
                    inv = n2(m)[:, j * 256:(j + 1) * 256].rearrange("p (b s) -> p b s", s=T // 2)
                    for c in range(2):
                        out = rot(n).rearrange("p (b c s) -> p c b s", c=2, s=T // 2)[:, c]
                        src = bank[2 + n % 4][:, c * 256:(c + 1) * 256].rearrange("p (b s) -> p b s", s=T // 2)
                        last = dve.scalar_tensor_tensor(out, inv, (QF, 1.0)[m % 2] * 1e12, src, ALU.min, ALU.mult)
                    last.then_inc(h_norm, 1)

            def value_blocks(t, b):
                dve.wait_ge(h_v, t + 1)
                keep = ccol("slot4").rearrange("p (a s x) -> p a s x", a=1, s=4).to_broadcast([P, 4, 4, HD])
                for j in range(SPT):
                    v = b[:, 32 * j:32 * j + 32].rearrange("p (g a x) -> p g a x", g=4, a=1).to_broadcast([P, 4, 4, HD])
                    last = dve.tensor_tensor(vb(t).rearrange("p (g b s x) -> p b g s x", g=4, b=4, s=4)[:, j], v, keep,
                                             ALU.mult)
                last.then_inc(h_vb, 1)

            def softmax_shift(u):
                dve.wait_ge(h_sxd, 2 * u + 2)
                dve.wait_ge(h_sxa, 2 * u + 2)
                s3 = sx(u).rearrange("p (g t) -> p g t", t=T)
                step(dve.tensor_reduce(hm, s3, AX.X, ALU.max))
                top = hm.rearrange("p (g a) -> p g a", a=1).to_broadcast([P, NH, T])
                dve.tensor_tensor(s3, s3, top, ALU.subtract).then_inc(h_sub, 1)

            def softmax_sum(u):
                dve.wait_ge(h_exp, u + 1)
                r = hsum(u)
                step(dve.tensor_reduce(r, ex(u).rearrange("p (g t) -> p g t", t=T), AX.X, ALU.add))
                dve.reciprocal(r, r).then_inc(h_sum, 1)

            def result(u):
                h, g = HEL[u]
                dve.wait_ge(h_pv, u + 1)
                dve.wait_ge(h_sum, u + 1)
                for j in range(SPT):
                    rows = slice(T * j, T * j + T)
                    inv = hsum(u)[rows, :].rearrange("p (i s a) -> p i s a", i=4, a=1).to_broadcast([T, HT, 4, HD])
                    src = bank[1][rows, :].rearrange("p (i b s x) -> p b i s x", i=4, b=4, s=4)[:, j]
                    out = Y[rows, h * HT:(h + 1) * HT, g * 32:(g + 1) * 32].rearrange("p i (s x) -> p i s x", s=4)
                    last = dve.tensor_tensor(out, src, inv, ALU.mult)
                last.then_inc(h_o, 1)
                if g == 3:
                    dve.wait_ge(h_o, u + 1)
                    v = Y[:, h * HT:(h + 1) * HT, :]
                    dve.tensor_tensor(v, v, along("bv"), ALU.add).then_inc(tok_ready, 1)
                    xv = X[:, h * HT:(h + 1) * HT, :]
                    step(dve.tensor_tensor(xv, xv, along("bo"), ALU.add))

            def add_out(h):
                dve.wait_ge(h_out, h + 1)
                dve.tensor_tensor(half(X, h), bank[(h + 1) % 2], half(X, h), ALU.add).then_inc(h_x, 1)

            dve.wait_ge(h_bias, 1)
            for u in range(len(HEL) + 2):
                if u == 0:
                    for t in range(HT):
                        value_blocks(t, bank[6 + t % 2])
                if u < len(HEL):
                    mask_dot(u)
                if u >= 2:
                    softmax_sum(u - 2)
                if u < len(HEL):
                    normalise(2 * u)
                    normalise(2 * u + 1)
                if 1 <= u <= len(HEL):
                    extract(u - 1, 0)
                if 1 <= u <= HT:
                    value_blocks(HT + u - 1, bank[0])
                if u >= 2:
                    result(u - 2)
                if 1 <= u <= len(HEL):
                    extract(u - 1, 1)
                    softmax_shift(u - 1)
                if u == 6:
                    add_out(0)
            add_out(1)
            dve.wait_ge(h_x, 2)
            for h in range(2):
                layernorm(h, X, Y).then_inc(tok_ready, 1)
            for h in range(2):
                split_y(h, turns + h + 1)
            softmax_router(NE1, 0, 1)
            keep_top(TOP1, NE1, 0, "rev1")
            step(dve.tensor_scalar(gs1[:, :], gs1[:, :], 1e-12, None, ALU.max))
            step(dve.reciprocal(gs1[:, :], gs1[:, :]))
            step(dve.tensor_tensor(gp[:, :, :], gp[:, :, :], over_experts(gs1, NE1), ALU.mult))
            routing_parts(NE1, 1)
            m = moe[1]
            dve.sem_inc(m["mul"], FREE1["mul"])
            dve.sem_inc(m["prod"], FREE1["prod"])

            def weigh(i, q):
                base = len(STEPS1) * i
                k, h, f = STEPS1[q % len(STEPS1)]
                dve.wait_ge(m["act"], base + q + 1 + FREE1["act"])
                if f == 0:
                    dve.wait_ge(m["gbc"], 8 * i + q // NF1 + 1)
                dve.wait_ge(m["prod"], base + q - 3 + FREE1["prod"])
                dve.tensor_tensor(prod[q % 4], act_out[q % 2], bank[h], ALU.mult).then_inc(m["mul"], 1)

            def body1(i, last):
                for q in range(len(STEPS1)):
                    if not last or q + 1 < len(STEPS1):
                        weigh(i, q + 1)
                    dve.wait_ge(m["hi"], len(STEPS1) * i + q + 1)
                    dve.tensor_tensor(pl4[q % 4], prod[q % 4], ph4[q % 4].bitcast(F32), ALU.subtract)\
                        .then_inc(m["prod"], 1)

            weigh(0, 0)
            bodies(dve, NE1 // 4, body1)
            moe_end(m)


def kernel(**inputs):
    import numpy as np
    import concourse.bacc as bacc
    from concourse.bass_utils import run_bass_kernel_spmd

    a = {k: np.asarray(v) for k, v in inputs.items()}
    f32 = np.float32

    def columns(v, n):
        return v.reshape(n, P).T

    def chunks(m):
        return m.reshape(-1, P, m.shape[1]).transpose(1, 0, 2).reshape(P, -1)

    slots = [4 * g + 2 * k + j for g in range(4) for j in range(2) for k in range(2)]
    slot_feats = np.array([s * HD + e for s in slots for e in range(HD)])
    strip_of = {0: 0, 2: 1, 1: 2, 3: 3}

    def strips(m):
        out = np.zeros((m.shape[1], 4, 4, T), f32)
        for g in range(4):
            for r, s in strip_of.items():
                out[:, g, s, 0:HD] = m[(4 * g + r) * HD:(4 * g + r + 1) * HD].T
        return out.reshape(m.shape[1], 4 * P)

    wh_ = a["L1_attn_Whel"].reshape(NH, HP, 2, HD)
    whel = np.zeros((2, 8, HD, NH // 2, 2, 2, 2, HP), f32)
    bhel = np.zeros((2, 2, HP, NH // 2, 2), f32)
    for u in range(NH // 2):
        for j in range(2):
            hd = 2 * u + j
            for par in range(2):
                for c in range(2):
                    whel[par, hd % 8, :, u, c, j, par, :] = wh_[hd, :, c, :].T
                    bhel[j, par, :, u, c] = a["L1_attn_bhel"][hd].reshape(HP, 2)[:, c]
    whel = whel.reshape(P, -1)
    bhel = bhel.reshape(P, -1)

    hb = np.concatenate([bhel.T.reshape(-1), strips(a["L1_attn_bq"][:, None]).reshape(-1),
                         strips(a["L1_attn_bk"][:, None]).reshape(-1)]).reshape(2, -1)
    hbias = np.zeros((34, hb.shape[1]), f32)
    hbias[0:2], hbias[32:34] = hb[0], hb[1]

    def parity_bias(b):
        return np.concatenate([b.reshape(2, 64).T] * 2, 0)

    vecs = {"tmk": a["L0_attn_time_mix_key"][:, None], "tmv": a["L0_attn_time_mix_value"][:, None],
            "tmr": a["L0_attn_time_mix_receptance"][:, None], "td": a["L0_attn_time_decay"][:, None],
            "tf": a["L0_attn_time_first"][:, None], "db1": columns(a["L1_xattn_b1"], FFD // P),
            "bqE": parity_bias(a["L1_attn_bq"]), "bkE": parity_bias(a["L1_attn_bk"]),
            "b1m": columns(a["L1_ffn_b1"].reshape(-1), NE1 * FF1 // P)}
    mats = {"Wk": a["L0_attn_Wk"], "Wv": a["L0_attn_Wv"], "Wr": a["L0_attn_Wr"], "Wo": a["L0_attn_Wo"],
            "router": a["L0_ffn_router_w"].T, "dw1": a["L1_xattn_w1"], "dw2": chunks(a["L1_xattn_w2"]),
            "WqE": a["L1_attn_Wq"].T, "WkE": a["L1_attn_Wk"].T, "WvT": a["L1_attn_Wv"][slot_feats].T,
            "WoT": a["L1_attn_Wo"].T[slot_feats], "Whel": whel, "WqD": strips(a["L1_attn_Wq"]),
            "WkD": strips(a["L1_attn_Wk"]), "gate": a["L1_ffn_gate"]}
    rows = {"g1": a["L1_xattn_g1"], "be1": a["L1_xattn_beta1"], "g2": a["L1_xattn_g2"], "be2": a["L1_xattn_beta2"],
            "g3": a["L1_xattn_g3"], "be3": a["L1_xattn_beta3"], "b2": a["L1_xattn_b2"],
            "bv": a["L1_attn_bv"][slot_feats], "bo": a["L1_attn_bo"]}

    tok = np.arange(P)
    same = tok[:, None] // T == tok[None, :] // T
    sel = np.zeros((P, NE0 + 1 + NE1), f32)
    for part in range(3):
        for e in range(NE0):
            sel[part * NE0 + e, e] = 1
        for e in range(NE1):
            sel[part * NE1 + e, NE0 + 1 + e] = 1
    consts = {"ident": np.eye(P), "causal": np.where(same & (tok[None, :] <= tok[:, None]), 0, NEG),
              "seq4": tok[:, None] // T == np.arange(SPT), "slot4": tok[:, None] // T == np.arange(SPT * HD) // HD,
              "maskA": (tok // T % 2 == 0)[:, None], "maskB": (tok // T % 2 == 1)[:, None],
              "biaslo": -(tok % 2).astype(f32)[:, None],
              "newseq": np.broadcast_to(np.where(np.arange(T) == 0, NEG, 0), (P, T)),
              "rev0": np.broadcast_to(np.arange(NE0 - 1, 0, -1), (P, NE0 - 1)),
              "rev1": np.broadcast_to(np.arange(NE1, 0, -1), (P, NE1)),
              "sel0": sel[:, 0:NE0 + 1], "sel1": sel[:, NE0 + 1:]}

    def pack(table, parts):
        for name, width in table:
            assert parts[name].shape[1] == width, (name, parts[name].shape)
        return np.concatenate([np.asarray(parts[name], f32) for name, _ in table], 1)

    ctx_ = a["ctx_1024"].reshape(NT, SPT, S, D)
    gate = np.concatenate([a["L0_ffn_shared_gate"][None], a["L0_ffn_routed_gate"]])
    up = np.concatenate([a["L0_ffn_shared_up"][None], a["L0_ffn_routed_up"]])
    down = np.concatenate([a["L0_ffn_shared_down"][None], a["L0_ffn_routed_down"]])
    down = down.transpose(0, 2, 1).reshape(NE0, FF0 // P, P, D).transpose(0, 2, 1, 3).reshape(NE0, P, FF0)
    w2 = a["L1_ffn_W2"].reshape(NE1, FF1 // P, P, D).transpose(0, 2, 1, 3).reshape(NE1, P, FF1)
    w1 = np.concatenate([a["L1_ffn_W1"], w2], 2)
    arrays = {
        "x": a["x"].reshape(NT * P, D),
        "zT": ctx_.transpose(0, 3, 1, 2), "z": ctx_[:, :, 0:2 * P].reshape(NT, SPT, 2, P, D).transpose(0, 3, 1, 2, 4),
        "zlast": ctx_[:, :, S - 1].transpose(1, 0, 2),
        "vec": pack(VECS, vecs), "mat": pack(MATS, mats), "row": pack(ROWS, {k: v[None] for k, v in rows.items()}),
        "con": pack(CONSTS, consts), "hbias": hbias,
        "mb2": np.concatenate([a["L1_ffn_b2"]] * 3),
        "w0": np.concatenate([gate.transpose(0, 2, 1), up.transpose(0, 2, 1), down], 2),
        "w1": w1.reshape(NE1 // 2, 2, P, 2 * FF1).transpose(0, 2, 1, 3).reshape(NE1 // 2, P, 4 * FF1),
    }
    arrays = {k: np.ascontiguousarray(v) for k, v in arrays.items()}

    nc = bacc.Bacc("TRN2", target_bir_lowering=False, num_devices=1)
    args = {k: nc.dram_tensor(f"in_{k}", v.shape, F32, kind="ExternalInput").ap() for k, v in arrays.items()}
    args["out"] = nc.dram_tensor("out_x", (NT * P, D), F32, kind="ExternalOutput").ap()
    build(nc, args)
    r = run_bass_kernel_spmd(nc, [{f"in_{k}": v for k, v in arrays.items()}], core_ids=[0])
    return r.results[0]["out_x"].reshape(NSEQ, T, D)
```

```python
import math
from contextlib import ExitStack

import concourse.bass as bass
from concourse import mybir

F32 = mybir.dt.float32
F32R = mybir.dt.float32r
BF16 = mybir.dt.bfloat16
ALU = mybir.AluOpType
ACT = mybir.ActivationFunctionType
AX = mybir.AxisListType

P = 128
NSEQ, T, D = 32, 32, 128
NT = NSEQ * T // P
HT = NT // 2
HN = HT * P
SPT = P // T
SPH = SPT * HT
S = 257
EPS = 1e-5
NE0, FF0, TOP0 = 8, 512, 2
NE1, FF1, TOP1 = 16, 256, 3
FFD = 512
NH, HD, HP = 16, 8, 32
NEG = -1e38
LN2 = math.log(2.0)
QF = float(HD) ** 0.5 / HP

VECS = [("tmk", 1), ("tmv", 1), ("tmr", 1), ("td", 1), ("tf", 1), ("db1", FFD // P), ("bqE", 2), ("bkE", 2), ("bqD", 4), ("bkD", 4),
        ("b1m", NE1 * FF1 // P)]
MATS = [("Wk", D), ("Wv", D), ("Wr", D), ("Wo", D), ("router", NE0 - 1), ("dw1", FFD), ("dw2", FFD),
        ("WqE", D), ("WkE", D), ("WvT", D), ("WoT", D), ("Whel", NH // 2 * 2 * P), ("WqD", 4 * P), ("WkD", 4 * P),
        ("gate", NE1)]
ROWS = [("g1", D), ("be1", D), ("g2", D), ("be2", D), ("g3", D), ("be3", D), ("b2", D), ("bv", D), ("bo", D)]
CONSTS = [("ident", P), ("causal", P), ("seq4", SPT), ("slot4", SPT * HD), ("biaslo", 1), ("maskA", 1), ("maskB", 1),
          ("newseq", T), ("rev0", NE0 - 1), ("rev1", NE1), ("sel0", NE0 + 1), ("sel1", NE1)]


def offsets(table):
    at, out = 0, {}
    for name, width in table:
        out[name] = (at, width)
        at += width
    return out, at


VEC_AT, VEC_W = offsets(VECS)
MAT_AT, MAT_W = offsets(MATS)
ROW_AT, ROW_W = offsets(ROWS)
CON_AT, CON_W = offsets(CONSTS)


def build(nc, d):
    with ExitStack() as ctx:
        def sb(name, shape, dt=F32):
            return ctx.enter_context(nc.sbuf_tensor(name, shape, dt))

        def sem(name):
            return ctx.enter_context(nc.semaphore(name))

        turn = [ctx.enter_context(nc.psum_tensor(f"turn{k}", [P, 512], F32)) for k in range(2)]
        pair = [ctx.enter_context(nc.psum_tensor(f"pair{k}", [P, 2, 512], F32)) for k in range(3)]
        bank = [turn[k][:, :] for k in range(2)] + [pair[k][:, j, :] for k in range(3) for j in range(2)]

        vec = sb("vec", [P, VEC_W])
        mat = sb("mat", [P, MAT_W])
        row = sb("row", [P, ROW_W])
        con = sb("con", [P, CON_W])
        selb = sb("selb", [3 * NE1, NE0 + 1 + NE1], BF16)
        mb2 = sb("mb2", [3 * NE1, D])
        identb = sb("identb", [P, P], BF16)
        zerob = sb("zerob", [P, P], BF16)
        cq, ck = sb("cq", [P, 1]), sb("ck", [P, 1])

        X = sb("X", [P, NT, D])
        Y = sb("Y", [P, NT, D])
        Y2b = sb("Y2b", [P, NT * D + 8])
        Y2 = Y2b[:, 0:NT * D].rearrange("p (t h) -> p t h", t=NT)
        YT = sb("YT", [P, NT * P])
        st = sb("st", [P, NT, 6])
        mv = sb("mv", [P, NT, 2])
        ve, ry, rt = sb("ve", [P, NT]), sb("ry", [P, NT]), sb("rt", [P, NT])
        nmx, ssum = sb("nmx", [P, NT]), sb("ssum", [P, NT])
        omt, tdn = sb("omt", [P, 3]), sb("tdn", [P, 1])
        hstat, lntiny = sb("hstat", [P, 48]), sb("lntiny", [P, 1])
        eps = sb("eps", [P, 1])

        with nc.sbuf_tensor("arena", [P, NSEQ * (S + 2 * D)], F32) as arena:
            pass
        arena_r = sb("arena_r", [P, NSEQ * (S + 2 * D)], F32R)
        zT = arena[:, 0:NSEQ * S].rearrange("p (b s) -> p b s", s=S)
        z = arena[:, NSEQ * S:NSEQ * (S + 2 * D)].rearrange("p (b c h) -> p b c h", c=2, h=D)
        zlast = sb("zlast", [SPT, NT, D])
        work = sb("work", [P, 18 * HN + 8])

        W0C, W1C = 3 * FF0, 2 * 2 * FF1
        yTh, yTl = sb("yTh", [P, NT * P], F32R), sb("yTl", [P, NT * P], F32R)
        gp, gq, gr = (sb(n, [P, NT, NE1]) for n in ("gp", "gq", "gr"))
        gs1 = sb("gs1", [P, NT])
        gpart = sb("gpart", [P, NT * 3 * NE1], BF16)
        g3b = sb("g3b", [3 * NE1, NT * P], BF16)
        wraw = sb("wraw", [P, W0C])
        wh = [sb(f"wh{k}", [P, W0C], F32R) for k in range(2)]
        wl = [sb(f"wl{k}", [P, W0C], F32R) for k in range(2)]
        xch = [sb(f"xch{k}", [P, HN], F32R) for k in range(2)]
        xcl = [sb(f"xcl{k}", [P, HN], F32R) for k in range(2)]
        ph = [sb(f"ph{k}", [P, HN], F32R) for k in range(2)]
        pl = [sb(f"pl{k}", [P, HN], F32R) for k in range(2)]

        def slot(k, n=1):
            return work[:, k * HN:(k + n) * HN]

        def vcol(name, k=0, n=1):
            return vec[:, VEC_AT[name][0] + k:VEC_AT[name][0] + k + n]

        def mcol(name, k=0, n=None):
            a, w = MAT_AT[name]
            return mat[:, a + k:a + k + (w if n is None else n)]

        def rcol(name):
            return row[:, ROW_AT[name][0]:ROW_AT[name][0] + D]

        def ccol(name):
            return con[:, CON_AT[name][0]:CON_AT[name][0] + CON_AT[name][1]]

        def half(buf, h):
            return buf[:, h * HT:(h + 1) * HT, :].rearrange("p t h -> p (t h)")

        def yt(h):
            return YT[:, h * HN:(h + 1) * HN]

        def blk(ap, i):
            return ap[:, i * P:(i + 1) * P]

        ident = ccol("ident")
        cprobs = lambda t: work[:, t * 260:t * 260 + S]
        clast = lambda t: work[:, 2100 + t * SPT:2100 + (t + 1) * SPT]
        cpT = lambda t: work[:, 2200 + t * 256:2200 + (t + 1) * 256]
        clastT = lambda t: work[0:SPT, 4300 + t * P:4300 + (t + 1) * P]
        rmix = lambda h, g: slot(3 * h + g)
        rexp = lambda h, k: slot(6 + 4 * h + k)
        mpo, mo, tdt = slot(14), slot(15), slot(16)
        run = [work[:, 17 * HN:18 * HN + 1], Y2b[:, 0:HN + 1], Y2b[:, HN + 2:2 * HN + 3]]
        rw = lambda h: rexp(h, 0)
        xc = slot(0)
        act_out, prod = [slot(1), slot(2)], [slot(3), slot(4), slot(9), slot(10)]
        moe_copy = lambda h: slot(5 + h)
        g3f = work[0:3 * NE1, 7 * HN:9 * HN]
        sprob, spT, smask = (lambda h: slot(11 + h)), (lambda h: slot(13 + h)), (lambda h: slot(15 + h))
        hid = lambda h: slot(4 * h, 4)
        HEL = [(u // 4, u % 4) for u in range(8)]
        aslot = lambda k: arena[:, k * HN:(k + 1) * HN]
        rot = lambda n: aslot(n % 8)
        dot_q, dot_k = (lambda u: aslot(8 + u % 2)), (lambda u, k: aslot(10 + 2 * k + u % 2))
        rslot = lambda k: arena_r[:, k * HN:(k + 1) * HN]
        qe_h, qe_l = (lambda h, w: rslot(22 + 4 * h + 2 * w)), (lambda h, w: rslot(23 + 4 * h + 2 * w))
        sq = lambda m: slot(4 + 2 * (m % 2), 2)
        n2 = lambda m: slot(8 + m % 2)
        sx, ex, ets = (lambda u: slot(10 + u % 2)), (lambda u: slot(12 + u % 2)), (lambda u: slot(14 + u % 2))
        oT = lambda h: slot(16)
        hsum, hm = (lambda u: hstat[:, 16 * (u % 2):16 * (u % 2) + 16]), hstat[:, 32:48]
        vb_at = [Y2b[:, 0:HN], Y2b[:, HN:2 * HN], arena[:, 30 * HN:31 * HN], arena[:, 31 * HN:32 * HN],
                 wraw[:, 0:HN], wraw[:, HN:2 * HN], wraw[:, 2 * HN:3 * HN], slot(17)]
        vb = lambda t: vb_at[t]
        bias_at, ones = [ph[0], ph[1], pl[0]], pl[1]

        def hel_bias(k):
            r, c = (0, k) if k < 12 else (32, k - 12)
            return bias_at[c // 4][r:r + 2, (c % 4) * P:(c % 4 + 1) * P], ones[r:r + 2, :]

        def own_banks(rows):
            return pair[2][rows, :, :].rearrange("p j (i k t) -> p j i k t", i=2, k=2)[:, :, :, :, rows]

        def own_scores(u, p, rows):
            return sx(u)[rows, :].rearrange("p (i j k t) -> p j i k t", i=4, j=2, k=2)[:, :, 2 * p:2 * p + 2]

        def whel(parts, k):
            return parts[k // 12][:, (k % 12) * P:(k % 12 + 1) * P]

        def parts_of(w):
            return gpart[:, 0:NT * 3 * w].rearrange("p (t n) -> p t n", t=NT)

        x_loaded, con_loaded, par_loaded, zl_loaded = sem("x_loaded"), sem("con_loaded"), sem("par_loaded"), sem("zl_loaded")
        z_loaded = [sem(f"z_loaded{t}") for t in range(NT)]
        dve_step, act_step, pool_step = sem("dve_step"), sem("act_step"), sem("pool_step")
        const_ready = sem("const_ready")
        eps_ready, n_var, n_inv = sem("eps_ready"), sem("n_var"), sem("n_inv")
        tok_ready = sem("tok_ready")
        tr_done = sem("tr_done")
        feat_ready = sem("feat_ready")
        y_hi, y_lo = sem("y_hi"), sem("y_lo")
        c_scores, c_max, c_probs, c_last, c_ptr, c_pT, c_out, c_x = (
            sem("c_" + n) for n in ("scores", "max", "probs", "last", "ptr", "pT", "out", "x"))
        r_decay = sem("r_decay")
        r_ymix, r_mix, r_kvr, r_kv, r_er, r_max, r_arg, r_parg, r_exp, r_ev, r_rw, r_out = (
            sem("r_" + n) for n in ("ymix", "mix", "kvr", "kv", "er", "max", "arg", "parg", "exp", "ev", "rw", "out"))
        m_logits, m_shift, m_exp, m_parts, m_gT, m_g3 = (
            sem("m_" + n) for n in ("logits", "shift", "exp", "parts", "gT", "g3"))
        a_scores, a_masked, a_prob, a_out, a_y2 = (sem("a_" + n) for n in ("scores", "masked", "prob", "out", "y2"))
        f_h, f_relu, f_out, f_sum = (sem("f_" + n) for n in ("h", "relu", "out", "sum"))
        h_w, bias_loaded, h_bias = sem("h_w"), sem("bias_loaded"), sem("h_bias")
        h_e, h_eh, h_ec, h_hel, h_sq, h_n2, h_inv, h_norm, h_d, h_dq, h_dk, h_v, h_vb = (
            sem("h_" + n) for n in ("e", "eh", "ec", "hel", "sq", "n2", "inv", "norm", "d", "dq", "dk", "v", "vb"))
        h_s, h_sxa, h_sxd, h_sub, h_exp, h_sum, h_et, h_ets, h_pv, h_o, h_out, h_x = (
            sem("h_" + n) for n in ("s", "sxa", "sxd", "sub", "exp", "sum", "et", "ets", "pv", "o", "out", "x"))
        moe = [{n: sem(f"moe{k}_{n}") for n in (
            "wload", "whi", "wsplit", "gbc", "xcm", "xch", "xcp", "gate", "mm", "act", "mul", "hi", "prod", "down",
            "accdone", "copied", "back", "x")} for k in range(2)]
        stored = sem("stored")
        NF0, NF1 = FF0 // P, FF1 // P
        STEPS0 = [(k, h, f) for k in range(2) for h in range(2) for f in range(NF0)]
        STEPS1 = [(k, h, f) for k in range(4) for h in range(2) for f in range(NF1)]
        FREE0 = {"mul": 2, "prod": 4, "down": 2, "xcm": 2, "mm": 2 * NF0}
        FREE1 = {"mul": 2 * NF1, "prod": 4, "down": 4, "act": 4}
        WC = FF0
        WCH0, WCH1 = W0C // WC, W1C // WC
        ph4 = [b[:, 0:HN] for b in ph] + [b[:, W1C:W1C + HN] for b in wh]
        pl4 = [b[:, 0:HN] for b in pl] + [b[:, W1C:W1C + HN] for b in wl]

        def bodies(eng, n, body):
            with eng.Fori(0, n - 1) as i:
                body(i, False)
            body(n - 1, True)

        def own_wait(eng):
            eng.nop(nofuse=True)

        block = ctx.enter_context(nc.Block())

        @block.sync
        def _(sp):
            xv = d["x"].rearrange("(t p) h -> p t h", p=P)
            sp.dma_start(X[:, :, :], xv).then_inc(x_loaded, 16)
            sp.dma_start(con[:, :], d["con"]).then_inc(con_loaded, 16)
            sp.dma_start(zlast[:, :, :], d["zlast"]).then_inc(zl_loaded, 16)
            for t in range(NT):
                sp.dma_start(zT[:, SPT * t:SPT * t + SPT, :], d["zT"][t]).then_inc(z_loaded[t], 16)
                sp.dma_start(z[:, SPT * t:SPT * t + SPT, :, :], d["z"][t]).then_inc(z_loaded[t], 16)
            sp.dma_start(vec[:, :], d["vec"]).then_inc(par_loaded, 16)
            sp.dma_start(mat[:, :], d["mat"]).then_inc(par_loaded, 16)
            sp.dma_start(row[:, :], d["row"].to_broadcast([P, ROW_W])).then_inc(par_loaded, 16)
            sp.dma_start(mb2[:, :], d["mb2"]).then_inc(par_loaded, 16)
            for k, (w, cols, n) in enumerate(((d["w0"], W0C, NE0), (d["w1"], W1C, NE1 // 2))):
                m = moe[k]
                if k == 1:
                    sp.wait_ge(moe[0]["wsplit"], NE0 * WCH0)
                    sp.dma_start(wraw[0:34, :], d["hbias"]).then_inc(bias_loaded, 16)
                    sp.wait_ge(h_pv, len(HEL))
                sp.dma_start(wraw[:, 0:cols], w[0]).then_inc(m["wload"], 16)
                with sp.Fori(1, n) as e:
                    sp.wait_ge(m["wsplit"], (WCH0, WCH1)[k] * e)
                    sp.dma_start(wraw[:, 0:cols], w[bass.ds(e, 1), :, :].rearrange("e p n -> p (e n)"))\
                        .then_inc(m["wload"], 16)
            ov = d["out"].rearrange("(t p) h -> p t h", p=P)
            for h in range(2):
                sp.wait_ge(moe[1]["x"], h + 1)
                sp.dma_start(ov[:, h * HT:(h + 1) * HT, :], X[:, h * HT:(h + 1) * HT, :]).then_inc(stored, 16)
            sp.wait_ge(stored, 32)

        @block.tensor
        def _(pe):
            turns = [0]

            def turn4(src):
                n = turns[0]
                turns[0] += 1
                pe.wait_ge(tok_ready, n + 1)
                if n >= 2:
                    pe.wait_ge(feat_ready, n - 1)
                for i in range(HT):
                    last = pe.transpose(blk(bank[n % 2], i), src(i), ident)
                last.then_inc(tr_done, 1)
                return n + 1

            def mm3(out, ah, al, bh, bl, start, stop):
                pe.matmul(out, ah, bh, start=start, stop=False)
                pe.matmul(out, ah, bl, start=False, stop=False)
                return pe.matmul(out, al, bh, start=False, stop=stop)

            def cross(call):
                def scores(t):
                    u = NT * call + t
                    pe.wait_ge(z_loaded[t], 32)
                    if u >= 2:
                        pe.wait_ge(c_last, u - 1)
                    for j in range(SPT):
                        b = SPT * t + j
                        last = pe.matmul(bank[2 + u % 2][T * j:T * j + T, 0:S], YT[:, b * T:(b + 1) * T], zT[:, b, :],
                                         start=True, stop=True)
                    last.then_inc(c_scores, 1)

                def turn_probs(t):
                    u = NT * call + t
                    pe.wait_ge(c_last, u + 1)
                    if u >= 2:
                        pe.wait_ge(c_pT, u - 1)
                    b = bank[4 + u % 2]
                    for c in range(2):
                        pe.transpose(blk(b, c), blk(cprobs(t), c), ident)
                    pe.transpose(b[0:SPT, 2 * P:3 * P], clast(t), ident).then_inc(c_ptr, 1)

                def weigh(t):
                    u = NT * call + t
                    pe.wait_ge(c_pT, u + 1)
                    if u >= 2:
                        pe.wait_ge(c_x, u - 1)
                    o = bank[6 + u % 2]
                    pe.matmul(o[:, 0:D], clastT(t), zlast[:, t, :], start=True, stop=False, skip_group_check=True)
                    for j in range(SPT):
                        for c in range(2):
                            last = pe.matmul(o[T * j:T * j + T, 0:D], cpT(t)[:, c * P + T * j:c * P + T * j + T],
                                             z[:, SPT * t + j, c, :], start=False, stop=c == 1, skip_group_check=True)
                    last.then_inc(c_out, 1)

                scores(0)
                scores(1)
                for t in range(NT + 1):
                    if t < NT:
                        turn_probs(t)
                    if t + 2 < NT:
                        scores(t + 2)
                    if t >= 1:
                        weigh(t - 1)

            def route(name, ne, rows, call):
                for t in range(NT):
                    last = pe.matmul(bank[2][:, t * NE1:t * NE1 + ne], blk(YT, t), mcol(name), start=True, stop=True)
                last.then_inc(m_logits, 1)
                for h in range(2):
                    pe.wait_ge(m_parts, call + 1)
                    for i in range(HT):
                        last = pe.transpose(blk(bank[3 + h].bitcast(BF16), i)[0:rows, :],
                                            parts_of(rows // 3)[:, h * HT + i, :], identb[:, :])
                    last.then_inc(m_gT, 1)

            def close(acc, rows, m):
                for h in range(2):
                    last = pe.matmul(acc[h], zerob[0:rows, :], g3b[0:rows, h * HN:(h + 1) * HN], start=False, stop=True)
                last.then_inc(m["accdone"], 1)

            def turn_back(m):
                for h in range(2):
                    pe.wait_ge(m["copied"], h + 1)
                    for i in range(HT):
                        last = pe.transpose(blk(bank[2 + h], i), blk(moe_copy(h), i), ident)
                    last.then_inc(m["back"], 1)

            acc = [bank[6], bank[7]]

            def moe0():
                m = moe[0]
                ROWS = 3 * NE0

                def spread(expert, un, g):
                    h = un % 2
                    pe.wait_ge(m["xcm"], g + FREE0["xcm"] - 1)
                    own_wait(pe)
                    pe.matmul(bank[h], selb[0:ROWS, bass.ds(expert, 1)].to_broadcast([ROWS, P]),
                              g3b[0:ROWS, h * HN:(h + 1) * HN], start=True, stop=True).then_inc(m["gbc"], 1)

                def up(i, q, last=False):
                    k, h, f = STEPS0[q % len(STEPS0)]
                    expert = 2 * i + q // (2 * NF0)
                    if h == 0 and f == 0:
                        pe.wait_ge(m["wsplit"], WCH0 * (expert + 1))
                    if f == 1 and not (last and q > len(STEPS0) - NF0):
                        spread(2 * i + (q // NF0 + 1) // 2, q // NF0 + 1, 4 * i + q // NF0 + 1)
                    pe.wait_ge(m["mul"], len(STEPS0) * i + q + FREE0["mul"] - 1)
                    a, b = slice(f * P, (f + 1) * P), slice(FF0 + f * P, FF0 + (f + 1) * P)
                    cols = slice(h * HN, (h + 1) * HN)
                    mm3(bank[2 + q % 2], wh[k][:, a], wl[k][:, a], yTh[:, cols], yTl[:, cols], True, True)\
                        .then_inc(m["gate"], 1)
                    if f == 0:
                        pe.wait_ge(m["xcp"], 4 * i + q // NF0 + 1)
                    mm3(bank[4 + q % 2], wh[k][:, b], wl[k][:, b], xch[h][:, :], xcl[h][:, :], True, True)\
                        .then_inc(m["mm"], 1)

                def down(i, q):
                    k, h, f = STEPS0[q]
                    pe.wait_ge(m["prod"], len(STEPS0) * i + q + 1 + FREE0["prod"])
                    c = slice(2 * FF0 + f * P, 2 * FF0 + (f + 1) * P)
                    mm3(acc[h], wh[k][:, c], wl[k][:, c], ph[q % 2][:, :], pl[q % 2][:, :], False, False)\
                        .then_inc(m["down"], 1)

                pe.wait_ge(m_g3, 2)
                pe.wait_ge(y_lo, 2)
                for h in range(2):
                    pe.matmul(acc[h], zerob[0:ROWS, :], g3b[0:ROWS, h * HN:(h + 1) * HN], start=True, stop=False)
                spread(0, 0, 0)
                pe.sem_inc(m["mm"], FREE0["mm"])
                pe.sem_inc(m["down"], FREE0["down"])
                up(0, 0)
                up(0, 1)

                def body(i, last):
                    for q in range(len(STEPS0)):
                        if not last or q + 2 < len(STEPS0):
                            up(i, q + 2, last)
                        down(i, q)

                bodies(pe, NE0 // 2, body)
                close(acc, ROWS, m)
                turn_back(m)

            def moe1():
                m = moe[1]
                pe.wait_ge(m_g3, 4)
                pe.wait_ge(y_lo, 6)
                for h in range(2):
                    pe.matmul(acc[h], mb2[:, :], g3f[:, h * HN:(h + 1) * HN], start=True, stop=False)
                pe.sem_inc(m["down"], FREE1["down"])

                def up(i, q):
                    k, h, f = STEPS1[q % len(STEPS1)]
                    base, expert = len(STEPS1) * i, 4 * i + q // (2 * NF1)
                    cols = slice(h * HN, (h + 1) * HN)
                    if f == 0:
                        if h == 0 and k % 2 == 0:
                            pe.wait_ge(m["wsplit"], WCH1 * (2 * i + q // (4 * NF1) + 1))
                        pe.wait_ge(m["mul"], base + q - 2 * NF1 + NF1 + FREE1["mul"])
                        own_wait(pe)
                        pe.matmul(bank[h], selb[:, bass.ds(expert + (NE0 + 1), 1)].to_broadcast([3 * NE1, P]),
                                  g3b[:, cols], start=True, stop=True).then_inc(m["gbc"], 1)
                    pe.wait_ge(m["act"], base + q - 3 + FREE1["act"])
                    a = slice((k % 2) * 2 * FF1 + f * P, (k % 2) * 2 * FF1 + (f + 1) * P)
                    mm3(bank[2 + q % 4], wh[k // 2][:, a], wl[k // 2][:, a], yTh[:, cols], yTl[:, cols], True, True)\
                        .then_inc(m["mm"], 1)

                def down(i, q):
                    k, h, f = STEPS1[q]
                    pe.wait_ge(m["prod"], len(STEPS1) * i + q + 1 + FREE1["prod"])
                    c = slice((k % 2) * 2 * FF1 + FF1 + f * P, (k % 2) * 2 * FF1 + FF1 + (f + 1) * P)
                    mm3(acc[h], wh[k // 2][:, c], wl[k // 2][:, c], ph4[q % 4], pl4[q % 4], False, False)\
                        .then_inc(m["down"], 1)

                for q in range(3):
                    up(0, q)

                def body(i, last):
                    for q in range(len(STEPS1)):
                        if not last or q + 3 < len(STEPS1):
                            up(i, q + 3)
                        down(i, q)

                bodies(pe, NE1 // 4, body)
                close(acc, 3 * NE1, m)
                turn_back(m)

            pe.wait_ge(con_loaded, 16)
            for h in range(2):
                n = turn4(lambda i: Y[:, h * HT + i, :])
            pe.wait_ge(feat_ready, n)
            pe.wait_ge(zl_loaded, 16)
            cross(0)
            pe.wait_ge(const_ready, 1)
            for h in range(2):
                turn4(lambda i: Y[:, h * HT + i, :])
                if h == 0:
                    pe.wait_ge(c_x, 2 * HT)
                for g, name in enumerate(("Wk", "Wv", "Wr")):
                    pe.wait_ge(r_mix, 3 * h + g + 1)
                    last = pe.matmul(bank[2 + 3 * h + g], mcol(name), rmix(h, g), start=True, stop=True)
                last.then_inc(r_kvr, 1)
            for h in range(2):
                pe.wait_ge(r_rw, h + 1)
                for i in range(HT):
                    last = pe.matmul(blk(bank[2 + h], i), blk(rw(h), i), mcol("Wo"), start=True, stop=True)
                last.then_inc(r_out, 1)
            for h in range(2):
                n = turn4(lambda i: Y[:, h * HT + i, :])
            pe.wait_ge(feat_ready, n)
            route("router", NE0 - 1, 3 * NE0, 0)
            moe0()
            for h in range(2):
                n = turn4(lambda i: Y[:, h * HT + i, :])
                pe.wait_ge(feat_ready, n)
                for i in range(HT):
                    y = blk(yt(h), i)
                    last = pe.matmul(blk(bank[2 + h], i), y, y, start=True, stop=True)
                last.then_inc(a_scores, 1)
            for h in range(2):
                n = turn4(lambda i: blk(sprob(h), i))
                pe.wait_ge(feat_ready, n)
                for i in range(HT):
                    last = pe.matmul(blk(bank[6 + h], i), blk(spT(h), i), Y[:, h * HT + i, :], start=True, stop=True)
                last.then_inc(a_out, 1)
            for h in range(2):
                n = turn4(lambda i: Y2[:, h * HT + i, :])
            pe.wait_ge(feat_ready, n)
            pe.wait_ge(a_y2, 2)
            cross(1)
            for h in range(2):
                n = turn4(lambda i: Y2[:, h * HT + i, :])
                pe.wait_ge(feat_ready, n)
                if h == 0:
                    pe.wait_ge(c_x, 4 * HT)
                for f in range(FFD // P):
                    u = h * (FFD // P) + f
                    if u >= 2:
                        pe.wait_ge(f_relu, u - 1)
                    pe.matmul(bank[2 + u % 2], blk(mcol("dw1"), f), yt(h), start=True, stop=True).then_inc(f_h, 1)
                pe.wait_ge(f_relu, (h + 1) * (FFD // P))
                for i in range(HT):
                    for f in range(FFD // P):
                        last = pe.matmul(blk(bank[4 + h], i), blk(hid(h), f * HT + i), blk(mcol("dw2"), f),
                                         start=f == 0, stop=f == FFD // P - 1)
                last.then_inc(f_out, 1)

            def project(h):
                parity = yt(h).rearrange("p (m c) -> p c m", c=2)
                if h == 1:
                    pe.wait_ge(h_ec, 2)
                    pe.wait_ge(h_vb, HT)
                for w, name in enumerate(("WqE", "WkE")):
                    for g in range(2):
                        for c in range(2):
                            last = pe.matmul(bank[6 + w][64 * c:64 * c + 64, g * 256:(g + 1) * 256],
                                             mcol(name, g * 64, 64), parity[:, c, :], start=True, stop=True)
                    last.then_inc(h_e, 1)

            def dots(u, w):
                h, g = HEL[u]
                cols = slice(h * HN, (h + 1) * HN)
                if u >= 1:
                    pe.wait_ge((h_dq, h_dk)[w], u)
                if w == 0:
                    if u >= 3:
                        pe.wait_ge(h_ets, u - 2)
                    if u >= 2:
                        pe.wait_ge(h_vb, min(HT + u - 1, NT))
                    if u == 7:
                        pe.wait_ge(feat_ready, 17)
                else:
                    if u >= 3:
                        pe.wait_ge(h_o, u - 2)
                    if u == 7:
                        pe.wait_ge(h_x, 1)
                    if u == 1:
                        pe.wait_ge(feat_ready, 16)
                mm3(bank[w], blk(xch[w], g), blk(xcl[w], g), yTh[:, cols], yTl[:, cols], True, True).then_inc(h_d, 1)

            def rotate(u, w, j):
                h, g = HEL[u]
                n, pr = 4 * u + 2 * w + j, 2 * g + j
                if n == 3:
                    pe.wait_ge(f_sum, 2)
                if n >= 4:
                    pe.wait_ge(h_norm, n - 3)
                cols = slice((pr // 4) * 256, (pr // 4 + 1) * 256)
                for c in range(2):
                    bias, one = hel_bias(2 * pr + c)
                    o = bank[2 + n % 4][:, c * 256:(c + 1) * 256]
                    pe.matmul(o, bias, one[:, 0:256], start=True, stop=False)
                    last = mm3(o, whel(wh, 2 * pr + c), whel(wl, 2 * pr + c), qe_h(h, w)[:, cols], qe_l(h, w)[:, cols],
                               False, True)
                last.then_inc(h_hel, 1)

            def score(u, p):
                if p == 0:
                    pe.wait_ge(h_norm, 4 * u + 4)
                    pe.wait_ge(h_dq, u + 1)
                    pe.wait_ge(h_dk, u + 1)
                if 2 * u + p >= 1:
                    pe.wait_ge(h_sxa, 2 * u + p)
                    pe.wait_ge(h_sxd, 2 * u + p)
                for i in range(2):
                    cols = slice((2 * p + i) * P, (2 * p + i + 1) * P)
                    for k in range(2):
                        for n, (a, b) in enumerate(((rot(4 * u + k), rot(4 * u + 2 + k)), (dot_q(u), dot_k(u, k)))):
                            for j in range(2):
                                rows = slice(64 * j, 64 * j + 64)
                                last = pe.matmul(pair[2][:, j, (2 * i + k) * P:(2 * i + k + 1) * P], a[rows, cols],
                                                 b[rows, cols], start=n == 0, stop=n == 1, skip_group_check=True)
                last.then_inc(h_s, 1)

            def turn_weights(u):
                pe.wait_ge(h_exp, u + 1)
                pe.wait_ge(h_dq, min(u + 3, 8))
                if u >= 1:
                    pe.wait_ge(h_ets, u)
                if u == 5:
                    pe.wait_ge(feat_ready, 17)
                for i in range(HT):
                    last = pe.transpose(blk(bank[0], i), blk(ex(u), i), ident)
                last.then_inc(h_et, 1)

            def weigh_values(u):
                h, g = HEL[u]
                pe.wait_ge(h_ets, u + 1)
                pe.wait_ge(h_vb, HT * (h + 1))
                pe.wait_ge(h_dk, min(u + 3, 8))
                if u >= 1:
                    pe.wait_ge(h_o, u)
                if u == 5:
                    pe.wait_ge(h_x, 1)
                for i in range(HT):
                    last = pe.matmul(blk(bank[1], i), blk(ets(u), i), blk(vb(h * HT + i), g), start=True, stop=True)
                last.then_inc(h_pv, 1)

            def values(t, b):
                by_slot = mcol("WvT").rearrange("p (g s x) -> p s g x", g=4, s=4)
                for s in range(4):
                    for j in range(SPT):
                        c = (t * SPT + j) * T
                        last = pe.matmul(b[32 * s:32 * s + 32, 32 * j:32 * j + 32], YT[:, c:c + T], by_slot[:, s],
                                         start=True, stop=True)
                last.then_inc(h_v, 1)

            def turn_results(h):
                pe.wait_ge(h_ets, 4 * h + 4 + (h == 0))
                turn4(lambda i: Y[:, h * HT + i, :])

            def project_out(h):
                pe.wait_ge(h_o, 4 * h + 4 + (h == 0))
                pe.wait_ge(feat_ready, 17 + 2 * h)
                for i in range(HT):
                    last = pe.matmul(blk(bank[1], i), blk(oT(h), i), mcol("WoT"), start=True, stop=True)
                last.then_inc(h_out, 1)

            def prepare(h):
                if h == 1:
                    pe.wait_ge(h_dk, 1)
                n = turn4(lambda i: Y[:, h * HT + i, :])
                pe.wait_ge(feat_ready, n)
                project(h)

            prepare(0)
            pe.wait_ge(h_w, 1)
            pe.wait_ge(h_bias, 1)
            for u in range(len(HEL) + 2):
                if u % 4 == 0 and u < len(HEL):
                    pe.wait_ge(y_lo, 3 + u // 4)
                    pe.wait_ge(h_ec, 2 + u // 2)
                if u < len(HEL):
                    for w in range(2):
                        dots(u, w)
                    for w in range(2):
                        for j in range(2):
                            rotate(u, w, j)
                if u == 0:
                    for t in range(HT):
                        if t >= 2:
                            pe.wait_ge(h_vb, t - 1)
                        values(t, bank[6 + t % 2])
                    prepare(1)
                    pe.wait_ge(h_ec, 4)
                if u >= 2:
                    turn_weights(u - 2)
                if 1 <= u <= len(HEL):
                    score(u - 1, 0)
                if 1 <= u <= HT:
                    pe.wait_ge(h_dq, u + 1)
                    if u >= 2:
                        pe.wait_ge(h_ets, u - 1)
                    values(HT + u - 1, bank[0])
                if u == 6:
                    turn_results(0)
                if u == 9:
                    pe.wait_ge(h_o, 7)
                    turn4(lambda i: Y[:, i, :])
                    pe.wait_ge(feat_ready, 18)
                if u >= 2:
                    weigh_values(u - 2)
                if 1 <= u <= len(HEL):
                    score(u - 1, 1)
                if u == 6:
                    project_out(0)
            turn_results(1)
            project_out(1)
            pe.wait_ge(h_x, 2)
            n = turn4(lambda i: Y[:, HT + i, :])
            pe.wait_ge(feat_ready, n)
            route("gate", NE1, 3 * NE1, 1)
            moe1()

        @block.scalar
        def _(act):
            count = {"turn": 0, "step": 0, "norm": 0}

            def step(ins):
                count["step"] += 1
                ins.then_inc(act_step, 1)
                act.wait_ge(act_step, count["step"])

            def copy_turned(dst):
                n = count["turn"]
                count["turn"] += 1
                act.wait_ge(tr_done, n + 1)
                act.activation(dst, bank[n % 2], ACT.Copy).then_inc(feat_ready, 1)

            def inverse_std(*halves):
                hs = slice(halves[0] * HT, (halves[-1] + 1) * HT)
                count["norm"] += 1
                act.wait_ge(n_var, count["norm"])
                step(act.activation(ry[:, hs], mv[:, hs, 1], ACT.Ln, bias=eps[:, :]))
                act.activation(ry[:, hs], ry[:, hs], ACT.Exp, scale=-0.5).then_inc(n_inv, 1)

            def round_turned(h):
                act.wait_ge(feat_ready, count["turn"])
                c = slice(h * HN, (h + 1) * HN)
                act.activation(yTh[:, c], YT[:, c], ACT.Copy).then_inc(y_hi, 1)

            scale = float(D) ** -0.5
            LN_EXP = "natural_log_exp_and_others"
            act.preload_act_table_set(LN_EXP)
            act.wait_ge(eps_ready, 1)
            inverse_std(0, 1)
            act.preload_act_table(ACT.Gelu_apprx_tanh)
            for h in range(2):
                copy_turned(yt(h))
            for t in range(NT):
                act.wait_ge(c_scores, t + 1)
                act.activation(cprobs(t), bank[2 + t % 2][:, 0:S], ACT.Gelu_apprx_tanh).then_inc(c_probs, 1)
            act.preload_act_table_set(LN_EXP)
            inverse_std(0, 1)
            act.wait_ge(const_ready, 1)
            act.activation(tdn[:, :], vcol("td"), ACT.Exp).then_inc(r_decay, 1)
            for h in range(2):
                copy_turned(yt(h))
                act.wait_ge(feat_ready, 2 + h + 1)
                for g, name in enumerate(("tmk", "tmv", "tmr")):
                    act.activation(rmix(h, g), yt(h), ACT.Copy, scale=vcol(name)).then_inc(r_ymix, 1)
            for h in range(2):
                act.wait_ge(r_kvr, h + 1)
                for g in range(2):
                    last = act.activation(rmix(h, g), bank[2 + 3 * h + g], ACT.Copy)
                last.then_inc(r_kv, 1)
                act.activation(rmix(h, 2), bank[4 + 3 * h], ACT.Exp, scale=-1.0).then_inc(r_er, 1)
            for h in range(2):
                for k, (ready, n) in enumerate(((r_arg, 3 * h + 1), (r_parg, h + 1), (r_arg, 3 * h + 2), (r_arg, 3 * h + 3))):
                    act.wait_ge(ready, n)
                    act.activation(rexp(h, k), rexp(h, k), ACT.Exp).then_inc(r_exp, 1)
            inverse_std(0, 1)
            for h in range(2):
                copy_turned(yt(h))
            for h in range(2):
                round_turned(h)
            act.wait_ge(m_shift, 1)
            act.activation(gq[:, :, 0:NE0 - 1], gq[:, :, 0:NE0 - 1], ACT.Exp).then_inc(m_exp, 1)
            def weights_hi(m, load, k, c, free):
                act.wait_ge(m["wload"], 16 * load + 16)
                if free is not None:
                    act.wait_ge(m["down"], free)
                cols = slice(c * WC, (c + 1) * WC)
                act.activation(wh[k][:, cols], wraw[:, cols], ACT.Copy).then_inc(m["whi"], 1)

            def body0(i, last):
                m, base = moe[0], len(STEPS0) * i
                for q in range(len(STEPS0)):
                    k, h, f = STEPS0[q]
                    act.wait_ge(m["gate"], base + q + 1)
                    act.wait_ge(m["mul"], base + q + FREE0["mul"] - 1)
                    act.activation(act_out[q % 2], bank[2 + q % 2], ACT.Silu).then_inc(m["act"], 1)
                    un = q // NF0
                    if f == 1 and not (last and un == 3):
                        act.wait_ge(m["xcm"], 4 * i + un + 2 + FREE0["xcm"])
                        act.wait_ge(m["mm"], NF0 * (4 * i + un) + FREE0["mm"])
                        act.activation(xch[(un + 1) % 2][:, :], xc, ACT.Copy).then_inc(m["xch"], 1)
                    c = q % (2 * NF0) - 2
                    if 0 <= c < WCH0 and not (last and k == 1):
                        weights_hi(m, 2 * i + k + 1, (k + 1) % 2, c, 2 * NF0 * (2 * i + k) + FREE0["down"])
                    act.wait_ge(m["mul"], base + q + 1 + FREE0["mul"])
                    act.wait_ge(m["down"], base + q + FREE0["down"] - 1)
                    act.activation(ph[q % 2][:, :], prod[q % 4], ACT.Copy).then_inc(m["hi"], 1)

            m = moe[0]
            act.preload_act_table(ACT.Silu)
            for c in range(WCH0):
                weights_hi(m, 0, 0, c, None)
            act.wait_ge(m["xcm"], 1 + FREE0["xcm"])
            act.activation(xch[0][:, :], xc, ACT.Copy).then_inc(m["xch"], 1)
            bodies(act, NE0 // 2, body0)
            act.wait_ge(m["accdone"], 1)
            for h in range(2):
                act.activation(moe_copy(h), bank[6 + h], ACT.Copy).then_inc(m["copied"], 1)
            act.preload_act_table_set(LN_EXP)
            inverse_std(0, 1)
            for h in range(2):
                copy_turned(yt(h))
            for h in range(2):
                act.wait_ge(a_masked, h + 1)
                for i in range(HT):
                    t = h * HT + i
                    last = act.activation(blk(sprob(h), i), blk(smask(h), i), ACT.Exp, bias=nmx[:, t:t + 1],
                                          scale=scale, accum_out=ssum[:, t:t + 1])
                last.then_inc(a_prob, 1)
            for h in range(2):
                copy_turned(spT(h))
            inverse_std(0, 1)
            for h in range(2):
                copy_turned(yt(h))
            for t in range(NT):
                act.wait_ge(c_max, t + 1)
                act.activation(cprobs(t), bank[2 + t % 2][:, 0:S], ACT.Exp, bias=nmx[:, t:t + 1], scale=scale,
                               accum_out=ssum[:, t:t + 1]).then_inc(c_probs, 1)
            inverse_std(0, 1)
            for h in range(2):
                copy_turned(yt(h))
                for f in range(FFD // P):
                    u = h * (FFD // P) + f
                    act.wait_ge(f_h, u + 1)
                    act.activation(hid(h)[:, f * HN:(f + 1) * HN], bank[2 + u % 2], ACT.Relu,
                                   bias=vcol("db1", f)).then_inc(f_relu, 1)
            def squares(m):
                if m >= 2:
                    act.wait_ge(h_n2, m - 1)
                for j in range(2):
                    n = 2 * m + j
                    act.wait_ge(h_hel, n + 1)
                    act.activation(sq(m)[:, j * HN:(j + 1) * HN], bank[2 + n % 4], ACT.Square).then_inc(h_sq, 1)

            def inverse(m):
                act.wait_ge(h_n2, m + 1)
                step(act.activation(n2(m), n2(m), ACT.Ln, scale=float(2 ** 20), bias=lntiny[:, :]))
                act.activation(n2(m), n2(m), ACT.Exp, scale=-0.5, bias=(cq, ck)[m % 2][:, :]).then_inc(h_inv, 1)

            def extract(u, p):
                act.wait_ge(h_s, 2 * u + p + 1)
                if u >= 2:
                    act.wait_ge(h_exp, u - 1)
                for j in (2, 3):
                    rows = slice(T * j, T * j + T)
                    last = act.activation(own_scores(u, p, rows), own_banks(rows), ACT.Copy)
                last.then_inc(h_sxa, 1)

            def prepare(h):
                copy_turned(yt(h))
                for w, name in enumerate(("bqE", "bkE")):
                    act.wait_ge(h_e, 2 * h + w + 1)
                    for g in range(2):
                        c = slice(g * 256, (g + 1) * 256)
                        last = act.activation(qe_h(h, w)[:, c], bank[6 + w][:, c], ACT.Identity, bias=vcol(name, g))
                    last.then_inc(h_eh, 1)
                round_turned(h)

            for h in range(2):
                inverse_std(h)
                inverse_std(h)
                if h == 0:
                    prepare(0)
            for u in range(len(HEL) + 2):
                if u < len(HEL):
                    act.wait_ge(h_d, 2 * u + 1)
                    if u >= 2:
                        act.wait_ge(h_s, 2 * u - 2)
                    act.activation(dot_q(u), bank[0], ACT.Identity, bias=vcol("bqD", u % 4)).then_inc(h_dq, 1)
                if u >= 2:
                    act.wait_ge(h_sub, u - 1)
                    if u >= 4:
                        act.wait_ge(h_et, u - 3)
                        act.wait_ge(h_sum, u - 3)
                    act.activation(ex(u - 2), sx(u - 2), ACT.Exp, scale=0.5 * float(HD) ** -0.5).then_inc(h_exp, 1)
                if u < len(HEL):
                    squares(2 * u)
                    squares(2 * u + 1)
                    inverse(2 * u)
                if u >= 2:
                    act.wait_ge(h_et, u - 1)
                    if u >= 4:
                        act.wait_ge(h_pv, u - 3)
                    act.activation(ets(u - 2), bank[0], ACT.Copy).then_inc(h_ets, 1)
                if u < len(HEL):
                    inverse(2 * u + 1)
                if u == 0:
                    prepare(1)
                if 1 <= u <= len(HEL):
                    extract(u - 1, 0)
                if u == 6:
                    copy_turned(oT(0))
                if 1 <= u <= len(HEL):
                    extract(u - 1, 1)
                if u == 9:
                    inverse_std(0)
                    copy_turned(yt(0))
                    round_turned(0)
            copy_turned(oT(1))
            inverse_std(1)
            copy_turned(yt(1))
            round_turned(1)
            act.wait_ge(m_shift, 2)
            act.activation(gq[:, :, 0:NE1], gq[:, :, 0:NE1], ACT.Exp).then_inc(m_exp, 1)
            m = moe[1]
            act.sem_inc(m["act"], FREE1["act"])

            def relu(i, q):
                base = len(STEPS1) * i
                m = moe[1]
                act.wait_ge(m["mm"], base + q + 1)
                act.wait_ge(m["mul"], base + q - 1 + FREE1["mul"])
                own_wait(act)
                k, h, f = STEPS1[q % len(STEPS1)]
                at = 4 * NF1 * i + (VEC_AT["b1m"][0] + q // (2 * NF1) * NF1 + f)
                act.activation(act_out[q % 2], bank[2 + q % 4], ACT.Relu, bias=vec[:, bass.ds(at, 1)])\
                    .then_inc(m["act"], 1)

            def body1(i, last):
                m, base = moe[1], len(STEPS1) * i
                for q in range(len(STEPS1)):
                    act.wait_ge(m["mul"], base + q + 1 + FREE1["mul"])
                    act.wait_ge(m["down"], base + q - 3 + FREE1["down"])
                    act.activation(ph4[q % 4], prod[q % 4], ACT.Copy).then_inc(m["hi"], 1)
                    if not last or q + 2 < len(STEPS1):
                        relu(i, q + 2)

            relu(0, 0)
            relu(0, 1)
            bodies(act, NE1 // 4, body1)
            act.wait_ge(m["accdone"], 1)
            for h in range(2):
                act.activation(moe_copy(h), bank[6 + h], ACT.Copy).then_inc(m["copied"], 1)

        @block.gpsimd
        def _(pool):
            pool.memset(zerob[:, :], 0.0)
            pool.memset(cq[:, :], LN2 * 10 + math.log(QF))
            pool.memset(lntiny[:, :], 1e-26)
            pool.memset(eps[:, :], EPS).then_inc(eps_ready, 1)
            pool.memset(ck[:, :], LN2 * 10)
            pool.wait_ge(con_loaded, 16)
            pool.tensor_copy(identb[:, :], ident)
            pool.tensor_copy(selb[:, :], con[0:3 * NE1, CON_AT["sel0"][0]:CON_AT["sel1"][0] + CON_AT["sel1"][1]])\
                .then_inc(pool_step, 1)
            pool.wait_ge(pool_step, 1)
            pool.wait_ge(par_loaded, 4 * 16)
            pool.sem_inc(const_ready, 1)

            for h in range(2):
                pool.wait_ge(r_max, h + 1)
                pool.tensor_tensor(rexp(h, 1), rmix(h, 0), run[0][:, 1:HN + 1], ALU.subtract).then_inc(r_parg, 1)
            for h in range(2):
                pool.wait_ge(r_exp, 4 * h + 2)
                pool.wait_ge(r_arg, 3 * h + 3)
                pool.tensor_tensor(rmix(h, 0), rexp(h, 1), rmix(h, 1), ALU.mult).then_inc(r_ev, 1)
                pool.wait_ge(r_exp, 4 * h + 4)
                pool.wait_ge(r_ev, 2 * h + 1)
                pool.tensor_tensor(rmix(h, 1), rexp(h, 3), rmix(h, 1), ALU.mult).then_inc(r_ev, 1)

            def y_rest(h, n):
                pool.wait_ge(y_hi, n)
                c = slice(h * HN, (h + 1) * HN)
                pool.tensor_tensor(yTl[:, c], YT[:, c], yTh[:, c].bitcast(F32), ALU.subtract).then_inc(y_lo, 1)

            def weights_lo(m, nch, load, k):
                for c in range(nch):
                    cols = slice(c * WC, (c + 1) * WC)
                    pool.wait_ge(m["whi"], nch * load + c + 1)
                    pool.tensor_tensor(wl[k][:, cols], wraw[:, cols], wh[k][:, cols].bitcast(F32), ALU.subtract)\
                        .then_inc(m["wsplit"], 1)

            def pool_body0(i, last):
                weights_lo(moe[0], WCH0, 2 * i + 1, 1)
                if not last:
                    weights_lo(moe[0], WCH0, 2 * i + 2, 0)

            for h in range(2):
                y_rest(h, h + 1)
            weights_lo(moe[0], WCH0, 0, 0)
            bodies(pool, NE0 // 2, pool_body0)
            pool.wait_ge(moe[0]["accdone"], 1)
            pool.memset(ones[0:34, :].bitcast(F32), 1.0)
            parts = [(wh[0][:, :], wl[0][:, :], mcol("Whel", 0, W0C)),
                     (wh[1][:, 0:HN], wl[1][:, 0:HN], mcol("Whel", W0C, HN)),
                     (xch[0][:, :], xcl[0][:, :], mcol("WqD")), (xch[1][:, :], xcl[1][:, :], mcol("WkD"))]
            for hi, lo, w in parts:
                pool.tensor_copy(hi, w).then_inc(pool_step, 1)
            pool.wait_ge(pool_step, 5)
            for hi, lo, w in parts:
                last = pool.tensor_tensor(lo, w, hi.bitcast(F32), ALU.subtract)
            last.then_inc(h_w, 1)

            def add_squares(m):
                pool.wait_ge(h_sq, 2 * m + 2)
                if m >= 2:
                    pool.wait_ge(h_norm, 2 * m - 2)
                s4 = sq(m).rearrange("p (j c m) -> p j c m", j=2, c=2)
                pool.tensor_tensor(n2(m).rearrange("p (j m) -> p j m", j=2), s4[:, :, 0], s4[:, :, 1], ALU.add)\
                    .then_inc(h_n2, 1)

            y_rest(0, 3)
            for m in range(2 * len(HEL)):
                add_squares(m)
                if m == 1:
                    y_rest(1, 4)

            def split_pair(load, k, free):
                m = moe[1]
                pool.wait_ge(m["wload"], 16 * load + 16)
                if free is not None:
                    pool.wait_ge(m["down"], free)
                for c in range(WCH1):
                    cols = slice(c * WC, (c + 1) * WC)
                    own_wait(pool)
                    pool.tensor_copy(wh[k][:, cols], wraw[:, cols]).then_inc(m["whi"], 1)
                for c in range(WCH1):
                    cols = slice(c * WC, (c + 1) * WC)
                    pool.wait_ge(m["whi"], WCH1 * load + c + 1)
                    pool.tensor_tensor(wl[k][:, cols], wraw[:, cols], wh[k][:, cols].bitcast(F32), ALU.subtract)\
                        .then_inc(m["wsplit"], 1)

            def pool_body1(i, last):
                split_pair(2 * i + 1, 1, 4 * NF1 * (2 * i) + FREE1["down"])
                if not last:
                    split_pair(2 * i + 2, 0, 4 * NF1 * (2 * i + 1) + FREE1["down"])

            for h in range(2):
                y_rest(h, h + 5)
            split_pair(0, 0, None)
            bodies(pool, NE1 // 4, pool_body1)

        @block.vector
        def _(dve):
            count = {"step": 0, "norm": 0}

            def step(ins):
                count["step"] += 1
                ins.then_inc(dve_step, 1)
                dve.wait_ge(dve_step, count["step"])

            def layernorm(halves, src, dst, after=None):
                ts = range(halves[0] * HT, (halves[-1] + 1) * HT)
                hs = slice(ts[0], ts[-1] + 1)
                for t in ts:
                    last = dve.bn_stats(st[:, t, :], src[:, t, :])
                step(last)
                for t in ts:
                    last = dve.bn_aggr(mv[:, t, :], st[:, t, :])
                count["norm"] += 1
                last.then_inc(n_var, 1)
                dve.wait_ge(n_var, count["norm"])
                v, r, w = ve[:, hs], ry[:, hs], rt[:, hs]
                step(dve.tensor_scalar(v, mv[:, hs, 1], EPS, None, ALU.add))
                dve.wait_ge(n_inv, count["norm"])
                step(dve.tensor_tensor(w, r, r, ALU.mult))
                step(dve.scalar_tensor_tensor(w, w, -0.5, v, ALU.mult, ALU.mult))
                step(dve.scalar_tensor_tensor(r, w, 1.5, r, ALU.add, ALU.mult))
                for h in halves:
                    for t in range(h * HT, (h + 1) * HT):
                        last = dve.tensor_scalar(dst[:, t, :], src[:, t, :], mv[:, t, 0:1], ry[:, t:t + 1],
                                                 ALU.subtract, ALU.mult)
                    if after is None:
                        last.then_inc(tok_ready, 1)
                    else:
                        step(last)
                        after(h)

            def along(name):
                return rcol(name).rearrange("p (a h) -> p a h", a=1).to_broadcast([P, HT, D])

            def affine(h, buf, g, b):
                v = buf[:, h * HT:(h + 1) * HT, :]
                step(dve.tensor_tensor(v, v, along(g), ALU.mult))
                return dve.tensor_tensor(v, v, along(b), ALU.add)

            def cross(call):
                def top(t):
                    dve.wait_ge(c_scores, NT * call + t + 1)
                    step(dve.tensor_reduce(nmx[:, t:t + 1], bank[2 + t % 2][:, 0:S], AX.X, ALU.max))
                    dve.tensor_scalar(nmx[:, t:t + 1], nmx[:, t:t + 1], -float(D) ** -0.5, None, ALU.mult)\
                        .then_inc(c_max, 1)

                def result(t):
                    dve.wait_ge(c_out, NT * call + t + 1)
                    o = bank[6 + t % 2]
                    if call == 0:
                        dve.tensor_tensor(X[:, t, :], o[:, 0:D], X[:, t, :], ALU.add).then_inc(c_x, 1)
                    else:
                        dve.scalar_tensor_tensor(Y2[:, t, :], o[:, 0:D], ssum[:, t:t + 1], Y2[:, t, :],
                                                 ALU.mult, ALU.add).then_inc(c_x, 1)

                if call == 1:
                    top(0)
                    top(1)
                for t in range(NT + 2):
                    if t < NT:
                        u = NT * call + t
                        dve.wait_ge(c_probs, u + 1)
                        dve.tensor_scalar(clast(t), ccol("seq4"), cprobs(t)[:, S - 1:S], None, ALU.mult)\
                            .then_inc(c_last, 1)
                        if call == 1:
                            step(dve.reciprocal(ssum[:, t:t + 1], ssum[:, t:t + 1]))
                        dve.wait_ge(c_ptr, u + 1)
                        b = bank[4 + u % 2]
                        dve.tensor_copy(clastT(t), b[0:SPT, 2 * P:3 * P])
                        dve.tensor_copy(cpT(t), b[:, 0:2 * P]).then_inc(c_pT, 1)
                    if t >= 2:
                        result(t - 2)
                    if call == 1 and t + 2 < NT:
                        top(t + 2)
                dve.wait_ge(c_x, (call + 1) * NT)

            def over_experts(v, ne):
                return v[:, :].rearrange("p (t a) -> p t a", a=1).to_broadcast([P, NT, ne])

            def softmax_router(ne, r0, call):
                dve.wait_ge(m_logits, call + 1)
                lg = bank[2][:, 0:NT * NE1].rearrange("p (t e) -> p t e", e=NE1)[:, :, 0:ne]
                step(dve.tensor_reduce(gs1[:, :], lg, AX.X, ALU.max))
                dve.tensor_tensor(gq[:, :, 0:ne], lg, over_experts(gs1, ne), ALU.subtract).then_inc(m_shift, 1)
                dve.wait_ge(m_exp, call + 1)
                step(dve.tensor_reduce(gs1[:, :], gq[:, :, 0:ne], AX.X, ALU.add))
                step(dve.reciprocal(gs1[:, :], gs1[:, :]))
                step(dve.tensor_tensor(gp[:, :, r0:r0 + ne], gq[:, :, 0:ne], over_experts(gs1, ne), ALU.mult))

            def keep_top(k, ne, r0, rev):
                pv, qv, rv = (b[:, :, r0:r0 + ne] for b in (gp, gq, gr))
                order = ccol(rev).rearrange("p (a e) -> p a e", a=1).to_broadcast([P, NT, ne])
                step(dve.tensor_copy(qv, pv))
                for j in range(k):
                    step(dve.tensor_reduce(gs1[:, :], qv, AX.X, ALU.max))
                    step(dve.tensor_tensor(rv, qv, over_experts(gs1, ne), ALU.is_equal))
                    step(dve.tensor_tensor(rv, rv, order, ALU.mult))
                    step(dve.tensor_reduce(gs1[:, :], rv, AX.X, ALU.max))
                    step(dve.tensor_tensor(rv, rv, over_experts(gs1, ne), ALU.is_equal))
                    step(dve.scalar_tensor_tensor(qv, rv, -2.0, qv, ALU.mult, ALU.add))
                step(dve.scalar_tensor_tensor(pv, qv, 0.0, pv, ALU.is_lt, ALU.mult))
                step(dve.tensor_reduce(gs1[:, :], pv, AX.X, ALU.add))

            def routing_parts(w, call):
                p3 = [parts_of(w)[:, :, a * w:(a + 1) * w] for a in range(3)]
                r, g = gr[:, :, 0:w], gp[:, :, 0:w]
                step(dve.tensor_copy(p3[0], g))
                step(dve.tensor_tensor(r, g, p3[0], ALU.subtract))
                step(dve.tensor_copy(p3[1], r))
                step(dve.tensor_tensor(r, r, p3[1], ALU.subtract))
                dve.tensor_copy(p3[2], r).then_inc(m_parts, 1)
                for h in range(2):
                    dve.wait_ge(m_gT, 2 * call + h + 1)
                    src = bank[3 + h].bitcast(BF16)[0:3 * w, 0:HN]
                    c = slice(h * HN, (h + 1) * HN)
                    if call == 1:
                        dve.tensor_copy(g3f[:, c], src)
                    dve.tensor_copy(g3b[0:3 * w, c], src).then_inc(m_g3, 1)

            def moe_end(m):
                for h in range(2):
                    dve.wait_ge(m["back"], h + 1)
                    dve.tensor_tensor(half(X, h), bank[2 + h], half(X, h), ALU.add).then_inc(m["x"], 1)

            dve.wait_ge(x_loaded, 16)
            layernorm((0, 1), X, Y)
            dve.wait_ge(con_loaded, 16)
            cross(0)
            layernorm((0, 1), X, Y)
            dve.wait_ge(const_ready, 1)
            for g, name in enumerate(("tmk", "tmv", "tmr")):
                dve.tensor_scalar(omt[:, g:g + 1], vcol(name), -1.0, 1.0, ALU.mult, ALU.add)
            for r in run:
                dve.memset(r[:, 0:1], 0.0)
            dve.wait_ge(r_decay, 1)
            step(dve.tensor_scalar(tdn[:, :], tdn[:, :], -1.0, None, ALU.mult))
            newseq = ccol("newseq").rearrange("p (a t) -> p a t", a=1).to_broadcast([P, SPH, T])
            step(dve.tensor_scalar(tdt.rearrange("p (b t) -> p b t", t=T), newseq, tdn[:, :], None, ALU.add))
            for h in range(2):
                dve.wait_ge(feat_ready, 2 + h + 1)
                yv = yt(h).rearrange("p (b t) -> p b t", t=T)
                for g, name in enumerate(("tmk", "tmv", "tmr")):
                    mix = rmix(h, g).rearrange("p (b t) -> p b t", t=T)
                    dve.wait_ge(r_ymix, 3 * h + g + 1)
                    dve.scalar_tensor_tensor(mix[:, :, 1:T], yv[:, :, 0:T - 1], omt[:, g:g + 1], mix[:, :, 1:T],
                                             ALU.mult, ALU.add).then_inc(r_mix, 1)
            for h in range(2):
                dve.wait_ge(r_kv, h + 1)
                K = rmix(h, 0)
                E1S, _, E1, E2 = (rexp(h, k) for k in range(4))
                mx, num, den = (r[:, 1:HN + 1] for r in run)
                mxp, nump, denp = (r[:, 0:HN] for r in run)
                if h == 1:
                    dve.wait_ge(r_parg, 1)
                dve.tensor_tensor_scan(mx, tdt, K, NEG, ALU.add, ALU.max).then_inc(r_max, 1)
                dve.wait_ge(r_max, h + 1)
                step(dve.tensor_tensor(E1S, mxp, tdt, ALU.add))
                dve.tensor_tensor(E1S, E1S, mx, ALU.subtract).then_inc(r_arg, 1)
                b3 = lambda a: a.rearrange("p (b t) -> p b t", t=T)
                step(dve.tensor_tensor(b3(mpo), b3(mxp), newseq, ALU.add))
                step(dve.scalar_tensor_tensor(mo, K, vcol("tf"), mpo, ALU.add, ALU.max))
                dve.tensor_tensor(E1, mpo, mo, ALU.subtract).then_inc(r_arg, 1)
                dve.scalar_tensor_tensor(E2, K, vcol("tf"), mo, ALU.add, ALU.subtract).then_inc(r_arg, 1)
            for h in range(2):
                E1S, E2S, E1, E2 = (rexp(h, k) for k in range(4))
                dve.wait_ge(r_exp, 4 * h + 4)
                dve.wait_ge(r_ev, 2 * h + 1)
                dve.tensor_tensor_scan(num, E1S, rmix(h, 0), 0.0, ALU.mult, ALU.add)
                step(dve.tensor_tensor_scan(den, E1S, E2S, 0.0, ALU.mult, ALU.add))
                dve.tensor_tensor(mpo, E1, nump, ALU.mult)
                step(dve.tensor_tensor(E1S, E1, denp, ALU.mult))
                dve.wait_ge(r_ev, 2 * h + 2)
                dve.tensor_tensor(mpo, mpo, rmix(h, 1), ALU.add)
                step(dve.tensor_tensor(mo, E1S, E2, ALU.add))
                dve.wait_ge(r_er, h + 1)
                step(dve.scalar_tensor_tensor(mo, rmix(h, 2), 1.0, mo, ALU.add, ALU.mult))
                step(dve.reciprocal(mo, mo))
                dve.tensor_tensor(rw(h), mpo, mo, ALU.mult).then_inc(r_rw, 1)
            for h in range(2):
                dve.wait_ge(r_out, h + 1)
                step(dve.tensor_tensor(half(X, h), bank[2 + h], half(X, h), ALU.add))
            layernorm((0, 1), X, Y)
            softmax_router(NE0 - 1, 1, 0)
            keep_top(TOP0, NE0 - 1, 1, "rev0")
            step(dve.tensor_scalar(gs1[:, :], gs1[:, :], 1e-9, None, ALU.add))
            step(dve.reciprocal(gs1[:, :], gs1[:, :]))
            step(dve.tensor_tensor(gp[:, :, 1:NE0], gp[:, :, 1:NE0], over_experts(gs1, NE0 - 1), ALU.mult))
            step(dve.memset(gp[:, :, 0:1], 1.0))
            routing_parts(NE0, 0)
            m = moe[0]
            dve.sem_inc(m["mul"], FREE0["mul"])
            dve.sem_inc(m["prod"], FREE0["prod"])
            dve.sem_inc(m["xcm"], FREE0["xcm"])

            def scale_input(un, g):
                dve.wait_ge(m["gbc"], g + 1)
                dve.tensor_tensor(xc, bank[un % 2], yt(un % 2), ALU.mult).then_inc(m["xcm"], 1)

            def input_lo(un, g):
                dve.wait_ge(m["xch"], g + 1)
                dve.tensor_tensor(xcl[un % 2][:, :], xc, xch[un % 2][:, :].bitcast(F32), ALU.subtract)\
                    .then_inc(m["xcp"], 1)

            scale_input(0, 0)
            input_lo(0, 0)

            def gated(i, q):
                base = len(STEPS0) * i
                dve.wait_ge(m["act"], base + q + 1)
                dve.wait_ge(m["mm"], base + q + 1 + FREE0["mm"])
                dve.wait_ge(m["prod"], base + q - 3 + FREE0["prod"])
                dve.tensor_tensor(prod[q % 4], act_out[q % 2], bank[4 + q % 2], ALU.mult).then_inc(m["mul"], 1)

            def next_input(i, q, last):
                f, un = q % NF0, q // NF0 + 1
                if last and un >= 4 or f > 1:
                    return
                if f == 0:
                    dve.wait_ge(m["xcp"], 4 * i + un)
                    scale_input(un, 4 * i + un)
                else:
                    input_lo(un, 4 * i + un)

            def body0(i, last):
                for q in range(len(STEPS0)):
                    if not last or q + 1 < len(STEPS0):
                        gated(i, q + 1)
                    dve.wait_ge(m["hi"], len(STEPS0) * i + q + 1)
                    dve.tensor_tensor(pl[q % 2][:, :], prod[q % 4], ph[q % 2][:, :].bitcast(F32), ALU.subtract)\
                        .then_inc(m["prod"], 1)
                    if not last or q + 1 < len(STEPS0):
                        next_input(i, q + 1, last)

            gated(0, 0)
            next_input(0, 0, False)
            bodies(dve, NE0 // 2, body0)
            moe_end(m)
            dve.wait_ge(m["x"], 2)
            layernorm((0, 1), X, Y)
            for h in range(2):
                hs = slice(h * HT, (h + 1) * HT)
                s3 = smask(h).rearrange("p (t k) -> p t k", t=HT)
                causal = ccol("causal").rearrange("p (a k) -> p a k", a=1).to_broadcast([P, HT, P])
                dve.wait_ge(a_scores, h + 1)
                step(dve.tensor_tensor(s3, bank[2 + h].rearrange("p (t k) -> p t k", t=HT), causal, ALU.add))
                step(dve.tensor_reduce(nmx[:, hs], s3, AX.X, ALU.max))
                dve.tensor_scalar(nmx[:, hs], nmx[:, hs], -float(D) ** -0.5, None, ALU.mult).then_inc(a_masked, 1)
            for h in range(2):
                hs = slice(h * HT, (h + 1) * HT)
                dve.wait_ge(a_prob, h + 1)
                dve.sem_inc(tok_ready, 1)
                step(dve.reciprocal(ssum[:, hs], ssum[:, hs]))
            for h in range(2):
                dve.wait_ge(a_out, h + 1)
                for i in range(HT):
                    t = h * HT + i
                    last = dve.scalar_tensor_tensor(Y2[:, t, :], blk(bank[6 + h], i), ssum[:, t:t + 1], Y[:, t, :],
                                                    ALU.mult, ALU.add)
                last.then_inc(a_y2, 1)
            dve.wait_ge(a_y2, 2)
            layernorm((0, 1), Y2, Y2, lambda h: affine(h, Y2, "g1", "be1").then_inc(tok_ready, 1))
            dve.wait_ge(tok_ready, 12)
            cross(1)
            layernorm((0, 1), Y2, Y2, lambda h: affine(h, Y2, "g2", "be2").then_inc(tok_ready, 1))
            dve.wait_ge(bias_loaded, 16)
            dve.wait_ge(moe[0]["accdone"], 1)
            for c, b in enumerate(bias_at):
                raw = wraw[0:34, c * HN:(c + 1) * HN]
                step(dve.tensor_copy(b[0:34, :], raw))
                last = dve.scalar_tensor_tensor(b[0:34, :], b[0:34, :].bitcast(F32), ccol("biaslo")[0:34, :], raw,
                                                ALU.mult, ALU.add)
            last.then_inc(h_bias, 1)
            def finish_decoder(h):
                dve.wait_ge(tok_ready, 13 + h)
                dve.wait_ge(tr_done, 13 + h)
                v = Y2[:, h * HT:(h + 1) * HT, :]
                step(dve.tensor_tensor(v, v, along("b2"), ALU.add))
                dve.wait_ge(f_out, h + 1)
                dve.tensor_tensor(half(Y2, h), bank[4 + h], half(Y2, h), ALU.add).then_inc(f_sum, 1)
                dve.wait_ge(f_sum, h + 1)
                layernorm((h,), Y2, Y2, lambda h: step(affine(h, Y2, "g3", "be3")))
                step(dve.tensor_tensor(half(X, h), half(Y2, h), half(X, h), ALU.add))
                layernorm((h,), X, Y)
            def split_qk(h):
                for w, name in enumerate(("bqE", "bkE")):
                    dve.wait_ge(h_eh, 2 * h + w + 1)
                    for g in range(2):
                        c = slice(g * 256, (g + 1) * 256)
                        last = dve.scalar_tensor_tensor(qe_l(h, w)[:, c], bank[6 + w][:, c], vcol(name, g),
                                                        qe_h(h, w)[:, c].bitcast(F32), ALU.add, ALU.subtract)
                    last.then_inc(h_ec, 1)

            finish_decoder(0)
            split_qk(0)
            finish_decoder(1)
            def mask_dot(u):
                dve.wait_ge(h_d, 2 * u + 2)
                if u >= 2:
                    dve.wait_ge(h_s, 2 * u - 2)
                bias = vcol("bkD", u % 4)
                dve.tensor_scalar(dot_k(u, 0), bank[1], bias, ccol("maskA"), ALU.add, ALU.mult)
                dve.tensor_scalar(dot_k(u, 1), bank[1], bias, ccol("maskB"), ALU.add, ALU.mult).then_inc(h_dk, 1)

            def extract(u, p):
                dve.wait_ge(h_s, 2 * u + p + 1)
                if u >= 2:
                    dve.wait_ge(h_exp, u - 1)
                for j in (0, 1):
                    rows = slice(T * j, T * j + T)
                    last = dve.tensor_copy(own_scores(u, p, rows), own_banks(rows))
                last.then_inc(h_sxd, 1)

            def normalise(m):
                dve.wait_ge(h_inv, m + 1)
                if m >= 4:
                    dve.wait_ge(h_s, 2 * (m // 2) - 2)
                for j in range(2):
                    n = 2 * m + j
                    inv = n2(m)[:, j * 256:(j + 1) * 256].rearrange("p (b s) -> p b s", s=T // 2)
                    for c in range(2):
                        out = rot(n).rearrange("p (b c s) -> p c b s", c=2, s=T // 2)[:, c]
                        src = bank[2 + n % 4][:, c * 256:(c + 1) * 256].rearrange("p (b s) -> p b s", s=T // 2)
                        last = dve.scalar_tensor_tensor(out, inv, (QF, 1.0)[m % 2] * 1e12, src, ALU.min, ALU.mult)
                    last.then_inc(h_norm, 1)

            def value_blocks(t, b):
                dve.wait_ge(h_v, t + 1)
                keep = ccol("slot4").rearrange("p (a s x) -> p a s x", a=1, s=4).to_broadcast([P, 4, 4, HD])
                for j in range(SPT):
                    v = b[:, 32 * j:32 * j + 32].rearrange("p (g a x) -> p g a x", g=4, a=1).to_broadcast([P, 4, 4, HD])
                    last = dve.tensor_tensor(vb(t).rearrange("p (g b s x) -> p b g s x", g=4, b=4, s=4)[:, j], v, keep,
                                             ALU.mult)
                last.then_inc(h_vb, 1)

            def softmax_shift(u):
                dve.wait_ge(h_sxd, 2 * u + 2)
                dve.wait_ge(h_sxa, 2 * u + 2)
                s3 = sx(u).rearrange("p (g t) -> p g t", t=T)
                step(dve.tensor_reduce(hm, s3, AX.X, ALU.max))
                top = hm.rearrange("p (g a) -> p g a", a=1).to_broadcast([P, NH, T])
                dve.tensor_tensor(s3, s3, top, ALU.subtract).then_inc(h_sub, 1)

            def softmax_sum(u):
                dve.wait_ge(h_exp, u + 1)
                r = hsum(u)
                step(dve.tensor_reduce(r, ex(u).rearrange("p (g t) -> p g t", t=T), AX.X, ALU.add))
                dve.reciprocal(r, r).then_inc(h_sum, 1)

            def result(u):
                h, g = HEL[u]
                dve.wait_ge(h_pv, u + 1)
                dve.wait_ge(h_sum, u + 1)
                for j in range(SPT):
                    rows = slice(T * j, T * j + T)
                    inv = hsum(u)[rows, :].rearrange("p (i s a) -> p i s a", i=4, a=1).to_broadcast([T, HT, 4, HD])
                    src = bank[1][rows, :].rearrange("p (i b s x) -> p b i s x", i=4, b=4, s=4)[:, j]
                    out = Y[rows, h * HT:(h + 1) * HT, g * 32:(g + 1) * 32].rearrange("p i (s x) -> p i s x", s=4)
                    last = dve.tensor_tensor(out, src, inv, ALU.mult)
                last.then_inc(h_o, 1)
                if g == 3:
                    dve.wait_ge(h_o, u + 1)
                    v = Y[:, h * HT:(h + 1) * HT, :]
                    dve.tensor_tensor(v, v, along("bv"), ALU.add).then_inc(tok_ready, 1)
                    xv = X[:, h * HT:(h + 1) * HT, :]
                    step(dve.tensor_tensor(xv, xv, along("bo"), ALU.add))

            def add_out(h):
                dve.wait_ge(h_out, h + 1)
                dve.tensor_tensor(half(X, h), bank[1], half(X, h), ALU.add).then_inc(h_x, 1)

            dve.wait_ge(h_bias, 1)
            for u in range(len(HEL) + 2):
                if u == 0:
                    for t in range(HT):
                        value_blocks(t, bank[6 + t % 2])
                if u < len(HEL):
                    mask_dot(u)
                if u >= 2:
                    softmax_sum(u - 2)
                if u < len(HEL):
                    normalise(2 * u)
                if 1 <= u <= len(HEL):
                    extract(u - 1, 0)
                if u < len(HEL):
                    normalise(2 * u + 1)
                if u == 0:
                    split_qk(1)
                if 1 <= u <= HT:
                    value_blocks(HT + u - 1, bank[0])
                if u >= 2:
                    result(u - 2)
                if 1 <= u <= len(HEL):
                    extract(u - 1, 1)
                if u == 6:
                    add_out(0)
                if 1 <= u <= len(HEL):
                    softmax_shift(u - 1)
                if u == 8:
                    layernorm((0,), X, Y)
            add_out(1)
            dve.wait_ge(h_x, 2)
            layernorm((1,), X, Y)
            softmax_router(NE1, 0, 1)
            keep_top(TOP1, NE1, 0, "rev1")
            step(dve.tensor_scalar(gs1[:, :], gs1[:, :], 1e-12, None, ALU.max))
            step(dve.reciprocal(gs1[:, :], gs1[:, :]))
            step(dve.tensor_tensor(gp[:, :, :], gp[:, :, :], over_experts(gs1, NE1), ALU.mult))
            routing_parts(NE1, 1)
            m = moe[1]
            dve.sem_inc(m["mul"], FREE1["mul"])
            dve.sem_inc(m["prod"], FREE1["prod"])

            def weigh(i, q):
                base = len(STEPS1) * i
                k, h, f = STEPS1[q % len(STEPS1)]
                dve.wait_ge(m["act"], base + q + 1 + FREE1["act"])
                if f == 0:
                    dve.wait_ge(m["gbc"], 8 * i + q // NF1 + 1)
                dve.wait_ge(m["prod"], base + q - 3 + FREE1["prod"])
                dve.tensor_tensor(prod[q % 4], act_out[q % 2], bank[h], ALU.mult).then_inc(m["mul"], 1)

            def body1(i, last):
                for q in range(len(STEPS1)):
                    if not last or q + 1 < len(STEPS1):
                        weigh(i, q + 1)
                    dve.wait_ge(m["hi"], len(STEPS1) * i + q + 1)
                    dve.tensor_tensor(pl4[q % 4], prod[q % 4], ph4[q % 4].bitcast(F32), ALU.subtract)\
                        .then_inc(m["prod"], 1)

            weigh(0, 0)
            bodies(dve, NE1 // 4, body1)
            moe_end(m)


def kernel(**inputs):
    import numpy as np
    import concourse.bacc as bacc
    from concourse.bass_utils import run_bass_kernel_spmd

    a = {k: np.asarray(v) for k, v in inputs.items()}
    f32 = np.float32

    def columns(v, n):
        return v.reshape(n, P).T

    def chunks(m):
        return m.reshape(-1, P, m.shape[1]).transpose(1, 0, 2).reshape(P, -1)

    slots = [4 * g + 2 * k + j for g in range(4) for j in range(2) for k in range(2)]
    slot_feats = np.array([s * HD + e for s in slots for e in range(HD)])
    strip_of = {0: 0, 2: 1, 1: 2, 3: 3}

    def strips(m):
        out = np.zeros((m.shape[1], 4, 4, T), f32)
        for g in range(4):
            for r, s in strip_of.items():
                out[:, g, s, 0:HD] = m[(4 * g + r) * HD:(4 * g + r + 1) * HD].T
        return out.reshape(m.shape[1], 4 * P)

    wh_ = a["L1_attn_Whel"].reshape(NH, HP, 2, HD)
    whel = np.zeros((2, 8, HD, NH // 2, 2, 2, 2, HP), f32)
    bhel = np.zeros((2, 2, HP, NH // 2, 2), f32)
    for u in range(NH // 2):
        for j in range(2):
            hd = 2 * u + j
            for par in range(2):
                for c in range(2):
                    whel[par, hd % 8, :, u, c, j, par, :] = wh_[hd, :, c, :].T
                    bhel[j, par, :, u, c] = a["L1_attn_bhel"][hd].reshape(HP, 2)[:, c]
    whel = whel.reshape(P, -1)
    bhel = bhel.reshape(P, -1)

    hbias = np.zeros((34, 3 * FF0), f32)
    hbias[0:2] = bhel.T.reshape(-1)[0:3 * FF0]
    hbias[32:34, 0:16 * P - 3 * FF0] = bhel.T.reshape(-1)[3 * FF0:]

    def parity_bias(b):
        return np.concatenate([b.reshape(2, 64).T] * 2, 0)

    vecs = {"tmk": a["L0_attn_time_mix_key"][:, None], "tmv": a["L0_attn_time_mix_value"][:, None],
            "tmr": a["L0_attn_time_mix_receptance"][:, None], "td": a["L0_attn_time_decay"][:, None],
            "tf": a["L0_attn_time_first"][:, None], "db1": columns(a["L1_xattn_b1"], FFD // P),
            "bqE": parity_bias(a["L1_attn_bq"]), "bkE": parity_bias(a["L1_attn_bk"]),
            "bqD": strips(a["L1_attn_bq"][:, None]).reshape(4, P).T, "bkD": strips(a["L1_attn_bk"][:, None]).reshape(4, P).T,
            "b1m": columns(a["L1_ffn_b1"].reshape(-1), NE1 * FF1 // P)}
    mats = {"Wk": a["L0_attn_Wk"], "Wv": a["L0_attn_Wv"], "Wr": a["L0_attn_Wr"], "Wo": a["L0_attn_Wo"],
            "router": a["L0_ffn_router_w"].T, "dw1": a["L1_xattn_w1"], "dw2": chunks(a["L1_xattn_w2"]),
            "WqE": a["L1_attn_Wq"].T, "WkE": a["L1_attn_Wk"].T, "WvT": a["L1_attn_Wv"][slot_feats].T,
            "WoT": a["L1_attn_Wo"].T[slot_feats], "Whel": whel, "WqD": strips(a["L1_attn_Wq"]),
            "WkD": strips(a["L1_attn_Wk"]), "gate": a["L1_ffn_gate"]}
    rows = {"g1": a["L1_xattn_g1"], "be1": a["L1_xattn_beta1"], "g2": a["L1_xattn_g2"], "be2": a["L1_xattn_beta2"],
            "g3": a["L1_xattn_g3"], "be3": a["L1_xattn_beta3"], "b2": a["L1_xattn_b2"],
            "bv": a["L1_attn_bv"][slot_feats], "bo": a["L1_attn_bo"]}

    tok = np.arange(P)
    same = tok[:, None] // T == tok[None, :] // T
    sel = np.zeros((P, NE0 + 1 + NE1), f32)
    for part in range(3):
        for e in range(NE0):
            sel[part * NE0 + e, e] = 1
        for e in range(NE1):
            sel[part * NE1 + e, NE0 + 1 + e] = 1
    consts = {"ident": np.eye(P), "causal": np.where(same & (tok[None, :] <= tok[:, None]), 0, NEG),
              "seq4": tok[:, None] // T == np.arange(SPT), "slot4": tok[:, None] // T == np.arange(SPT * HD) // HD,
              "maskA": (tok // T % 2 == 0)[:, None], "maskB": (tok // T % 2 == 1)[:, None],
              "biaslo": -(tok % 2).astype(f32)[:, None],
              "newseq": np.broadcast_to(np.where(np.arange(T) == 0, NEG, 0), (P, T)),
              "rev0": np.broadcast_to(np.arange(NE0 - 1, 0, -1), (P, NE0 - 1)),
              "rev1": np.broadcast_to(np.arange(NE1, 0, -1), (P, NE1)),
              "sel0": sel[:, 0:NE0 + 1], "sel1": sel[:, NE0 + 1:]}

    def pack(table, parts):
        for name, width in table:
            assert parts[name].shape[1] == width, (name, parts[name].shape)
        return np.concatenate([np.asarray(parts[name], f32) for name, _ in table], 1)

    ctx_ = a["ctx_1024"].reshape(NT, SPT, S, D)
    gate = np.concatenate([a["L0_ffn_shared_gate"][None], a["L0_ffn_routed_gate"]])
    up = np.concatenate([a["L0_ffn_shared_up"][None], a["L0_ffn_routed_up"]])
    down = np.concatenate([a["L0_ffn_shared_down"][None], a["L0_ffn_routed_down"]])
    down = down.transpose(0, 2, 1).reshape(NE0, FF0 // P, P, D).transpose(0, 2, 1, 3).reshape(NE0, P, FF0)
    w2 = a["L1_ffn_W2"].reshape(NE1, FF1 // P, P, D).transpose(0, 2, 1, 3).reshape(NE1, P, FF1)
    w1 = np.concatenate([a["L1_ffn_W1"], w2], 2)
    arrays = {
        "x": a["x"].reshape(NT * P, D),
        "zT": ctx_.transpose(0, 3, 1, 2), "z": ctx_[:, :, 0:2 * P].reshape(NT, SPT, 2, P, D).transpose(0, 3, 1, 2, 4),
        "zlast": ctx_[:, :, S - 1].transpose(1, 0, 2),
        "vec": pack(VECS, vecs), "mat": pack(MATS, mats), "row": pack(ROWS, {k: v[None] for k, v in rows.items()}),
        "con": pack(CONSTS, consts), "hbias": hbias,
        "mb2": np.concatenate([a["L1_ffn_b2"]] * 3),
        "w0": np.concatenate([gate.transpose(0, 2, 1), up.transpose(0, 2, 1), down], 2),
        "w1": w1.reshape(NE1 // 2, 2, P, 2 * FF1).transpose(0, 2, 1, 3).reshape(NE1 // 2, P, 4 * FF1),
    }
    arrays = {k: np.ascontiguousarray(v) for k, v in arrays.items()}

    nc = bacc.Bacc("TRN2", target_bir_lowering=False, num_devices=1)
    args = {k: nc.dram_tensor(f"in_{k}", v.shape, F32, kind="ExternalInput").ap() for k, v in arrays.items()}
    args["out"] = nc.dram_tensor("out_x", (NT * P, D), F32, kind="ExternalOutput").ap()
    build(nc, args)
    r = run_bass_kernel_spmd(nc, [{f"in_{k}": v for k, v in arrays.items()}], core_ids=[0])
    return r.results[0]["out_x"].reshape(NSEQ, T, D)
```
